# Optimizing a Trainium2 kernel written in Bass

```python
import numpy as np
import jax
import jax.numpy as jnp

def _softmax(x, axis=-1):
    return jax.nn.softmax(x, axis=axis)

def _gelu(x):
    return jax.nn.gelu(x, approximate=True)

def _silu(x):
    return jax.nn.silu(x)

def _sigmoid(x):
    return jax.nn.sigmoid(x)

def _layernorm(x, axis=-1, eps=1e-05):
    m = jnp.mean(x, axis=axis, keepdims=True)
    v = jnp.var(x, axis=axis, keepdims=True)
    return (x - m) / jnp.sqrt(v + eps)

def _scatter_add(tgt, idx, src, axis=0):
    return tgt.at[idx].add(src)

def _segment_sum(src, seg, n):
    return jax.ops.segment_sum(src, seg, n)
kernel_name = 'mk_xattn_ffn_d2_seqx_r8_328ecb'

def setup_inputs(seed: int=0):
    np.random.seed(seed)
    _w = jnp.asarray

    def _rec_inputs():
        import jax
        import jax.numpy as jnp
        _rk = jax.random.key(seed)
        x = 7.22e-05 + 1 * jax.random.normal(jax.random.fold_in(_rk, 1), (8, 256, 128), jnp.float32)
        _lenS = 256 - jax.random.randint(jax.random.fold_in(_rk, 7), (8,), 0, max(1, 256 // 4) + 1, jnp.int32)
        _lenS2 = 1601 - jax.random.randint(jax.random.fold_in(_rk, 8), (8,), 0, max(1, 1601 // 4) + 1, jnp.int32)
        _ctx_1024P = jax.random.normal(jax.random.fold_in(_rk, 11), (8, 16, 128), jnp.float32)
        _ctx_1024c = jax.random.dirichlet(jax.random.fold_in(_rk, 511), 0.3 * jnp.ones((16,), jnp.float32), (8, 1601))
        _ctx_1024t = jnp.einsum('bsk,bkd->bsd', _ctx_1024c, _ctx_1024P)
        _ctx_1024t = _ctx_1024t * jax.lax.rsqrt(jnp.mean(jnp.square(_ctx_1024t)) + 1e-12) * 0.953939
        ctx_1024 = -0.000519255 + 0.935342 * (_ctx_1024t + 0.3 * jax.random.normal(jax.random.fold_in(_rk, 611), (8, 1601, 128), jnp.float32))
        return (x, ctx_1024)
    x, ctx_1024 = _rec_inputs()

    def _L0_xattn_setup():
        import jax, jax.numpy as jnp
        import numpy as np
        NUM_HEADS = 16
        HEAD_SIZE = 64
        key = jax.random.key(seed)
        ks = jax.random.split(key, 6)
        B, S, CH = (2, 512, 128)
        N, CD = (128, 128)
        x = jax.random.normal(ks[0], (B, S, CH), dtype=jnp.float32)
        c = jax.random.normal(ks[1], (B, N, CD), dtype=jnp.float32)
        c = c.at[:, N - 128:, :].set(0.0)
        sd = 1.0 / np.sqrt(CH)
        Wq = jax.random.normal(ks[2], (CH, NUM_HEADS * HEAD_SIZE), dtype=jnp.float32) * sd
        Wk = jax.random.normal(ks[3], (CD, NUM_HEADS * HEAD_SIZE), dtype=jnp.float32) * sd
        Wv = jax.random.normal(ks[4], (CD, NUM_HEADS * HEAD_SIZE), dtype=jnp.float32) * sd
        Wo = jax.random.normal(ks[5], (NUM_HEADS * HEAD_SIZE, CH), dtype=jnp.float32) * sd
        return {'x': x, 'c': c, 'Wq': Wq, 'Wk': Wk, 'Wv': Wv, 'Wo': Wo}
    _L0_xattn_all = _L0_xattn_setup()
    _L0_xattn_in = {k: v for k, v in _L0_xattn_all.items() if k in ('Wq', 'Wk', 'Wv', 'Wo')}
    del _L0_xattn_all

    def _L0_ffn_setup():
        import jax, jax.numpy as jnp
        import numpy as np
        B, SEQ, D, E, F = (4, 128, 128, 8, 512)
        CAPACITY = 2
        key = jax.random.key(seed)
        ks = jax.random.split(key, 8)
        x = jax.random.normal(ks[0], (B, SEQ, D), jnp.float32)
        gate_weight = jax.random.normal(ks[1], (E, D), jnp.float32) * 0.006
        W1 = jax.random.normal(ks[2], (E, D, F), jnp.float32) * (1.0 / np.sqrt(D))
        b1 = jnp.zeros((E, F), jnp.float32)
        W2 = jax.random.normal(ks[3], (E, F, D), jnp.float32) * (1.0 / np.sqrt(F))
        b2 = jnp.zeros((E, D), jnp.float32)
        Ws1 = jax.random.normal(ks[4], (D, F), jnp.float32) * (1.0 / np.sqrt(D))
        bs1 = jnp.zeros((F,), jnp.float32)
        Ws2 = jax.random.normal(ks[5], (F, D), jnp.float32) * (1.0 / np.sqrt(F))
        bs2 = jnp.zeros((D,), jnp.float32)
        return {'x': x, 'gate_weight': gate_weight, 'W1': W1, 'b1': b1, 'W2': W2, 'b2': b2, 'Ws1': Ws1, 'bs1': bs1, 'Ws2': Ws2, 'bs2': bs2}
    _L0_ffn_all = _L0_ffn_setup()
    _L0_ffn_in = {k: v for k, v in _L0_ffn_all.items() if k in ('gate_weight', 'W1', 'b1', 'W2', 'b2', 'Ws1', 'bs1', 'Ws2', 'bs2')}
    del _L0_ffn_all

    def _L1_xattn_setup():
        import jax, jax.numpy as jnp
        import numpy as np
        B, S, D = (4, 256, 128)
        key = jax.random.key(seed)
        ks = jax.random.split(key, 10)
        sc = 1.0 / np.sqrt(D)
        return {'x': jax.random.normal(ks[0], (B, S, D), dtype=jnp.float32), 'y': jax.random.normal(ks[1], (B, S, D), dtype=jnp.float32), 'Wq': jax.random.normal(ks[2], (D, D), dtype=jnp.float32) * sc, 'bq': jnp.zeros((D,), dtype=jnp.float32), 'Wk': jax.random.normal(ks[3], (D, D), dtype=jnp.float32) * sc, 'bk': jnp.zeros((D,), dtype=jnp.float32), 'Wv': jax.random.normal(ks[4], (D, D), dtype=jnp.float32) * sc, 'bv': jnp.zeros((D,), dtype=jnp.float32), 'Wr': jax.random.normal(ks[5], (D, D), dtype=jnp.float32) * sc, 'br': jnp.zeros((D,), dtype=jnp.float32)}
    _L1_xattn_all = _L1_xattn_setup()
    _L1_xattn_in = {k: v for k, v in _L1_xattn_all.items() if k in ('Wq', 'bq', 'Wk', 'bk', 'Wv', 'bv', 'Wr', 'br')}
    del _L1_xattn_all

    def _L1_ffn_setup():
        import jax, jax.numpy as jnp
        import numpy as np
        B, S, D = (8, 512, 128)
        E, R, K = (6, 16, 2)
        key = jax.random.key(seed)
        ks = jax.random.split(key, 9)
        sc = 0.02
        return {'x': jax.random.normal(ks[0], (B, S, D), jnp.float32), 'base_W': jax.random.normal(ks[1], (D, D), jnp.float32) * sc, 'base_b': jax.random.normal(ks[2], (D,), jnp.float32) * sc, 'shared_A': jax.random.normal(ks[3], (R, D), jnp.float32) * sc, 'shared_B': jax.random.normal(ks[4], (D, R), jnp.float32) * sc, 'routed_A': jax.random.normal(ks[5], (E, R, D), jnp.float32) * sc, 'routed_B': jax.random.normal(ks[6], (E, D, R), jnp.float32) * sc, 'router_W': jax.random.normal(ks[7], (E, D), jnp.float32) * sc, 'router_b': jax.random.normal(ks[8], (E,), jnp.float32) * sc}
    _L1_ffn_all = _L1_ffn_setup()
    _L1_ffn_in = {k: v for k, v in _L1_ffn_all.items() if k in ('base_W', 'base_b', 'shared_A', 'shared_B', 'routed_A', 'routed_B', 'router_W', 'router_b')}
    del _L1_ffn_all
    return {'x': x, 'ctx_1024': ctx_1024, 'L0_xattn_Wq': _L0_xattn_in['Wq'], 'L0_xattn_Wk': _L0_xattn_in['Wk'], 'L0_xattn_Wv': _L0_xattn_in['Wv'], 'L0_xattn_Wo': _L0_xattn_in['Wo'], 'L0_ffn_gate_weight': _L0_ffn_in['gate_weight'], 'L0_ffn_W1': _L0_ffn_in['W1'], 'L0_ffn_b1': _L0_ffn_in['b1'], 'L0_ffn_W2': _L0_ffn_in['W2'], 'L0_ffn_b2': _L0_ffn_in['b2'], 'L0_ffn_Ws1': _L0_ffn_in['Ws1'], 'L0_ffn_bs1': _L0_ffn_in['bs1'], 'L0_ffn_Ws2': _L0_ffn_in['Ws2'], 'L0_ffn_bs2': _L0_ffn_in['bs2'], 'L1_xattn_Wq': _L1_xattn_in['Wq'], 'L1_xattn_bq': _L1_xattn_in['bq'], 'L1_xattn_Wk': _L1_xattn_in['Wk'], 'L1_xattn_bk': _L1_xattn_in['bk'], 'L1_xattn_Wv': _L1_xattn_in['Wv'], 'L1_xattn_bv': _L1_xattn_in['bv'], 'L1_xattn_Wr': _L1_xattn_in['Wr'], 'L1_xattn_br': _L1_xattn_in['br'], 'L1_ffn_base_W': _L1_ffn_in['base_W'], 'L1_ffn_base_b': _L1_ffn_in['base_b'], 'L1_ffn_shared_A': _L1_ffn_in['shared_A'], 'L1_ffn_shared_B': _L1_ffn_in['shared_B'], 'L1_ffn_routed_A': _L1_ffn_in['routed_A'], 'L1_ffn_routed_B': _L1_ffn_in['routed_B'], 'L1_ffn_router_W': _L1_ffn_in['router_W'], 'L1_ffn_router_b': _L1_ffn_in['router_b']}

def reference(x, ctx_1024, L0_xattn_Wq, L0_xattn_Wk, L0_xattn_Wv, L0_xattn_Wo, L0_ffn_gate_weight, L0_ffn_W1, L0_ffn_b1, L0_ffn_W2, L0_ffn_b2, L0_ffn_Ws1, L0_ffn_bs1, L0_ffn_Ws2, L0_ffn_bs2, L1_xattn_Wq, L1_xattn_bq, L1_xattn_Wk, L1_xattn_bk, L1_xattn_Wv, L1_xattn_bv, L1_xattn_Wr, L1_xattn_br, L1_ffn_base_W, L1_ffn_base_b, L1_ffn_shared_A, L1_ffn_shared_B, L1_ffn_routed_A, L1_ffn_routed_B, L1_ffn_router_W, L1_ffn_router_b):
    import jax
    import jax.numpy as jnp

    def _L0_xattn_ref(x, c, Wq, Wk, Wv, Wo):
        import jax, jax.numpy as jnp
        import numpy as np
        NUM_HEADS = 16
        HEAD_SIZE = 64
        H, D = (NUM_HEADS, HEAD_SIZE)
        B, S = (x.shape[0], x.shape[1])
        N = c.shape[1]
        scale = D ** (-0.5)
        q = (x @ Wq).reshape(B, S, H, D).transpose(0, 2, 1, 3)
        k = (c @ Wk).reshape(B, N, D, H).transpose(0, 3, 2, 1)
        v = (c @ Wv).reshape(B, N, D, H).transpose(0, 3, 1, 2)
        mask = jnp.all(c == 0, axis=-1)[:, None, None, :]
        scores = jnp.einsum('bhsd,bhdn->bhsn', q, k) * scale
        scores = jnp.where(mask, -jnp.inf, scores)
        att = jax.nn.softmax(scores, axis=-1)
        out = jnp.einsum('bhsn,bhnd->bhsd', att, v)
        out = out.transpose(0, 2, 1, 3).reshape(B, S, H * D)
        return out @ Wo

    def _L0_ffn_ref(x, gate_weight, W1, b1, W2, b2, Ws1, bs1, Ws2, bs2):
        import jax, jax.numpy as jnp
        import numpy as np
        B, SEQ, D, E, F = (4, 128, 128, 8, 512)
        CAPACITY = 2
        Bb, s, Dd = x.shape
        Ee = gate_weight.shape[0]
        xf = x.reshape(-1, Dd)
        S = xf.shape[0]
        logits = xf @ gate_weight.T
        scores = jax.nn.softmax(logits, axis=-1).T
        k = S * CAPACITY
        vals, idx = jax.lax.top_k(scores.reshape(-1), k)
        eidx = idx // S
        tidx = idx % S
        gate = jnp.zeros((Ee, S), x.dtype).at[eidx, tidx].add(vals)
        h = jax.nn.gelu(jnp.einsum('sd,edf->esf', xf, W1) + b1[:, None, :], approximate=True)
        y = jnp.einsum('esf,efd->esd', h, W2) + b2[:, None, :]
        out = jnp.einsum('es,esd->sd', gate, y)
        shared = jax.nn.gelu(xf @ Ws1 + bs1, approximate=True) @ Ws2 + bs2
        out = out + shared
        return out.reshape(Bb, s, Dd)

    def _L1_xattn_ref(x, y, Wq, bq, Wk, bk, Wv, bv, Wr, br):
        import jax, jax.numpy as jnp
        import numpy as np
        B, S, D = (4, 256, 128)
        Q = jnp.einsum('bsd,de->bse', x, Wq) + bq
        K = jnp.einsum('bsd,de->bse', y, Wk) + bk
        V = jnp.einsum('bsd,de->bse', y, Wv) + bv
        K_hat = jnp.cos(jnp.einsum('bsd,dr->bsr', K, Wr) + br)
        scores = jnp.einsum('bqr,bkr->bqk', Q, K_hat)
        probs = jax.nn.softmax(scores, axis=-1)
        return jnp.einsum('bqk,bkd->bqd', probs, V)

    def _L1_ffn_ref(x, base_W, base_b, shared_A, shared_B, routed_A, routed_B, router_W, router_b):
        import jax, jax.numpy as jnp
        import numpy as np
        B, S, D = (8, 512, 128)
        E, R, K = (6, 16, 2)
        base_out = jax.lax.stop_gradient(jnp.einsum('bsi,oi->bso', x, base_W) + base_b)
        shared_out = jnp.einsum('bsr,or->bso', jnp.einsum('bsi,ri->bsr', x, shared_A), shared_B)
        logits = jnp.einsum('bsi,ei->bse', x, router_W) + router_b
        gate = jax.nn.softmax(logits, axis=-1)
        topk_w, topk_i = jax.lax.top_k(gate, K)
        sparse_w = jnp.sum(jax.nn.one_hot(topk_i, E, dtype=gate.dtype) * topk_w[..., None], axis=-2)
        sparse_w = sparse_w / (jnp.sum(sparse_w, axis=-1, keepdims=True) + 1e-06)
        h = jnp.einsum('bsi,eri->bser', x, routed_A)
        routed_outs = jnp.einsum('bser,eor->bseo', h, routed_B)
        routed_out = jnp.einsum('bseo,bse->bso', routed_outs, sparse_w)
        return base_out + shared_out + routed_out
    x = x + _L0_xattn_ref(_layernorm(x, axis=-1), ctx_1024, L0_xattn_Wq, L0_xattn_Wk, L0_xattn_Wv, L0_xattn_Wo)
    x = x + _L0_ffn_ref(_layernorm(x, axis=-1), L0_ffn_gate_weight, L0_ffn_W1, L0_ffn_b1, L0_ffn_W2, L0_ffn_b2, L0_ffn_Ws1, L0_ffn_bs1, L0_ffn_Ws2, L0_ffn_bs2)
    x = x + _L1_xattn_ref(_layernorm(x, axis=-1), ctx_1024, L1_xattn_Wq, L1_xattn_bq, L1_xattn_Wk, L1_xattn_bk, L1_xattn_Wv, L1_xattn_bv, L1_xattn_Wr, L1_xattn_br)
    x = x + _L1_ffn_ref(_layernorm(x, axis=-1), L1_ffn_base_W, L1_ffn_base_b, L1_ffn_shared_A, L1_ffn_shared_B, L1_ffn_routed_A, L1_ffn_routed_B, L1_ffn_router_W, L1_ffn_router_b)
    return x

_drawn_inputs = setup_inputs


def setup_inputs(seed=0):
    import zlib

    import numpy as np

    out = dict(_drawn_inputs(seed))
    spreads = {'L0_ffn_b1': (0.0, 0.8),
     'L0_ffn_b2': (0.0, 0.664),
     'L0_ffn_bs1': (0.0, 0.1),
     'L0_ffn_bs2': (0.0, 0.1),
     'L1_xattn_bq': (0.0, 0.1),
     'L1_xattn_bk': (0.0, 0.1),
     'L1_xattn_bv': (0.0, 0.1),
     'L1_xattn_br': (0.0, 0.1)}
    factors = {'L1_ffn_base_b': 5.857,
     'L1_ffn_shared_A': 6.696,
     'L1_ffn_shared_B': 6.986,
     'L1_ffn_routed_A': 8.0,
     'L1_ffn_routed_B': 8.0,
     'L1_ffn_router_W': 8.0,
     'L1_ffn_router_b': 8.0}
    for name, (base, spread) in spreads.items():
        noise = np.random.default_rng([zlib.crc32(name.encode()), seed]).standard_normal(out[name].shape)
        drawn = base * np.exp(spread * noise) if base else spread * noise
        out[name] = jnp.asarray(drawn.astype(out[name].dtype))
    for name, factor in factors.items():
        out[name] = (out[name] * factor).astype(out[name].dtype)
    return out
```

```python
import concourse.bass as bass
from concourse import mybir
from contextlib import ExitStack
import math

F32 = mybir.dt.float32
F32R = mybir.dt.float32r
BF16 = mybir.dt.bfloat16
U32 = mybir.dt.uint32
ACT = mybir.ActivationFunctionType
ALU = mybir.AluOpType
AX = mybir.AxisListType

P = 128
B, S, D = 8, 256, 128
N = 1601
H, HD = 16, 64
NC = -(-N // P)
LAST = N - (NC - 1) * P
TILES = B * S // P
MASKED = -1e30
EPS = 1e-5


def at(it, per, first):
    return first if it is None else it * per + first


def f32(ap):
    return ap.bitcast(F32)


def bc(ap, n):
    return ap.unsqueeze(2).to_broadcast([ap.shape[0], ap.shape[1], n])


def layer_norm(nc, link, src, out, squares, stats, var_ready, wait_std):
    mean, var = stats[:, 0, :], stats[:, 1, :]
    link(nc.vector.tensor_reduce(mean, src, AX.X, ALU.add))
    link(nc.vector.tensor_scalar(mean, mean, 1.0 / D, None, ALU.mult))
    link(nc.vector.tensor_tensor(out, src, bc(mean, D), ALU.subtract))
    link(nc.vector.tensor_tensor(squares, out, out, ALU.mult))
    link(nc.vector.tensor_reduce(var, squares, AX.X, ALU.add))
    nc.vector.tensor_scalar(var, var, 1.0 / D, EPS, ALU.mult, ALU.add).then_inc(var_ready, 1)
    wait_std()
    link(nc.vector.reciprocal(var, var))
    return nc.vector.tensor_tensor(out, out, bc(var, D), ALU.mult)


def attention_0(nc, x, ctx_in, wq, wk, wv, wo, XS, ident):
    G8 = H // 2
    STEPS = 2 * NC
    SLOTS = 4 * STEPS
    STAGES = 2 * B
    PIECES = [(0, 402), (402, 400), (802, 400), (1202, 400)]
    UNITS = G8 * 2

    def prep_items(group):
        items = []
        if group == 0:
            items += [("cT", i) for i in range(4)] + [("xT", 0)] + [("mask", i) for i in range(4)]
        items += [("q", i) for i in range(4)]
        vs = [("v", c) for c in range(NC)]
        mx = [("max", u) for u in range(UNITS * 4)]
        for n, m in enumerate(mx):
            items.append(m)
            if n % 5 == 2 and vs:
                items.append(vs.pop(0))
        return items + vs

    PREP = [len(prep_items(0)), len(prep_items(1))]
    TAIL = 3

    def first_use(c):
        n = PREP[0]
        for s in range(c):
            n += (TAIL if s else 0) + (PREP[(s + 1) % 2] if s + 1 < STAGES else 0)
        return n

    PER_TURN = first_use(5) - first_use(1)
    assert PER_TURN % 2 == 0 and PREP[0] % 2 == 0

    def plan(c, tail, prep):
        slots = [[] for _ in range(SLOTS)]
        if tail:
            slots[3].append(("den", 0))
            slots[7].append(("den", 1))
            for i in range(8):
                slots[8 + i].append(("recip", i))
            slots[16].append(("norm", 0))
            slots[22].append(("proj", 0))
        if prep:
            items = prep_items((c + 1) % 2)
            for n, item in enumerate(items):
                slots[n * 94 // len(items)].append(item)
            slots[95].append(("shift", 0))
        use = first_use(c)
        out = []
        for slot in slots:
            row = []
            for kind, i in slot:
                takes = kind not in ("recip", "norm", "shift")
                row.append((kind, i, use if takes else None))
                use += takes
            out.append(row)
        return out

    with ExitStack() as es:
        def sb(name, shape, dt=F32):
            return es.enter_context(nc.sbuf_tensor("a_" + name, shape, dt))

        def sem(name):
            return es.enter_context(nc.semaphore("a_" + name))

        c_nat = sb("c_nat", [P, NC, D])
        cT = [[sb(f"cT_{part}{i}", [P, NC * P], F32R) for part in ("hi", "lo")] for i in range(2)]
        V = sb("V", [P, 2, NC, G8 * HD])
        Q = [[sb(f"Q_{part}{i}", [P, G8 * S], F32R) for part in ("hi", "lo")] for i in range(2)]
        shift_diag = sb("shift_diag", [P, 2, UNITS, P], BF16)
        probs = sb("probs", [P, 4, 4 * S])
        den = sb("den", [P, G8 * S])
        G = [sb("G_hi", [P, H, D], F32R), sb("G_lo", [P, H, D], F32R)]
        Wv = [sb("Wv_hi", [P, H * HD], F32R), sb("Wv_lo", [P, H * HD], F32R)]
        Wo = sb("Wo", [P, H // 2, D])
        mask_row = sb("mask_row", [P, NC * P], BF16)
        mask_col = sb("mask_col", [P, 2, NC])
        c_flag = sb("c_flag", [P, 402], BF16)
        junk = sb("junk", [P, 2, 402], BF16)
        acc = sb("acc", [P, 2, 2, D])
        xn_b = sb("xn_b", [P, 2, D])
        xnT = [sb("xnT_hi", [P, S], F32R), sb("xnT_lo", [P, S], F32R)]
        outT = sb("outT", [P, 4 * S])
        rden = sb("rden", [P, 4 * S])
        maxes = sb("maxes", [P, 2, UNITS * 4])
        neg_max = sb("neg_max", [P, 2, UNITS])
        stats = sb("stats", [P, 2, TILES])
        c_largest = sb("c_largest", [P, NC])
        ones = sb("ones", [P, HD])

        ones_b = sb("ones_b", [P, P], BF16)
        raw = [V[:, 1, :, :].rearrange("p c n -> p (c n)")[:, i * 1024:(i + 1) * 1024] for i in range(6)]
        wq_raw, wk_raw, wv_raw, wk_heads, wqT, wkT = raw
        squares = probs[:, 0:2, :].rearrange("p a (t d) -> p (a t) d", d=D)

        Sc = es.enter_context(nc.psum_tensor("a_scores", [P, 2, 4 * S], F32))
        PV = es.enter_context(nc.psum_tensor("a_pv", [P, 4 * S], F32))
        X = es.enter_context(nc.psum_tensor("a_work", [P, 2, 512], F32))

        x_loaded, w_loaded, c_loaded = sem("x_loaded"), sem("w_loaded"), sem("c_loaded")
        res_loaded = sem("res_loaded")
        consts = sem("consts")
        dve_chain = sem("dve_chain")
        var_ready, std_ready = sem("var_ready"), sem("std_ready")
        wk_ready = sem("wk_ready")
        wT_filled, wT_copied = sem("wT_filled"), sem("wT_copied")
        G_filled, G_hi_done, G_ready = sem("G_filled"), sem("G_hi_done"), sem("G_ready")
        xn_all, wv_ready = sem("xn_all"), sem("wv_ready")
        bank_full = [sem("bank0_full"), sem("bank1_full")]
        bank_free = [sem("bank0_free"), sem("bank1_free")]
        hi_done = sem("hi_done")
        flag_done = sem("flag_done")
        col_done = sem("col_done")
        xn_ready = sem("xn_ready")
        shift_steps = sem("shift_steps")
        scores_done, probs_done, pv_done = sem("scores_done"), sem("probs_done"), sem("pv_done")
        pv_free = sem("pv_free")
        den_init, den_added = sem("den_init"), sem("den_added")
        recip_done, norm_done = sem("recip_done"), sem("norm_done")
        block = es.enter_context(nc.Block())

        def filled(eng, it, use):
            eng.wait_ge(bank_full[use % 2], at(it, PER_TURN // 2, use // 2 + 1))

        def taken(eng, it, use):
            eng.wait_ge(bank_free[use % 2], at(it, PER_TURN // 2, use // 2 + 1))

        def stages(eng, body):
            body(None, 0)
            with eng.Fori(0, 3) as it:
                for c in range(1, 5):
                    body(it, c)
            for c in range(13, STAGES):
                body(None, c)

        def steps_of(it, c, first):
            return at(it, 4 * STEPS, c * STEPS + first)

        def batch_of(it, c):
            return at(it, 2, c // 2)

        def flags(it, c):
            return c > 0 or it is not None, it is not None or c + 1 < STAGES

        def use_of(slots, kind, index):
            return [use for slot in slots for k, i, use in slot if (k, i) == (kind, index)][0]

        def the_plan(it, c):
            return plan(c, *flags(it, c))

        def prologue_items():
            return [(kind, i, use) for use, (kind, i) in enumerate(prep_items(0))]

        def buffer(c, j):
            return (c * STEPS + j) % 4

        @block.sync
        def _(sp):
            sp.dma_start(XS[:, :, :], x.rearrange("b (j p) d -> p (b j) d", p=P)).then_inc(x_loaded, 16)
            sp.dma_start(wq_raw, wq).then_inc(w_loaded, 16)
            sp.dma_start(wk_raw, wk).then_inc(w_loaded, 16)
            sp.dma_start(wv_raw, wv).then_inc(w_loaded, 16)
            sp.dma_start(Wo[:, :, :], wo.rearrange("(g p) n -> p g n", p=P)).then_inc(w_loaded, 16)
            sp.wait_ge(consts, 2)

            def load_context(b):
                sp.dma_start(c_nat[:, 0:NC - 1, :],
                             ctx_in[b, 0:(NC - 1) * P, :].rearrange("(c p) d -> p c d", p=P)).then_inc(c_loaded, 16)
                sp.dma_start(c_nat[0:LAST, NC - 1, :], ctx_in[b, (NC - 1) * P:N, :]).then_inc(c_loaded, 16)

            def load_residual(b, parity):
                sp.dma_start(acc[:, parity, :, :],
                             x[b, :, :].rearrange("(j p) d -> p j d", p=P)).then_inc(res_loaded, 16)

            load_context(0)
            load_residual(0, 0)

            def body(it, c):
                if c % 2 == 0 and (it is not None or c < STAGES - 2):
                    transposed, scanned = at(it, 26, c // 2 * 13 + 4), at(it, 4, c // 2 * 2 + 1)
                    sp.wait_ge(hi_done, transposed)
                    sp.nop(nofuse=True)
                    sp.wait_ge(col_done, scanned)
                    load_context(at(it, 2, c // 2 + 1))
                    if c > 0:
                        taken(sp, it, use_of(the_plan(it, c), "proj", 0))
                    load_residual(at(it, 2, c // 2 + 1), (c // 2 + 1) % 2)

            stages(sp, body)

        @block.gpsimd
        def _(pool):
            nc.gpsimd.memset(ident[:, :], 0.0).then_inc(consts, 1)
            nc.gpsimd.memset(c_nat[:, NC - 1, :], 0.0).then_inc(consts, 1)
            nc.gpsimd.memset(ones[:, :], 1.0).then_inc(consts, 1)
            nc.gpsimd.memset(ones_b[:, :], 1.0).then_inc(consts, 1)
            pool.wait_ge(consts, 4)
            nc.gpsimd.affine_select(out=ident[:, :], in_=ident[:, :], compare_op=ALU.not_equal, fill=1.0,
                                    base=0, pattern=[[-1, P]], channel_multiplier=1).then_inc(consts, 1)

            def body(it, c):
                for j in range(2, STEPS):
                    half = den[:, (j % 2) * 4 * S:(j % 2 + 1) * 4 * S]
                    if j < 4:
                        pool.wait_ge(den_init, at(it, 8, 2 * c + j - 1))
                    else:
                        pool.wait_ge(den_added, at(it, 4 * (STEPS - 2), c * (STEPS - 2) + j - 3))
                    pool.wait_ge(probs_done, steps_of(it, c, j + 1))
                    nc.gpsimd.tensor_tensor(half, half, probs[:, buffer(c, j), :], ALU.add).then_inc(den_added, 1)

            stages(pool, body)

        @block.tensor
        def _(pe):
            pe.wait_ge(consts, 5)
            pe.wait_ge(w_loaded, 64)
            for g in range(H // 2):
                nc.tensor.transpose(Sc[:, 0, g * P:(g + 1) * P], wq_raw[:, g * P:(g + 1) * P], ident[:, :])
            pe.wait_ge(wk_ready, 1)
            for g in range(H // 2):
                last = nc.tensor.transpose(PV[:, g * P:(g + 1) * P], wk_heads[:, g * P:(g + 1) * P], ident[:, :])
            last.then_inc(wT_filled, 1)
            pe.wait_ge(wT_copied, 2)
            for g in range(H // 2):
                for odd in range(2):
                    rows = slice(HD * odd, HD * odd + HD)
                    last = nc.tensor.matmul(Sc[:, odd, g * P:(g + 1) * P], wqT[rows, g * P:(g + 1) * P],
                                            wkT[rows, g * P:(g + 1) * P], start=True, stop=True)
            last.then_inc(G_filled, 1)
            pe.wait_ge(G_ready, 2)
            pe.wait_ge(wv_ready, 1)

            def split_product(out, a, b, cols_a, cols_b, stop=True):
                nc.tensor.matmul(out, a[0][:, cols_a], b[0][:, cols_b], start=True, stop=False)
                nc.tensor.matmul(out, a[0][:, cols_a], b[1][:, cols_b], start=False, stop=False)
                return nc.tensor.matmul(out, a[1][:, cols_a], b[0][:, cols_b], start=False, stop=stop)

            def item(it, c, kind, i, use):
                bank, s = use % 2, c + 1
                if use >= 2:
                    taken(pe, it, use - 2)
                out = X[:, bank, :]
                if kind == "cT":
                    pe.wait_ge(c_loaded, at(it, 64, 32 * (s // 2 + 1)))
                    for ch in range(4 * i, min(4 * i + 4, NC)):
                        last = nc.tensor.transpose(out[:, ch % 4 * P:(ch % 4 + 1) * P], c_nat[:, ch, :], ident[:, :])
                elif kind == "xT":
                    pe.wait_ge(xn_ready, at(it, 2, s // 2 + 1))
                    for j in range(2):
                        last = nc.tensor.transpose(out[:, j * P:(j + 1) * P], xn_b[:, j, :], ident[:, :])
                elif kind == "mask":
                    pe.wait_ge(flag_done, at(it, 8, s // 2 * 4 + i + 1))
                    w = PIECES[i][1]
                    last = nc.tensor.matmul(out[:, :w], ones_b[:, :], c_flag[:, :w], start=True, stop=True)
                elif kind == "q":
                    for k in range(2):
                        h = s % 2 * G8 + 2 * i + k
                        last = split_product(out[:, k * S:(k + 1) * S], [g[:, h, :] for g in G], xnT,
                                             slice(0, D), slice(0, S))
                elif kind == "v":
                    last = split_product(out, cT[s // 2 % 2], Wv, slice(i * P, (i + 1) * P),
                                         slice(s % 2 * G8 * HD, (s % 2 + 1) * G8 * HD))
                elif kind == "max":
                    off, w = PIECES[i % 4]
                    last = nc.tensor.matmul(out[:, :w], Q[s % 2][0][:, i // 4 * P:(i // 4 + 1) * P],
                                            cT[s // 2 % 2][0][:, off:off + w], start=True, stop=True)
                elif kind == "den":
                    pe.wait_ge(den_added, at(it, 4 * (STEPS - 2), c * (STEPS - 2) - 1 + i))
                    for k in range(2):
                        for odd in range(2):
                            h = 4 * i + 2 * k + odd
                            last = nc.tensor.matmul(out[HD * odd:HD * odd + HD, k * S:(k + 1) * S], ones[:, :],
                                                    den[:, h * S:(h + 1) * S], start=True, stop=True)
                elif kind == "proj":
                    pe.wait_ge(norm_done, at(it, 4, c))
                    for j in range(2):
                        for g in range(4):
                            last = nc.tensor.matmul(out[:, j * D:(j + 1) * D],
                                                    outT[:, g * S + j * P:g * S + (j + 1) * P],
                                                    Wo[:, (c - 1) % 2 * 4 + g, :], start=(g == 0), stop=(g == 3))
                last.then_inc(bank_full[bank], 1)

            def qk(it, c, j, pair):
                if pair == 0:
                    if c > 0 or j > 1:
                        pe.wait_ge(probs_done, steps_of(it, c, j - 1))
                    if j == 0:
                        last_use = first_use(c) - 1
                        taken(pe, it, last_use - 1)
                        taken(pe, it, last_use)
                out = Sc[:, j % 2, pair * 2 * S:(pair + 1) * 2 * S]
                first = (j % 2 * 4 + pair * 2)
                split_product(out, cT[c // 2 % 2], Q[c % 2], slice(j // 2 * P, (j // 2 + 1) * P),
                              slice(first * S, (first + 2) * S), stop=False)
                if j == 0 and pair == 0:
                    pe.wait_ge(shift_steps, at(it, 12, 3 * c + 3))
                last = nc.tensor.matmul(out, ones_b[:, :], shift_diag[:, c % 2, 2 * first:2 * first + 4, :],
                                        start=False, stop=True)
                if pair == 1:
                    last.then_inc(scores_done, 1)

            def pv(it, c, j, pair):
                if pair == 0:
                    pe.wait_ge(probs_done, steps_of(it, c, j + 1))
                    if j < 2 and c > 0:
                        pe.wait_ge(pv_free, at(it, 8, 2 * c - 1 + j))
                for odd in range(2):
                    h = j % 2 * 4 + pair * 2 + odd
                    cols = (j % 2 * 2 + pair) * S
                    last = nc.tensor.matmul(PV[HD * odd:HD * odd + HD, cols:cols + S],
                                            V[:, c % 2, j // 2, h * HD:(h + 1) * HD],
                                            probs[:, buffer(c, j), (pair * 2 + odd) * S:(pair * 2 + odd + 1) * S],
                                            start=(j < 2 and pair == 0), stop=(j >= STEPS - 2), skip_group_check=True)
                if pair == 1:
                    last.then_inc(pv_done, 1)

            def body(it, c):
                tail, prep = flags(it, c)
                slots = the_plan(it, c)
                for j in range(STEPS):
                    for part in range(4):
                        if part < 2:
                            pv(it, c, j, part)
                        elif j + 2 < STEPS:
                            qk(it, c, j + 2, part - 2)
                        elif prep:
                            qk(it, c + 1, j + 2 - STEPS, part - 2)
                        for kind, i, use in slots[4 * j + part]:
                            if use is not None:
                                item(it, c, kind, i, use)

            for kind, i, use in prologue_items():
                item(None, -1, kind, i, use)
            for j in range(2):
                for pair in range(2):
                    qk(None, 0, j, pair)
            stages(pe, body)
            for n, kind in enumerate(("den", "den", "proj")):
                item(None, STAGES, kind, n % 2, first_use(STAGES) + n)

        @block.scalar
        def _(act):
            act.wait_ge(var_ready, 1)
            nc.scalar.activation(stats[:, 1, :], stats[:, 1, :], ACT.Sqrt).then_inc(std_ready, 1)
            act.wait_ge(wT_filled, 1)
            nc.scalar.activation(wqT, Sc[:, 0, :], ACT.Copy).then_inc(wT_copied, 1)
            act.wait_ge(G_filled, 1)
            for odd in range(2):
                heads = G[0].rearrange("p (g two) d -> p two g d", two=2)[:, odd, :, :]
                nc.scalar.activation(heads, Sc[:, odd, :].rearrange("p (g d) -> p g d", d=D), ACT.Copy,
                                     scale=HD ** -0.5).then_inc(G_hi_done, 1)

            def item(it, c, kind, i, use):
                bank, s = use % 2, c + 1
                if kind not in ("cT", "xT", "q", "v"):
                    return
                filled(act, it, use)
                if kind == "cT":
                    w = min(4, NC - 4 * i) * P
                    nc.scalar.activation(cT[s // 2 % 2][0][:, i * 512:i * 512 + w], X[:, bank, :w], ACT.Copy)\
                      .then_inc(hi_done, 1)
                elif kind == "xT":
                    nc.scalar.activation(xnT[0][:, :], X[:, bank, :S], ACT.Copy).then_inc(hi_done, 1)
                elif kind == "q":
                    nc.scalar.activation(Q[s % 2][0][:, i * 512:(i + 1) * 512], X[:, bank, :], ACT.Copy)\
                      .then_inc(hi_done, 1)
                elif kind == "v":
                    nc.scalar.activation(V[:, s % 2, i, :], X[:, bank, :], ACT.Copy).then_inc(bank_free[bank], 1)

            def exp(it, c, j):
                act.wait_ge(scores_done, steps_of(it, c, j + 1))
                if j == 0:
                    act.wait_ge(col_done, at(it, 4, 2 * (c // 2) + 2))
                if c > 0 or j > 3:
                    act.wait_ge(pv_done, steps_of(it, c, j - 3))
                    if j in (4, 5):
                        act.wait_ge(den_init, at(it, 8, 2 * c + j - 3))
                    else:
                        added = j - 5 if j > 5 else j - 3
                        act.wait_ge(den_added, at(it, 4 * (STEPS - 2), c * (STEPS - 2) + added))
                nc.scalar.activation(probs[:, buffer(c, j), :], Sc[:, j % 2, :], ACT.Exp,
                                     bias=mask_col[:, c // 2 % 2, j // 2:j // 2 + 1]).then_inc(probs_done, 1)

            def body(it, c):
                tail, prep = flags(it, c)
                slots = the_plan(it, c)
                for j in range(STEPS):
                    if j + 1 < STEPS:
                        exp(it, c, j + 1)
                    elif prep:
                        exp(it, c + 1, 0)
                    for slot in slots[4 * j:4 * j + 4]:
                        for kind, i, use in slot:
                            item(it, c, kind, i, use) if use is not None else None

            for kind, i, use in prologue_items():
                item(None, -1, kind, i, use)
            exp(None, 0, 0)
            stages(act, body)

        @block.vector
        def _(dve):
            chain = [0]

            def link(ins):
                chain[0] += 1
                ins.then_inc(dve_chain, 1)
                dve.wait_ge(dve_chain, chain[0])

            dve.wait_ge(x_loaded, 16)
            layer_norm(nc, link, XS[:, :, :], XS[:, :, :], squares, stats, var_ready,
                       lambda: dve.wait_ge(std_ready, 1)).then_inc(xn_all, 1)
            dve.wait_ge(w_loaded, 64)
            nc.vector.tensor_copy(wk_heads.rearrange("p (h e) -> p h e", h=H),
                                  wk_raw.rearrange("p (e h) -> p h e", h=H)).then_inc(wk_ready, 1)
            wv_heads = wv_raw.rearrange("p (e h) -> p h e", h=H)
            link(nc.vector.tensor_copy(Wv[0].rearrange("p (h e) -> p h e", h=H), wv_heads))
            nc.vector.tensor_tensor(Wv[1].rearrange("p (h e) -> p h e", h=H), wv_heads,
                                    f32(Wv[0][:, :]).rearrange("p (h e) -> p h e", h=H), ALU.subtract)\
              .then_inc(wv_ready, 1)
            dve.wait_ge(consts, 5)
            dve.wait_ge(wT_filled, 1)
            nc.vector.tensor_copy(wkT, PV[:, :]).then_inc(wT_copied, 1)
            for odd in range(2):
                dve.wait_ge(G_hi_done, odd + 1)
                hi, lo = [g.rearrange("p (g two) d -> p two g d", two=2)[:, odd, :, :] for g in
                          (f32(G[0][:, :, :]), G[1][:, :, :])]
                nc.vector.scalar_tensor_tensor(out=lo, in0=Sc[:, odd, :].rearrange("p (g d) -> p g d", d=D),
                                               scalar=HD ** -0.5, in1=hi, op0=ALU.mult, op1=ALU.subtract)\
                  .then_inc(G_ready, 1)
            dve.wait_ge(xn_all, 1)

            def low_part(it, c, out, hi, bank, w, done):
                dve.wait_ge(hi_done, at(it, 26, done))
                nc.vector.tensor_tensor(out, X[:, bank, :w], f32(hi), ALU.subtract).then_inc(bank_free[bank], 1)

            def item(it, c, kind, i, use):
                s = c + 1
                b, pb = s // 2, s // 2 % 2
                bank = None if use is None else use % 2
                if kind == "cT":
                    if i == 0:
                        filled(dve, it, use)
                        nc.vector.tensor_reduce(c_largest[:, :], c_nat[:, :, :], AX.X, ALU.max,
                                                apply_absolute_value=True).then_inc(col_done, 1)
                        nc.vector.tensor_copy(xn_b[:, :, :], XS[:, bass.ds(at(it, 4, 2 * b), 2), :])\
                          .then_inc(xn_ready, 1)
                        dve.wait_ge(col_done, at(it, 4, 2 * b + 1))
                        nc.vector.tensor_scalar(mask_col[:, pb, :], c_largest[:, :], 0.0, MASKED,
                                                ALU.is_equal, ALU.mult).then_inc(col_done, 1)
                    w = min(4, NC - 4 * i) * P
                    low_part(it, c, cT[pb][1][:, i * 512:i * 512 + w], cT[pb][0][:, i * 512:i * 512 + w], bank, w,
                             13 * b + i + 1)
                elif kind == "xT":
                    low_part(it, c, xnT[1][:, :], xnT[0][:, :], bank, S, 13 * b + 5)
                elif kind == "mask":
                    off, w = PIECES[i]
                    nc.vector.tensor_scalar(c_flag[:, :w], f32(cT[pb][0][:, off:off + w]), 0.0, None, ALU.not_equal)\
                      .then_inc(flag_done, 1)
                    filled(dve, it, use)
                    nc.vector.tensor_scalar(mask_row[:, off:off + w], X[:, bank, :w], 0.0, MASKED,
                                            ALU.is_equal, ALU.mult).then_inc(bank_free[bank], 1)
                elif kind == "q":
                    cols = slice(i * 512, (i + 1) * 512)
                    low_part(it, c, Q[s % 2][1][:, cols], Q[s % 2][0][:, cols], bank, 512,
                             13 * b + (9 if s % 2 else 5) + i + 1)
                elif kind == "max":
                    off, w = PIECES[i % 4]
                    filled(dve, it, use)
                    dve.nop(nofuse=True)
                    nc.vector.tensor_tensor_reduce(out=junk[:, bank, :w], in0=X[:, bank, :w],
                                                   in1=mask_row[:, off:off + w], scale=1.0, scalar=-3e38,
                                                   op0=ALU.add, op1=ALU.max, accum_out=maxes[:, s % 2, i:i + 1])\
                      .then_inc(bank_free[bank], 1)
                elif kind == "shift":
                    taken(dve, it, first_use(c + 1) - 2)
                    taken(dve, it, first_use(c + 1) - 1)
                    steps = [at(it, 12, 3 * s + k) for k in (1, 2)]
                    nc.vector.tensor_reduce(neg_max[:, s % 2, :], maxes[:, s % 2, :].rearrange("p (u k) -> p u k", k=4),
                                            AX.X, ALU.max, negate=True).then_inc(shift_steps, 1)
                    dve.wait_ge(shift_steps, steps[0])
                    nc.vector.tensor_scalar(neg_max[:, s % 2, :], neg_max[:, s % 2, :], 1e20, None, ALU.min)\
                      .then_inc(shift_steps, 1)
                    dve.wait_ge(shift_steps, steps[1])
                    nc.vector.tensor_tensor(shift_diag[:, s % 2, :, :],
                                            ident[:, :].unsqueeze(1).to_broadcast([P, UNITS, P]),
                                            bc(neg_max[:, s % 2, :], P), ALU.mult).then_inc(shift_steps, 1)
                elif kind == "den":
                    if c > 1 or it is not None:
                        dve.wait_ge(norm_done, at(it, 4, c - 1))
                    filled(dve, it, use)
                    nc.vector.tensor_copy(rden[:, i * 512:(i + 1) * 512], X[:, bank, :]).then_inc(bank_free[bank], 1)
                elif kind == "recip":
                    if i % 4 == 0:
                        taken(dve, it, use_of(the_plan(it, c), "den", i // 4))
                    part = rden[:, i * P:(i + 1) * P]
                    nc.vector.reciprocal(part, part).then_inc(recip_done, 1)
                elif kind == "norm":
                    dve.wait_ge(recip_done, at(it, 32, 8 * c))
                    dve.wait_ge(pv_free, at(it, 8, 2 * c))
                    nc.vector.tensor_tensor(outT[:, :], outT[:, :], rden[:, :], ALU.mult).then_inc(norm_done, 1)
                elif kind == "proj":
                    filled(dve, it, use)
                    pb = (c - 1) // 2 % 2
                    psum = X[:, bank, :2 * D].rearrange("p (j d) -> p j d", d=D)
                    if (c - 1) % 2 == 0:
                        dve.wait_ge(res_loaded, at(it, 32, 16 * ((c - 1) // 2 + 1)))
                        out = acc[:, pb, :, :]
                    else:
                        taken(dve, it, use_of(the_plan(it, c - 1), "proj", 0))
                        out = XS[:, bass.ds(at(it, 4, 2 * ((c - 1) // 2)), 2), :]
                    nc.vector.tensor_tensor(out, acc[:, pb, :, :], psum, ALU.add).then_inc(bank_free[bank], 1)

            def copy_outT(it, c):
                for bank in range(2):
                    dve.wait_ge(pv_done, steps_of(it, c, bank - 1))
                    nc.vector.tensor_copy(outT[:, bank * 512:(bank + 1) * 512], PV[:, bank * 512:(bank + 1) * 512])\
                      .then_inc(pv_free, 1)

            def body(it, c):
                tail, prep = flags(it, c)
                slots = the_plan(it, c)
                if tail:
                    copy_outT(it, c)
                for n, slot in enumerate(slots):
                    for kind, i, use in slot:
                        item(it, c, kind, i, use)
                    if n in (3, 7):
                        j = n // 4
                        dve.wait_ge(probs_done, steps_of(it, c, j + 1))
                        nc.vector.tensor_copy(den[:, j * 4 * S:(j + 1) * 4 * S], probs[:, buffer(c, j), :])\
                          .then_inc(den_init, 1)

            for kind, i, use in prologue_items():
                item(None, -1, kind, i, use)
            item(None, -1, "shift", 0, None)
            stages(dve, body)
            copy_outT(None, STAGES)
            last = first_use(STAGES)
            for i in range(2):
                item(None, STAGES, "den", i, last + i)
            taken(dve, None, last)
            taken(dve, None, last + 1)
            for i in range(8):
                part = rden[:, i * P:(i + 1) * P]
                nc.vector.reciprocal(part, part).then_inc(recip_done, 1)
            item(None, STAGES, "norm", 0, None)
            item(None, STAGES, "proj", 0, last + 2)


def moe_0(nc, gate_w, w1, b1, w2, b2, ws1, bs1, ws2, bs2, XS, ident):
    E, F = w1.shape[0], w1.shape[2]
    T = B * S
    TOPK = T * 2
    FC = F // P
    TG = T // 512
    STEPS = FC * TG
    LAG = 3
    ROUNDS = 15
    ROWS = FC * (E + 1) + (E + 1) + E
    B2, GW = FC * (E + 1), FC * (E + 1) + E + 1

    with ExitStack() as es:
        def sb(name, shape, dt=F32):
            return es.enter_context(nc.sbuf_tensor("m_" + name, shape, dt))

        def sem(name):
            return es.enter_context(nc.semaphore("m_" + name))

        xn = sb("xn", [P, TILES, D])
        squares = sb("squares", [P, TILES, D])
        stats = sb("stats", [P, 2, TILES])
        xT = [sb("xT_hi", [P, T], F32R), sb("xT_lo", [P, T], F32R)]
        small = sb("small", [ROWS, D])
        smallT = sb("smallT", [P, ROWS])
        gwT = [sb("gwT_hi", [P, E], F32R), sb("gwT_lo", [P, E], F32R)]
        logits = sb("logits", [P, TILES, E])
        top = sb("top", [P, 2, TILES])
        scores = sb("scores", [P, E, TILES])
        bit_steps = sb("bit_steps", [P, ROUNDS, 3], U32)
        found = sb("found", [P, 1], U32)
        found_bits = sb("found_bits", [P, 1], U32)
        candidates = sb("candidates", [P, 3], U32)
        above = sb("above", [P, 3], BF16)
        passed = sb("passed", [P, 3])
        n_passed = sb("n_passed", [P, 1])
        junk = sb("junk", [P, 3, E * TILES], BF16)
        greater = sb("greater", [P, E * TILES])
        n_greater = sb("n_greater", [P, 1], BF16)
        n_greater_all = sb("n_greater_all", [P, 1])
        equal = sb("equal", [P, E * TILES], BF16)
        zeros = sb("zeros", [P, E * TILES])
        rank = sb("rank", [P, E * TILES])
        gate = sb("gate", [P, E * TILES])
        gateT = sb("gateT", [P, P])
        ones_b = sb("ones_b", [P, P], BF16)
        before = sb("before", [P, P], BF16)
        gate_rows = sb("gate_rows", [P, 2, T])
        w1_raw = sb("w1_raw", [P, 2, F])
        w2_raw = sb("w2_raw", [P, 2, F])
        W1 = [[sb(f"W1_{part}{i}", [P, F], F32R) for part in ("hi", "lo")] for i in range(2)]
        W2 = [[sb(f"W2_{part}{i}", [P, F], F32R) for part in ("hi", "lo")] for i in range(2)]
        h = sb("h", [P, 4, 512])
        h_hi = sb("h_hi", [P, 4, 512], F32R)
        h_lo = sb("h_lo", [P, 4, 512], F32R)
        gated = sb("gated", [P, 2, 512])
        acc = sb("acc", [P, T])
        gate_dram = nc.dram_tensor("gate_scratch", [P, P], F32, kind="Internal").ap()

        U = es.enter_context(nc.psum_tensor("m_up", [P, 4, 512], F32))
        Y = es.enter_context(nc.psum_tensor("m_y", [P, 2, 512], F32))
        R = es.enter_context(nc.psum_tensor("m_route", [P, 2, 512], F32))

        small_loaded, w_loaded = sem("small_loaded"), [sem("w_loaded0"), sem("w_loaded1")]
        consts = sem("consts")
        dve_chain = sem("dve_chain")
        var_ready, std_ready, xn_ready = sem("var_ready"), sem("std_ready"), sem("xn_ready")
        xT_filled, xT_hi_done, xT_done = sem("xT_filled"), sem("xT_hi_done"), sem("xT_done")
        small_filled, small_done = sem("small_filled"), sem("small_done")
        logits_filled, centred, exped, softmax_done = sem("logits_filled"), sem("centred"), sem("exped"), sem("softmax")
        counted, summed = sem("counted"), sem("summed")
        ties_ready, ties_summed = sem("ties_ready"), sem("ties_summed")
        gate_ready, gateT_filled, gateT_done = sem("gate_ready"), sem("gateT_filled"), sem("gateT_done")
        gate_stored, gate_loaded = sem("gate_stored"), [sem("gate_loaded0"), sem("gate_loaded1")]
        w_split, w_hi = sem("w_split"), sem("w_hi")
        up_done, gelu_done, hi_done, lo_done = sem("up_done"), sem("gelu_done"), sem("hi_done"), sem("lo_done")
        down_done, y_taken, added = sem("down_done"), sem("y_taken"), sem("added")
        accT_filled, accT_added = sem("accT_filled"), sem("accT_added")
        block = es.enter_context(nc.Block())

        def experts(eng, body):
            body(None, 0)
            body(None, 1)
            with eng.Fori(0, E // 2 - 1) as it:
                for c in (2, 3):
                    body(it, c)
            body(None, E)

        def step_of(it, c, k):
            return at(it, 2 * STEPS, c * STEPS + k)

        @block.sync
        def _(sp):
            sp.dma_start(small[0:FC, :], bs1.rearrange("(k p) -> k p", p=P)).then_inc(small_loaded, 16)
            sp.dma_start(small[FC:B2, :], b1.rearrange("e (k p) -> (e k) p", p=P)).then_inc(small_loaded, 16)
            sp.dma_start(small[B2:B2 + 1, :], bs2.rearrange("(a d) -> a d", a=1)).then_inc(small_loaded, 16)
            sp.dma_start(small[B2 + 1:GW, :], b2).then_inc(small_loaded, 16)
            sp.dma_start(small[GW:ROWS, :], gate_w).then_inc(small_loaded, 16)

            def load_weights(c, up, down):
                sp.dma_start(w1_raw[:, c % 2, :], up).then_inc(w_loaded[c % 2], 16)
                sp.dma_start(w2_raw[:, c % 2, :].rearrange("p (k d) -> p k d", d=D),
                             down.rearrange("(k p) d -> p k d", p=P)).then_inc(w_loaded[c % 2], 16)

            load_weights(0, ws1, ws2)
            load_weights(1, w1[0, :, :], w2[0, :, :])
            sp.wait_ge(gateT_done, 1)
            sp.dma_start(gate_dram, gateT[:, :]).then_inc(gate_stored, 16)
            sp.wait_ge(gate_stored, 16)

            def load_gate(c, e):
                sp.dma_start(gate_rows[:, c % 2, :].rearrange("p (t q) -> p t q", q=P),
                             gate_dram[bass.ds(e * TILES, TILES), :].partition_broadcast(P))\
                  .then_inc(gate_loaded[c % 2], 16)

            load_gate(1, 0)
            def body(it, c):
                sp.wait_ge(w_split, at(it, 8, 4 * c))
                e = at(it, 2, c)
                load_weights(c + 1, w1[e, :, :], w2[e, :, :])
                if it is not None or c > 1:
                    sp.wait_ge(y_taken, at(it, 2 * TG, c * TG))
                load_gate(c + 1, e)

            body(None, 1)
            with sp.Fori(0, E // 2 - 1) as it:
                for c in (2, 3):
                    body(it, c)

        @block.gpsimd
        def _(pool):
            nc.gpsimd.memset(ones_b[:, :], 1.0).then_inc(consts, 1)
            nc.gpsimd.memset(before[:, :], 1.0).then_inc(consts, 1)
            nc.gpsimd.memset(zeros[:, :], 0.0).then_inc(consts, 1)
            for r in range(ROUNDS):
                for j in range(3):
                    last = nc.gpsimd.memset(bit_steps[:, r, j:j + 1], (j + 1) << 2 * (ROUNDS - 1 - r))
            last.then_inc(consts, 1)
            pool.wait_ge(consts, 4)
            nc.gpsimd.affine_select(out=before[:, :], in_=before[:, :], compare_op=ALU.is_gt, fill=0.0,
                                    base=0, pattern=[[1, P]], channel_multiplier=-1).then_inc(consts, 1)

            def split(it, c):
                pool.wait_ge(w_loaded[c % 2], at(it, 32, 32 * (c // 2 + 1)))
                if it is not None or c >= 2:
                    pool.wait_ge(down_done, step_of(it, c - 1, 0))
                for n, (raw, W) in enumerate(((w1_raw, W1), (w2_raw, W2))):
                    pool.nop(nofuse=True)
                    nc.gpsimd.tensor_copy(W[c % 2][0][:, :], raw[:, c % 2, :]).then_inc(w_split, 1)
                    pool.wait_ge(w_split, at(it, 8, 4 * c + 2 * n + 1))
                    nc.gpsimd.tensor_tensor(W[c % 2][1][:, :], raw[:, c % 2, :], f32(W[c % 2][0][:, :]),
                                            ALU.subtract).then_inc(w_split, 1)

            def body(it, c):
                if c < E:
                    split(it, c + 1)
                for tg in range(TG):
                    if c > 0:
                        cols = acc[:, tg * 512:(tg + 1) * 512]
                        pool.wait_ge(y_taken, at(it, 2 * TG, c * TG + tg + 1))
                        if c > 1:
                            pool.wait_ge(added, at(it, 2 * TG, (c - 2) * TG + tg + 1))
                        nc.gpsimd.tensor_tensor(cols, cols, gated[:, tg % 2, :], ALU.add).then_inc(added, 1)

            split(None, 0)
            experts(pool, body)

        @block.tensor
        def _(pe):
            pe.wait_ge(small_loaded, 80)
            nc.tensor.transpose(R[:, 1, 0:ROWS], small[:, :], ident[0:ROWS, 0:ROWS]).then_inc(small_filled, 1)
            for g in range(4):
                pe.wait_ge(xn_ready, 1)
                for t in range(4):
                    last = nc.tensor.transpose(U[:, g, t * P:(t + 1) * P], xn[:, 4 * g + t, :], ident[:, :])
                last.then_inc(xT_filled, 1)
            pe.wait_ge(small_done, 3)
            for t in range(TILES):
                if t % 4 == 0:
                    pe.wait_ge(xT_done, t // 4 + 1)
                out, cols = R[:, 0, t * E:(t + 1) * E], slice(t * P, (t + 1) * P)
                nc.tensor.matmul(out, xT[0][:, cols], gwT[0][:, :], start=True, stop=False)
                nc.tensor.matmul(out, xT[0][:, cols], gwT[1][:, :], start=False, stop=False)
                last = nc.tensor.matmul(out, xT[1][:, cols], gwT[0][:, :], start=False, stop=True)
            last.then_inc(logits_filled, 1)

            def up(it, c, k):
                tg, fc = k // FC, k % FC
                if k == 0:
                    pe.wait_ge(w_split, at(it, 8, 4 * c + 4))
                if it is not None or c * STEPS + k >= 4:
                    pe.wait_ge(gelu_done, step_of(it, c, k - 3))
                out, W = U[:, k % 4, :], W1[c % 2]
                cols, tok = slice(fc * P, (fc + 1) * P), slice(tg * 512, (tg + 1) * 512)
                nc.tensor.matmul(out, W[0][:, cols], xT[0][:, tok], start=True, stop=False)
                nc.tensor.matmul(out, W[0][:, cols], xT[1][:, tok], start=False, stop=False)
                nc.tensor.matmul(out, W[1][:, cols], xT[0][:, tok], start=False, stop=True).then_inc(up_done, 1)

            def down(it, c, k):
                tg, fc = k // FC, k % FC
                pe.wait_ge(lo_done, step_of(it, c, k + 1))
                if fc == 0 and (it is not None or c * TG + tg >= 2):
                    pe.wait_ge(y_taken, at(it, 2 * TG, c * TG + tg - 1))
                out, W, cols = Y[:, tg % 2, :], W2[c % 2], slice(fc * P, (fc + 1) * P)
                nc.tensor.matmul(out, W[0][:, cols], h_hi[:, k % 4, :], start=(fc == 0), stop=False)
                nc.tensor.matmul(out, W[0][:, cols], h_lo[:, k % 4, :], start=False, stop=False)
                nc.tensor.matmul(out, W[1][:, cols], h_hi[:, k % 4, :], start=False, stop=(fc == FC - 1))\
                  .then_inc(down_done, 1)

            def body(it, c):
                for k in range(STEPS):
                    up(it, c, k)
                    if k >= LAG:
                        down(it, c, k - LAG)
                    elif c > 0:
                        down(it, c - 1, STEPS + k - LAG)
                    if c == 0:
                        if k < ROUNDS:
                            pe.wait_ge(counted, 3 * (k + 1))
                            nc.tensor.matmul(R[:, 1, 0:3], ones_b[:, :], above[:, :], start=True, stop=True)\
                              .then_inc(summed, 1)
                        else:
                            pe.wait_ge(ties_ready, 2)
                            nc.tensor.matmul(R[:, 0, 0:1], ones_b[:, :], n_greater[:, :], start=True, stop=True)
                            nc.tensor.matmul(R[:, 0, P:2 * P], ones_b[:, :], equal[:, :], start=True, stop=True)
                            nc.tensor.matmul(R[:, 0, 2 * P:3 * P], before[:, :], equal[:, :], start=True,
                                             stop=True).then_inc(ties_summed, 1)
                            pe.wait_ge(gate_ready, 1)
                            nc.tensor.transpose(R[:, 1, P:2 * P], gate[:, :], ident[:, :]).then_inc(gateT_filled, 1)

            pe.wait_ge(consts, 5)
            experts(pe, body)
            for k in range(STEPS - LAG, STEPS):
                down(None, E, k)
            pe.wait_ge(added, E * TG)
            for g in range(4):
                for t in range(4):
                    tile = 4 * g + t
                    last = nc.tensor.transpose(U[:, g, t * P:(t + 1) * P], acc[:, tile * P:(tile + 1) * P], ident[:, :])
                last.then_inc(accT_filled, 1)

        @block.scalar
        def _(act):
            act.wait_ge(var_ready, 1)
            nc.scalar.activation(stats[:, 1, :], stats[:, 1, :], ACT.Sqrt).then_inc(std_ready, 1)
            for g in range(4):
                act.wait_ge(xT_filled, g + 1)
                nc.scalar.activation(xT[0][:, g * 512:(g + 1) * 512], U[:, g, :], ACT.Copy).then_inc(xT_hi_done, 1)
            act.wait_ge(centred, 1)
            nc.scalar.activation(logits[:, :, :], logits[:, :, :], ACT.Exp).then_inc(exped, 1)
            act.wait_ge(xT_done, 4)

            def body(it, c):
                for k in range(STEPS):
                    act.wait_ge(up_done, step_of(it, c, k + 1))
                    if it is not None or c * STEPS + k >= 4:
                        act.wait_ge(lo_done, step_of(it, c, k - 3))
                    col = at(it, 2 * FC, c * FC + k % FC)
                    act.nop(nofuse=True)
                    nc.scalar.activation(h[:, k % 4, :], U[:, k % 4, :], ACT.Gelu_apprx_tanh,
                                         bias=smallT[:, bass.ds(col, 1)]).then_inc(gelu_done, 1)

            experts(act, body)

        @block.vector
        def _(dve):
            chain = [0]

            def link(ins):
                chain[0] += 1
                ins.then_inc(dve_chain, 1)
                dve.wait_ge(dve_chain, chain[0])

            layer_norm(nc, link, XS[:, :, :], xn[:, :, :], squares[:, :, :], stats, var_ready,
                       lambda: dve.wait_ge(std_ready, 1)).then_inc(xn_ready, 1)
            dve.wait_ge(small_filled, 1)
            nc.vector.tensor_copy(smallT[:, :], R[:, 1, 0:ROWS]).then_inc(small_done, 1)
            dve.wait_ge(small_done, 1)
            nc.vector.tensor_copy(gwT[0][:, :], smallT[:, GW:ROWS]).then_inc(small_done, 1)
            dve.wait_ge(small_done, 2)
            nc.vector.tensor_tensor(gwT[1][:, :], smallT[:, GW:ROWS], f32(gwT[0][:, :]), ALU.subtract)\
              .then_inc(small_done, 1)
            for g in range(4):
                cols = slice(g * 512, (g + 1) * 512)
                dve.wait_ge(xT_hi_done, g + 1)
                nc.vector.tensor_tensor(xT[1][:, cols], U[:, g, :], f32(xT[0][:, cols]), ALU.subtract)\
                  .then_inc(xT_done, 1)
            dve.wait_ge(logits_filled, 1)
            L = R[:, 0, 0:TILES * E].rearrange("p (t e) -> p t e", e=E)
            link(nc.vector.tensor_reduce(top[:, 0, :], L, AX.X, ALU.max))
            nc.vector.tensor_tensor(logits[:, :, :], L, bc(top[:, 0, :], E), ALU.subtract).then_inc(centred, 1)
            dve.wait_ge(exped, 1)
            link(nc.vector.tensor_reduce(top[:, 1, :], logits[:, :, :], AX.X, ALU.add))
            link(nc.vector.reciprocal(top[:, 1, :], top[:, 1, :]))
            link(nc.vector.tensor_tensor(scores[:, :, :].rearrange("p e t -> p t e"), logits[:, :, :],
                                         bc(top[:, 1, :], E), ALU.mult))
            flat = scores[:, :, :].rearrange("p e t -> p (e t)")
            dve.wait_ge(consts, 5)
            link(nc.vector.memset(found[:, :], 0))
            link(nc.vector.tensor_copy(candidates[:, :], bit_steps[:, 0, :]))

            def count():
                for j in range(3):
                    nc.vector.tensor_scalar(junk[:, j, :], flat, f32(candidates[:, j:j + 1]), None, ALU.is_ge, ALU.add,
                                            accum_out=above[:, j:j + 1]).then_inc(counted, 1)

            def narrow(r):
                dve.wait_ge(summed, r + 1)
                link(nc.vector.tensor_scalar(passed[:, :], R[:, 1, 0:3], float(TOPK), None, ALU.is_ge, ALU.add,
                                             accum_out=n_passed[:, :]))
                link(nc.vector.tensor_scalar(found_bits[:, :], n_passed[:, :], float(1 << 2 * (ROUNDS - 1 - r)), None,
                                             ALU.mult))
                link(nc.vector.tensor_tensor(found[:, :], found[:, :], found_bits[:, :], ALU.bitwise_or))
                if r + 1 < ROUNDS:
                    link(nc.vector.tensor_tensor(candidates[:, :], bit_steps[:, r + 1, :],
                                                 found[:, :].to_broadcast([P, 3]), ALU.bitwise_or))

            def tie_counts():
                threshold = f32(found[:, :])
                nc.vector.tensor_scalar(greater[:, :], flat, threshold, None, ALU.is_gt, ALU.add,
                                        accum_out=n_greater[:, :]).then_inc(ties_ready, 1)
                nc.vector.tensor_scalar(equal[:, :], flat, threshold, None, ALU.is_equal).then_inc(ties_ready, 1)

            def select():
                dve.wait_ge(ties_summed, 1)
                per_column, rows_before = R[:, 0, P:2 * P], R[:, 0, 2 * P:3 * P]
                link(nc.vector.tensor_copy(n_greater_all[:, :], R[:, 0, 0:1]))
                link(nc.vector.tensor_tensor_scan(rank[:, :], zeros[:, :], per_column, 0.0, ALU.add, ALU.add))
                link(nc.vector.tensor_tensor(rank[:, :], rank[:, :], per_column, ALU.subtract))
                link(nc.vector.tensor_tensor(rank[:, :], rank[:, :], rows_before, ALU.add))
                link(nc.vector.tensor_scalar(rank[:, :], rank[:, :], n_greater_all[:, 0:1], float(TOPK), ALU.add,
                                             ALU.is_lt))
                link(nc.vector.tensor_tensor(rank[:, :], rank[:, :], equal[:, :], ALU.mult))
                link(nc.vector.tensor_tensor(rank[:, :], rank[:, :], greater[:, :], ALU.add))
                nc.vector.tensor_tensor(gate[:, :], rank[:, :], flat, ALU.mult).then_inc(gate_ready, 1)
                dve.wait_ge(gateT_filled, 1)
                nc.vector.tensor_copy(gateT[:, :], R[:, 1, P:2 * P]).then_inc(gateT_done, 1)

            def cut(it, c, k):
                dve.wait_ge(gelu_done, step_of(it, c, k + 1))
                if it is not None or c * STEPS + k >= 4:
                    dve.wait_ge(down_done, step_of(it, c, k - 3))
                nc.vector.tensor_copy(h_hi[:, k % 4, :], h[:, k % 4, :]).then_inc(hi_done, 1)
                dve.wait_ge(hi_done, step_of(it, c, k + 1))
                nc.vector.tensor_tensor(h_lo[:, k % 4, :], h[:, k % 4, :], f32(h_hi[:, k % 4, :]), ALU.subtract)\
                  .then_inc(lo_done, 1)

            def take_y(it, c, tg):
                dve.wait_ge(down_done, step_of(it, c, (tg + 1) * FC))
                bias = smallT[:, bass.ds(at(it, 2, B2 + c), 1)]
                if c == 0:
                    nc.vector.tensor_scalar(acc[:, tg * 512:(tg + 1) * 512], Y[:, tg % 2, :], bias, None, ALU.add)\
                      .then_inc(y_taken, 1)
                    return
                if tg == 0:
                    dve.wait_ge(gate_loaded[c % 2], at(it, 16, 16 * ((c + 1) // 2)))
                if c > 1 or tg >= 2:
                    dve.wait_ge(added, at(it, 2 * TG, (c - 1) * TG + tg - 1))
                nc.vector.scalar_tensor_tensor(out=gated[:, tg % 2, :], in0=Y[:, tg % 2, :], scalar=bias,
                                               in1=gate_rows[:, c % 2, tg * 512:(tg + 1) * 512], op0=ALU.add,
                                               op1=ALU.mult).then_inc(y_taken, 1)

            def body(it, c):
                for k in range(STEPS):
                    if c == 0:
                        if k > 0 and k <= ROUNDS:
                            narrow(k - 1)
                        if k < ROUNDS:
                            count()
                        else:
                            tie_counts()
                            select()
                    cut(it, c, k)
                    if k % FC == FC - 1:
                        if k >= FC:
                            take_y(it, c, k // FC - 1)
                        elif c > 0:
                            take_y(it, c - 1, TG - 1)

            experts(dve, body)
            take_y(None, E, TG - 1)
            for g in range(4):
                dve.wait_ge(accT_filled, g + 1)
                rows = XS[:, 4 * g:4 * g + 4, :]
                nc.vector.tensor_tensor(rows, rows, U[:, g, :].rearrange("p (t d) -> p t d", d=D), ALU.add)\
                  .then_inc(accT_added, 1)


def attention_1(nc, ctx_in, wq, bq, wk, bk, wv, bv, wr, br, XS, ident):
    STEPS = (NC + 1) // 2
    SLOTS = 2 * STEPS
    STAGES = B
    PIECES = [(0, 402), (402, 400), (802, 400), (1202, 400)]
    TWO_PI = 6.2831850
    ROUND = float(3 << 22)

    PREP_USES, TAIL_USES = 16, 2

    def first_use(c):
        return PREP_USES * (1 + min(c, STAGES - 1)) + TAIL_USES * max(c - 1, 0)

    def plan(c, tail, prep):
        slots = [[] for _ in range(SLOTS)]
        if prep:
            for i in range(4):
                slots[i].append(("cT", i))
                slots[i + 2].append(("angle", i))
            for i in range(8):
                slots[6 + i // 2].append(("max", i))
            slots[9].append(("shift", 0))
        if tail:
            slots[1].append(("den", 0))
            slots[1].append(("norm", 0))
            slots[5].append(("proj", 0))
        use, out = first_use(c), []
        for slot in slots:
            row = []
            for kind, i in slot:
                takes = kind not in ("norm", "shift")
                row.append((kind, i, use if takes else None))
                use += takes
            out.append(row)
        return out

    with ExitStack() as es:
        def sb(name, shape, dt=F32):
            return es.enter_context(nc.sbuf_tensor("b_" + name, shape, dt))

        def sem(name):
            return es.enter_context(nc.semaphore("b_" + name))

        xn = sb("xn", [P, TILES, D])
        squares = sb("squares", [P, TILES, D])
        stats = sb("stats", [P, 2, TILES])
        xT = [sb("xT_hi", [P, B * S], F32R), sb("xT_lo", [P, B * S], F32R)]
        Qf = sb("Qf", [P, B * S])
        w_raw = sb("w_raw", [P, 4, D])
        wkT = sb("wkT", [P, D])
        Wq = [sb("Wq_hi", [P, D], F32R), sb("Wq_lo", [P, D], F32R)]
        Wkr = [sb("Wkr_hi", [P, D], F32R), sb("Wkr_lo", [P, D], F32R)]
        b_rows = sb("b_rows", [3, D])
        b_cols = sb("b_cols", [P, 3])
        bv_row = sb("bv_row", [1, D])
        turn = sb("turn", [P, 2])
        c_in = sb("c_in", [P, NC, D])
        c_nat = sb("c_nat", [P, 2, NC, D])
        cT = [sb("cT_hi", [P, NC * P], F32R), sb("cT_lo", [P, NC * P], F32R)]
        turns = sb("turns", [P, 4, 402])
        whole = sb("whole", [P, 4, 402])
        cosT = sb("cosT", [P, 4, 402])
        K = [[sb(f"K_{part}{i}", [P, NC * P], F32R) for part in ("hi", "lo")] for i in range(2)]
        Qs = [[sb(f"Qs_{part}{i}", [P, S], F32R) for part in ("hi", "lo")] for i in range(2)]
        maxes = sb("maxes", [P, 2, 8])
        neg_max = sb("neg_max", [P, 2, 2])
        shift_diag = sb("shift_diag", [P, 2, 2, P], BF16)
        probs = sb("probs", [P, 4, 2 * S])
        den = sb("den", [P, 2 * S])
        outT = sb("outT", [P, S])
        rden = sb("rden", [P, S])
        ones = sb("ones", [P, P])
        ones_b = sb("ones_b", [P, P], BF16)

        Sc = es.enter_context(nc.psum_tensor("b_scores", [P, 4, 512], F32))
        PV = es.enter_context(nc.psum_tensor("b_pv", [P, 2, 512], F32))
        X = es.enter_context(nc.psum_tensor("b_work", [P, 2, 512], F32))

        w_loaded, c_in_loaded, c_loaded = sem("w_loaded"), sem("c_in_loaded"), [sem("c_loaded0"), sem("c_loaded1")]
        consts, dve_chain = sem("consts"), sem("dve_chain")
        var_ready, std_ready, xn_ready = sem("var_ready"), sem("std_ready"), sem("xn_ready")
        wT_filled, wT_done = sem("wT_filled"), sem("wT_done")
        wkr_filled, w_ready = sem("wkr_filled"), sem("w_ready")
        xT_filled, xT_hi_done, xT_done = sem("xT_filled"), sem("xT_hi_done"), sem("xT_done")
        q_filled, q_biased, q_done = sem("q_filled"), sem("q_biased"), sem("q_done")
        bank_full = [sem("bank0_full"), sem("bank1_full")]
        bank_free = [sem("bank0_free"), sem("bank1_free")]
        qs_ready = sem("qs_ready")
        c_hi_done = sem("c_hi_done")
        angle_steps = sem("angle_steps")
        cos_done, k_hi_done, k_lo_done = sem("cos_done"), sem("k_hi_done"), sem("k_lo_done")
        shift_steps = sem("shift_steps")
        scores_done, probs_done, pv_done = sem("scores_done"), sem("probs_done"), sem("pv_done")
        den_added, norm_done = sem("den_added"), sem("norm_done")
        block = es.enter_context(nc.Block())

        TURN = first_use(3) - first_use(1)
        assert TURN % 2 == 0

        def filled(eng, it, use):
            eng.wait_ge(bank_full[use % 2], at(it, TURN // 2, use // 2 + 1))

        def taken(eng, it, use):
            eng.wait_ge(bank_free[use % 2], at(it, TURN // 2, use // 2 + 1))

        def stages(eng, body):
            body(None, 0)
            with eng.Fori(0, 3) as it:
                for c in (1, 2):
                    body(it, c)
            body(None, STAGES - 1)

        def flags(it, c):
            return c > 0, it is not None or c + 1 < STAGES

        def the_plan(it, c):
            return plan(c, *flags(it, c))

        def step_of(it, c, first):
            return at(it, 2 * STEPS, c * STEPS + first)

        def before_in_buffer(it, c, j):
            if j >= 4:
                return step_of(it, c, j - 3)
            return step_of(it, c - 1, (j + 4 if j < 3 else 3) + 1)

        def rows_of(j, k):
            return LAST if 2 * j + k == NC - 1 else P

        def chunks_of(j):
            return min(2, NC - 2 * j)

        @block.sync
        def _(sp):
            for i, w in enumerate((wq, wk, wr, wv)):
                sp.dma_start(w_raw[:, i, :], w).then_inc(w_loaded, 16)
            for i, b in enumerate((bq, bk, br)):
                sp.dma_start(b_rows[i:i + 1, :], b.rearrange("(a d) -> a d", a=1)).then_inc(w_loaded, 16)
            sp.dma_start(bv_row[:, :], bv.rearrange("(a d) -> a d", a=1)).then_inc(w_loaded, 16)
            sp.wait_ge(consts, 1)

            def load(dst, b, loaded):
                sp.dma_start(dst[:, 0:NC - 1, :],
                             ctx_in[b, 0:(NC - 1) * P, :].rearrange("(c p) d -> p c d", p=P)).then_inc(loaded, 16)
                sp.dma_start(dst[0:LAST, NC - 1, :], ctx_in[b, (NC - 1) * P:N, :]).then_inc(loaded, 16)

            def load_for_transposes(it, s):
                sp.wait_ge(c_hi_done, at(it, 8, 4 * s))
                load(c_in[:, :, :], at(it, 2, s), c_in_loaded)

            load(c_in[:, :, :], 0, c_in_loaded)
            load(c_nat[:, 0, :, :], 0, c_loaded[0])
            load_for_transposes(None, 1)
            load(c_nat[:, 1, :, :], 1, c_loaded[1])

            with sp.Fori(0, 3) as it:
                for c in (1, 2):
                    load_for_transposes(it, c + 1)
                    sp.wait_ge(pv_done, step_of(it, c, 0))
                    load(c_nat[:, (c + 1) % 2, :, :], at(it, 2, c + 1), c_loaded[(c + 1) % 2])

        @block.gpsimd
        def _(pool):
            nc.gpsimd.memset(c_in[:, NC - 1, :], 0.0).then_inc(consts, 1)
            nc.gpsimd.memset(ones[:, :], 1.0).then_inc(consts, 1)
            nc.gpsimd.memset(ones_b[:, :], 1.0).then_inc(consts, 1)

            def body(it, c):
                for j in range(1, STEPS - 1):
                    pool.wait_ge(probs_done, step_of(it, c, j + 1))
                    if j == 1:
                        if c > 0:
                            filled(pool, it, [u for s in the_plan(it, c) for k, i, u in s if k == "den"][0])
                        first = probs[:, 0, :]
                    else:
                        pool.wait_ge(den_added, at(it, 2 * (STEPS - 2), c * (STEPS - 2) + j - 1))
                        first = den[:, :]
                    nc.gpsimd.tensor_tensor(den[:, :], first, probs[:, j % 4, :], ALU.add).then_inc(den_added, 1)

            stages(pool, body)

        @block.tensor
        def _(pe):
            pe.wait_ge(w_loaded, 128)
            nc.tensor.transpose(X[:, 0, 0:D], w_raw[:, 1, :], ident[:, :])
            nc.tensor.transpose(X[:, 0, D:D + 3], b_rows[:, :], ident[0:3, 0:3]).then_inc(wT_filled, 1)
            pe.wait_ge(wT_done, 2)
            nc.tensor.matmul(X[:, 1, 0:D], wkT[:, :], w_raw[:, 2, :], start=True, stop=True)
            nc.tensor.matmul(X[:, 1, D:D + 1], w_raw[:, 2, :], b_cols[:, 1:2], start=True, stop=True)\
              .then_inc(wkr_filled, 1)
            pe.wait_ge(xn_ready, 1)
            for g in range(4):
                for t in range(4):
                    last = nc.tensor.transpose(Sc[:, g, t * P:(t + 1) * P], xn[:, 4 * g + t, :], ident[:, :])
                last.then_inc(xT_filled, 1)
            pe.wait_ge(w_ready, 2)

            def split_product(out, a, b, cols_a, cols_b, stop=True):
                nc.tensor.matmul(out, a[0][:, cols_a], b[0][:, cols_b], start=True, stop=False)
                nc.tensor.matmul(out, a[0][:, cols_a], b[1][:, cols_b], start=False, stop=False)
                return nc.tensor.matmul(out, a[1][:, cols_a], b[0][:, cols_b], start=False, stop=stop)

            for g in range(4):
                pe.wait_ge(xT_done, g + 1)
                if g >= 2:
                    pe.wait_ge(q_done, g - 1)
                split_product(PV[:, g % 2, :], Wq, xT, slice(0, D), slice(g * 512, (g + 1) * 512)).then_inc(q_filled, 1)
            pe.wait_ge(w_ready, 5)
            pe.wait_ge(q_done, 4)

            def item(it, c, kind, i, use):
                bank, s = use % 2, c + 1
                if use >= 2:
                    taken(pe, it, use - 2)
                out = X[:, bank, :]
                if kind == "cT":
                    pe.wait_ge(c_in_loaded, at(it, 64, 32 * (s + 1)))
                    for ch in range(4 * i, min(4 * i + 4, NC)):
                        last = nc.tensor.transpose(out[:, ch % 4 * P:(ch % 4 + 1) * P], c_in[:, ch, :],
                                                   ident[:, :])
                elif kind == "angle":
                    off, w = PIECES[i]
                    last = split_product(out[:, :w], Wkr, cT, slice(0, D), slice(off, off + w))
                elif kind == "max":
                    off, w = PIECES[i % 4]
                    if i < 4:
                        pe.wait_ge(k_hi_done, at(it, 8, 4 * s + i + 1))
                    if i == 0:
                        pe.wait_ge(qs_ready, at(it, 4, 2 * s + 2))
                    last = nc.tensor.matmul(out[:, :w], Qs[s % 2][0][:, i // 4 * P:(i // 4 + 1) * P],
                                            K[s % 2][0][:, off:off + w], start=True, stop=True)
                elif kind == "den":
                    pe.wait_ge(den_added, at(it, 2 * (STEPS - 2), c * (STEPS - 2)))
                    for k in range(2):
                        nc.tensor.matmul(out[:, 0:S], ones[:, :], den[:, k * S:(k + 1) * S], start=(k == 0), stop=False)
                    last = nc.tensor.matmul(out[:, 0:S], ones[0:LAST, :], probs[0:LAST, (STEPS - 1) % 4, 0:S],
                                            start=False, stop=True)
                elif kind == "proj":
                    pe.wait_ge(norm_done, at(it, 2, c))
                    for j in range(2):
                        half = out[:, j * D:(j + 1) * D]
                        nc.tensor.matmul(half, outT[:, j * P:(j + 1) * P], w_raw[:, 3, :], start=True, stop=False)
                        last = nc.tensor.matmul(half, ones[0:1, :], bv_row[:, :], start=False, stop=True)
                last.then_inc(bank_full[bank], 1)

            def qk(it, c, j, k):
                if k == 0:
                    if c > 0 or j > 3:
                        pe.wait_ge(probs_done, before_in_buffer(it, c, j))
                    if j == 0:
                        pe.wait_ge(shift_steps, at(it, 4, 2 * c + 2))
                        pe.wait_ge(k_lo_done, at(it, 8, 4 * c + 4))
                if k >= chunks_of(j):
                    return
                rows = rows_of(j, k)
                out = Sc[0:rows, j % 4, k * S:(k + 1) * S]
                first = (2 * j + k) * P
                split_product(out, K[c % 2], Qs[c % 2], slice(first, first + rows), slice(0, S), stop=False)
                last = nc.tensor.matmul(out, ones_b[:, 0:rows], shift_diag[:, c % 2, :, :], start=False, stop=True)
                if k == chunks_of(j) - 1:
                    last.then_inc(scores_done, 1)

            def pv(it, c, j, k):
                if k == 0:
                    pe.wait_ge(probs_done, step_of(it, c, j + 1))
                    if j == 0:
                        pe.wait_ge(c_loaded[c % 2], at(it, 32, 32 * (c // 2 + 1)))
                        if c > 1:
                            pe.wait_ge(norm_done, at(it, 2, c - 1))
                if k >= chunks_of(j):
                    return
                rows = rows_of(j, k)
                last = nc.tensor.matmul(PV[:, c % 2, 0:S], c_nat[0:rows, c % 2, 2 * j + k, :],
                                        probs[0:rows, j % 4, k * S:(k + 1) * S],
                                        start=(j == 0 and k == 0), stop=(j == STEPS - 1))
                if k == chunks_of(j) - 1:
                    last.then_inc(pv_done, 1)

            def body(it, c):
                tail, prep = flags(it, c)
                slots = the_plan(it, c)
                for j in range(STEPS):
                    for k in range(2):
                        pv(it, c, j, k)
                        if j + 2 < STEPS:
                            qk(it, c, j + 2, k)
                        elif prep:
                            qk(it, c + 1, j + 2 - STEPS, k)
                        for kind, i, use in slots[2 * j + k]:
                            if use is not None:
                                item(it, c, kind, i, use)

            pe.wait_ge(consts, 3)
            for use, (kind, i) in enumerate([("cT", i) for i in range(4)] + [("angle", i) for i in range(4)] +
                                            [("max", i) for i in range(8)]):
                item(None, -1, kind, i, use)
            for j in range(2):
                for k in range(2):
                    qk(None, 0, j, k)
            stages(pe, body)
            for n, kind in enumerate(("den", "proj")):
                item(None, STAGES, kind, 0, first_use(STAGES) + n)

        @block.scalar
        def _(act):
            act.wait_ge(var_ready, 1)
            nc.scalar.activation(stats[:, 1, :], stats[:, 1, :], ACT.Sqrt).then_inc(std_ready, 1)
            for g in range(4):
                act.wait_ge(xT_filled, g + 1)
                nc.scalar.activation(xT[0][:, g * 512:(g + 1) * 512], Sc[:, g, :], ACT.Copy).then_inc(xT_hi_done, 1)
            act.wait_ge(wT_done, 2)
            for g in range(4):
                act.wait_ge(q_filled, g + 1)
                nc.scalar.activation(Qf[:, g * 512:(g + 1) * 512], PV[:, g % 2, :], ACT.Identity, bias=b_cols[:, 0:1])\
                  .then_inc(q_done, 1)

            def item(it, c, kind, i, use):
                s = c + 1
                if kind == "cT":
                    filled(act, it, use)
                    w = min(4, NC - 4 * i) * P
                    nc.scalar.activation(cT[0][:, i * 512:i * 512 + w], X[:, use % 2, :w], ACT.Copy)\
                      .then_inc(c_hi_done, 1)
                elif kind == "angle":
                    off, w = PIECES[i]
                    act.wait_ge(angle_steps, at(it, 24, 12 * s + 3 * i + 3))
                    if s > 0:
                        act.wait_ge(k_lo_done, at(it, 8, 4 * s + i - 3))
                    nc.scalar.activation(cosT[:, i, :w], turns[:, i, :w], ACT.Sin, scale=TWO_PI)\
                      .then_inc(cos_done, 1)
                    act.wait_ge(cos_done, at(it, 8, 4 * s + i + 1))
                    nc.scalar.activation(K[s % 2][0][:, off:off + w], cosT[:, i, :w], ACT.Copy)\
                      .then_inc(k_hi_done, 1)

            def exp(it, c, j):
                act.wait_ge(scores_done, step_of(it, c, j + 1))
                if c > 0 or j > 3:
                    act.wait_ge(pv_done, before_in_buffer(it, c, j))
                if j >= 4:
                    act.wait_ge(den_added, at(it, 2 * (STEPS - 2), c * (STEPS - 2) + (j - 4 or 1)))
                elif c > 0 and j == 2:
                    filled(act, it, [u for s in the_plan(it, c) for k, i, u in s if k == "den"][0])
                elif c > 0:
                    act.wait_ge(den_added, at(it, 2 * (STEPS - 2), (c - 1) * (STEPS - 2) + (j + 4 if j < 2 else j)))
                rows, cols = rows_of(j, 0) if chunks_of(j) == 1 else P, chunks_of(j) * S
                nc.scalar.activation(probs[0:rows, j % 4, 0:cols], Sc[0:rows, j % 4, 0:cols], ACT.Exp)\
                  .then_inc(probs_done, 1)

            def body(it, c):
                tail, prep = flags(it, c)
                slots = the_plan(it, c)
                for j in range(STEPS):
                    if j + 1 < STEPS:
                        exp(it, c, j + 1)
                    elif prep:
                        exp(it, c + 1, 0)
                    for slot in slots[2 * j:2 * j + 2]:
                        for kind, i, use in slot:
                            item(it, c, kind, i, use)

            for use, (kind, i) in enumerate([("cT", i) for i in range(4)] + [("angle", i) for i in range(4)]):
                item(None, -1, kind, i, use)
            exp(None, 0, 0)
            stages(act, body)

        @block.vector
        def _(dve):
            chain = [0]

            def link(ins):
                chain[0] += 1
                ins.then_inc(dve_chain, 1)
                dve.wait_ge(dve_chain, chain[0])

            dve.wait_ge(wT_filled, 1)
            nc.vector.tensor_copy(wkT[:, :], X[:, 0, 0:D]).then_inc(wT_done, 1)
            nc.vector.tensor_copy(b_cols[:, :], X[:, 0, D:D + 3]).then_inc(wT_done, 1)
            link(nc.vector.tensor_copy(Wq[0][:, :], w_raw[:, 0, :]))
            nc.vector.tensor_tensor(Wq[1][:, :], w_raw[:, 0, :], f32(Wq[0][:, :]), ALU.subtract).then_inc(w_ready, 2)
            layer_norm(nc, link, XS[:, :, :], xn[:, :, :], squares[:, :, :], stats, var_ready,
                       lambda: dve.wait_ge(std_ready, 1)).then_inc(xn_ready, 1)
            dve.wait_ge(wkr_filled, 1)
            link(nc.vector.tensor_copy(Wkr[0][:, :], X[:, 1, 0:D]))
            nc.vector.tensor_tensor(Wkr[1][:, :], X[:, 1, 0:D], f32(Wkr[0][:, :]), ALU.subtract).then_inc(w_ready, 1)
            link(nc.vector.tensor_tensor(turn[:, 0:1], X[:, 1, D:D + 1], b_cols[:, 2:3], ALU.add))
            nc.vector.tensor_scalar(turn[:, 1:2], turn[:, 0:1], 1.0 / (2.0 * math.pi), 0.25, ALU.mult, ALU.add)\
              .then_inc(w_ready, 2)
            for g in range(4):
                cols = slice(g * 512, (g + 1) * 512)
                dve.wait_ge(xT_hi_done, g + 1)
                nc.vector.tensor_tensor(xT[1][:, cols], Sc[:, g, :], f32(xT[0][:, cols]), ALU.subtract).then_inc(xT_done, 1)
            dve.wait_ge(q_done, 4)
            dve.wait_ge(w_ready, 5)

            def take_q(it, s):
                rows = Qf[:, bass.ds(at(it, 2 * S, s * S), S)]
                nc.vector.tensor_copy(Qs[s % 2][0][:, :], rows).then_inc(qs_ready, 1)
                dve.wait_ge(qs_ready, at(it, 4, 2 * s + 1))
                nc.vector.tensor_tensor(Qs[s % 2][1][:, :], rows, f32(Qs[s % 2][0][:, :]), ALU.subtract)\
                  .then_inc(qs_ready, 1)

            def item(it, c, kind, i, use):
                s = c + 1
                bank = None if use is None else use % 2
                if kind == "cT":
                    w = min(4, NC - 4 * i) * P
                    cols = slice(i * 512, i * 512 + w)
                    dve.wait_ge(c_hi_done, at(it, 8, 4 * s + i + 1))
                    nc.vector.tensor_tensor(cT[1][:, cols], X[:, bank, :w], f32(cT[0][:, cols]), ALU.subtract)\
                      .then_inc(bank_free[bank], 1)
                    if i == 3:
                        take_q(it, s)
                elif kind == "angle":
                    off, w = PIECES[i]
                    filled(dve, it, use)
                    if s > 0:
                        dve.wait_ge(cos_done, at(it, 8, 4 * s + i - 3))
                    t, n = turns[:, i, :w], whole[:, i, :w]
                    done = at(it, 24, 12 * s + 3 * i + 1), at(it, 24, 12 * s + 3 * i + 2)
                    nc.vector.tensor_scalar(t, X[:, bank, :w], 1.0 / (2.0 * math.pi), turn[:, 1:2], ALU.mult, ALU.add)\
                      .then_inc(bank_free[bank], 1)
                    taken(dve, it, use)
                    nc.vector.tensor_scalar(n, t, ROUND, ROUND, ALU.add, ALU.subtract).then_inc(angle_steps, 1)
                    dve.wait_ge(angle_steps, done[0])
                    nc.vector.tensor_tensor(t, t, n, ALU.subtract).then_inc(angle_steps, 1)
                    dve.wait_ge(angle_steps, done[1])
                    nc.vector.tensor_scalar(t, t, 0.5, -0.5, ALU.min, ALU.max).then_inc(angle_steps, 1)
                elif kind == "max":
                    if i < 4:
                        off, w = PIECES[i]
                        dve.wait_ge(k_hi_done, at(it, 8, 4 * s + i + 1))
                        nc.vector.tensor_tensor(K[s % 2][1][:, off:off + w], cosT[:, i, :w],
                                                f32(K[s % 2][0][:, off:off + w]), ALU.subtract).then_inc(k_lo_done, 1)
                    filled(dve, it, use)
                    w = min(PIECES[i % 4][1], N - PIECES[i % 4][0])
                    nc.vector.tensor_reduce(maxes[:, s % 2, i:i + 1], X[:, bank, :w], AX.X, ALU.max)\
                      .then_inc(bank_free[bank], 1)
                elif kind == "shift":
                    taken(dve, it, last_max_use(c) - 1)
                    taken(dve, it, last_max_use(c))
                    nc.vector.tensor_reduce(neg_max[:, s % 2, :], maxes[:, s % 2, :].rearrange("p (u k) -> p u k", k=4),
                                            AX.X, ALU.max, negate=True).then_inc(shift_steps, 1)
                    dve.wait_ge(shift_steps, at(it, 4, 2 * s + 1))
                    nc.vector.tensor_tensor(shift_diag[:, s % 2, :, :],
                                            ident[:, :].unsqueeze(1).to_broadcast([P, 2, P]),
                                            bc(neg_max[:, s % 2, :], P), ALU.mult).then_inc(shift_steps, 1)
                elif kind == "den":
                    filled(dve, it, use)
                    nc.vector.reciprocal(rden[:, :], X[:, bank, 0:S]).then_inc(bank_free[bank], 1)
                    taken(dve, it, use)
                elif kind == "norm":
                    dve.wait_ge(pv_done, step_of(it, c, 0))
                    nc.vector.tensor_tensor(outT[:, :], PV[:, (c - 1) % 2, 0:S], rden[:, :], ALU.mult)\
                      .then_inc(norm_done, 1)
                elif kind == "proj":
                    filled(dve, it, use)
                    rows = XS[:, bass.ds(at(it, 4, 2 * (c - 1)), 2), :]
                    nc.vector.tensor_tensor(rows, rows, X[:, bank, :2 * D].rearrange("p (j d) -> p j d", d=D), ALU.add)\
                      .then_inc(bank_free[bank], 1)

            def last_max_use(c):
                if c < 0:
                    return PREP_USES - 1
                return max(u for slot in plan(c, c > 0, True) for k, i, u in slot if k == "max")

            def body(it, c):
                for slot in the_plan(it, c):
                    for kind, i, use in slot:
                        item(it, c, kind, i, use)

            for use, (kind, i) in enumerate([("cT", i) for i in range(4)] + [("angle", i) for i in range(4)] +
                                            [("max", i) for i in range(8)]):
                item(None, -1, kind, i, use)
            item(None, -1, "shift", 0, None)
            stages(dve, body)
            for n, (kind, use) in enumerate((("den", first_use(STAGES)), ("norm", None), ("proj", first_use(STAGES) + 1))):
                item(None, STAGES, kind, 0, use)


def ffn_1(nc, base_w, base_b, shared_a, shared_b, routed_a, routed_b, router_w, router_b, XS, ident, out):
    E, RK = routed_a.shape[0], routed_a.shape[1]
    ER = E * RK
    T = B * S
    ROWS = E + ER

    with ExitStack() as es:
        def sb(name, shape, dt=F32):
            return es.enter_context(nc.sbuf_tensor("f_" + name, shape, dt))

        def sem(name):
            return es.enter_context(nc.semaphore("f_" + name))

        xn = sb("xn", [P, TILES, D])
        squares = sb("squares", [P, TILES, D])
        stats = sb("stats", [P, 2, TILES])
        xT = sb("xT", [P, T])
        small = sb("small", [ROWS, D])
        smallT = sb("smallT", [P, ROWS])
        base = sb("base", [P, D])
        sa = sb("sa", [RK, D])
        sbn = sb("sbn", [P, RK])
        sbT = sb("sbT", [RK, D])
        rb = sb("rb", [P, E, RK])
        rbT = sb("rbT", [ER, D])
        rows = sb("rows", [1, D + E])
        Wb = sb("Wb", [P, D])
        ones = sb("ones", [1, P])
        select = sb("select", [E, ER])
        gate = sb("gate", [P, TILES, E])
        top = sb("top", [P, 2, TILES])
        rank = sb("rank", [P, TILES, E])
        ahead = sb("ahead", [P, TILES, E])
        weights = sb("weights", [P, TILES, E])
        wT = sb("wT", [E, T])
        spread = sb("spread", [ER, T])
        hT = sb("hT", [ER, T])

        A = es.enter_context(nc.psum_tensor("f_a", [P, 4, 512], F32))
        C = es.enter_context(nc.psum_tensor("f_c", [P, 4, 512], F32))

        loaded, consts, dve_chain = sem("loaded"), sem("consts"), sem("dve_chain")
        var_ready, std_ready, xn_ready = sem("var_ready"), sem("std_ready"), sem("xn_ready")
        small_filled, small_done, wb_filled, wb_done = sem("small_filled"), sem("small_done"), sem("wb_filled"), sem("wb_done")
        xT_filled, xT_done = sem("xT_filled"), sem("xT_done")
        logits_filled, centred, exped = sem("logits_filled"), sem("centred"), sem("exped")
        h_filled, weighted, wT_filled, wT_done = sem("h_filled"), sem("weighted"), sem("wT_filled"), sem("wT_done")
        spread_filled, spread_done, h_done = sem("spread_filled"), sem("spread_done"), sem("h_done")
        y_filled, y_added, stored = sem("y_filled"), sem("y_added"), sem("stored")
        block = es.enter_context(nc.Block())

        @block.sync
        def _(sp):
            sp.dma_start(small[0:E, :], router_w).then_inc(loaded, 16)
            sp.dma_start(small[E:ROWS, :], routed_a.rearrange("e r d -> (e r) d")).then_inc(loaded, 16)
            sp.dma_start(base[:, :], base_w).then_inc(loaded, 16)
            sp.dma_start(sa[:, :], shared_a).then_inc(loaded, 16)
            sp.dma_start(sbn[:, :], shared_b).then_inc(loaded, 16)
            sp.dma_start(rb[:, :, :], routed_b.rearrange("e o r -> o e r")).then_inc(loaded, 16)
            sp.dma_start(rows[:, 0:D], base_b.rearrange("(a d) -> a d", a=1)).then_inc(loaded, 16)
            sp.dma_start(rows[:, D:D + E], router_b.rearrange("(a d) -> a d", a=1)).then_inc(loaded, 16)
            tokens = out.rearrange("b (j p) d -> p (b j) d", p=P)
            for g in range(4):
                sp.wait_ge(y_added, g + 1)
                sp.dma_start(tokens[:, 4 * g:4 * g + 4, :], XS[:, 4 * g:4 * g + 4, :]).then_inc(stored, 16)
            sp.wait_ge(stored, 64)

        @block.gpsimd
        def _(pool):
            nc.gpsimd.memset(ones[:, :], 1.0).then_inc(consts, 1)
            nc.gpsimd.memset(select[:, :], 1.0).then_inc(consts, 1)
            for e in range(E):
                nc.gpsimd.memset(rank[:, :, e:e + 1], float(e)).then_inc(consts, 1)
            pool.wait_ge(consts, 2 + E)
            nc.gpsimd.affine_select(out=select[:, :], in_=select[:, :], compare_op=ALU.is_ge, fill=0.0,
                                    base=0, pattern=[[1, ER]], channel_multiplier=-RK).then_inc(consts, 1)
            pool.wait_ge(consts, 3 + E)
            nc.gpsimd.affine_select(out=select[:, :], in_=select[:, :], compare_op=ALU.is_ge, fill=0.0,
                                    base=RK - 1, pattern=[[-1, ER]], channel_multiplier=RK).then_inc(consts, 1)

        @block.tensor
        def _(pe):
            pe.wait_ge(loaded, 128)
            pe.wait_ge(consts, 4 + E)
            nc.tensor.transpose(A[:, 0, 0:ROWS], small[:, :], ident[0:ROWS, 0:ROWS])
            nc.tensor.transpose(A[0:RK, 1, 0:D], sbn[:, :], ident[:, :])
            nc.tensor.transpose(A[0:ER, 1, D:2 * D], rb[:, :, :].rearrange("p e r -> p (e r)"), ident[:, :])\
              .then_inc(small_filled, 1)
            pe.wait_ge(small_done, 3)
            nc.tensor.matmul(A[:, 2, 0:D], base[:, :], ident[:, :], start=True, stop=False)
            nc.tensor.matmul(A[:, 2, 0:D], sa[:, :], sbT[:, :], start=False, stop=True).then_inc(wb_filled, 1)
            pe.wait_ge(xn_ready, 1)
            for g in range(4):
                for t in range(4):
                    last = nc.tensor.transpose(C[:, g, t * P:(t + 1) * P], xn[:, 4 * g + t, :], ident[:, :])
                last.then_inc(xT_filled, 1)
            for t in range(TILES):
                if t % 4 == 0:
                    pe.wait_ge(xT_done, t // 4 + 1)
                o = A[:, 3, t * E:(t + 1) * E]
                nc.tensor.matmul(o, xT[:, t * P:(t + 1) * P], smallT[:, 0:E], start=True, stop=False)
                last = nc.tensor.matmul(o, ones[:, :], rows[:, D:D + E], start=False, stop=True)
            last.then_inc(logits_filled, 1)
            for g in range(4):
                nc.tensor.matmul(C[0:ER, g, :], smallT[:, E:ROWS], xT[:, g * 512:(g + 1) * 512], start=True,
                                 stop=True).then_inc(h_filled, 1)
            pe.wait_ge(weighted, 1)
            for g in range(4):
                if g == 2:
                    pe.wait_ge(wb_done, 1)
                if g == 3:
                    pe.wait_ge(centred, 1)
                for t in range(4):
                    last = nc.tensor.transpose(A[0:E, g, t * P:(t + 1) * P], weights[:, 4 * g + t, :], ident[:, :])
                last.then_inc(wT_filled, 1)
            for g in range(4):
                pe.wait_ge(wT_done, g + 1)
                nc.tensor.matmul(A[0:ER, g, :], select[:, :], wT[:, g * 512:(g + 1) * 512], start=True, stop=True)\
                  .then_inc(spread_filled, 1)
            for g in range(4):
                pe.wait_ge(h_done, g + 1)
                for t in range(4):
                    tok = slice((4 * g + t) * P, (4 * g + t + 1) * P)
                    o = A[:, g, t * D:(t + 1) * D]
                    nc.tensor.matmul(o, xT[:, tok], Wb[:, :], start=True, stop=False)
                    nc.tensor.matmul(o, hT[:, tok], rbT[:, :], start=False, stop=False)
                    last = nc.tensor.matmul(o, ones[:, :], rows[:, 0:D], start=False, stop=True)
                last.then_inc(y_filled, 1)

        @block.scalar
        def _(act):
            act.wait_ge(var_ready, 1)
            nc.scalar.activation(stats[:, 1, :], stats[:, 1, :], ACT.Sqrt).then_inc(std_ready, 1)
            act.wait_ge(wb_filled, 1)
            nc.scalar.activation(Wb[:, :], A[:, 2, 0:D], ACT.Copy).then_inc(wb_done, 1)
            for g in range(0, 4, 2):
                act.wait_ge(xT_filled, g + 2)
                nc.scalar.activation(xT[:, g * 512:(g + 2) * 512], C[:, g:g + 2, :].rearrange("p a n -> p (a n)"),
                                     ACT.Copy).then_inc(xT_done, 2)
            act.wait_ge(centred, 1)
            nc.scalar.activation(gate[:, :, :], gate[:, :, :], ACT.Exp).then_inc(exped, 1)
            for g in range(4):
                act.wait_ge(spread_filled, g + 1)
                nc.scalar.activation(spread[:, g * 512:(g + 1) * 512], A[0:ER, g, :], ACT.Copy).then_inc(spread_done, 1)

        @block.vector
        def _(dve):
            chain = [0]

            def link(ins):
                chain[0] += 1
                ins.then_inc(dve_chain, 1)
                dve.wait_ge(dve_chain, chain[0])

            layer_norm(nc, link, XS[:, :, :], xn[:, :, :], squares[:, :, :], stats, var_ready,
                       lambda: dve.wait_ge(std_ready, 1)).then_inc(xn_ready, 1)
            dve.wait_ge(small_filled, 1)
            nc.vector.tensor_copy(smallT[:, :], A[:, 0, 0:ROWS]).then_inc(small_done, 1)
            nc.vector.tensor_copy(sbT[:, :], A[0:RK, 1, 0:D]).then_inc(small_done, 1)
            nc.vector.tensor_copy(rbT[:, :], A[0:ER, 1, D:2 * D]).then_inc(small_done, 1)
            dve.wait_ge(logits_filled, 1)
            L = A[:, 3, 0:TILES * E].rearrange("p (t e) -> p t e", e=E)
            link(nc.vector.tensor_reduce(top[:, 0, :], L, AX.X, ALU.max))
            nc.vector.tensor_tensor(gate[:, :, :], L, bc(top[:, 0, :], E), ALU.subtract).then_inc(centred, 1)
            dve.wait_ge(exped, 1)
            link(nc.vector.tensor_reduce(top[:, 1, :], gate[:, :, :], AX.X, ALU.add))
            link(nc.vector.reciprocal(top[:, 1, :], top[:, 1, :]))
            link(nc.vector.tensor_tensor(gate[:, :, :], gate[:, :, :], bc(top[:, 1, :], E), ALU.mult))
            dve.wait_ge(consts, 4 + E)
            for k in range(1, E):
                link(nc.vector.tensor_tensor(ahead[:, :, 0:E - k], gate[:, :, k:E], gate[:, :, 0:E - k], ALU.is_gt))
                link(nc.vector.tensor_tensor(rank[:, :, 0:E - k], rank[:, :, 0:E - k], ahead[:, :, 0:E - k], ALU.add))
                link(nc.vector.tensor_tensor(rank[:, :, k:E], rank[:, :, k:E], ahead[:, :, 0:E - k], ALU.subtract))
            link(nc.vector.scalar_tensor_tensor(out=weights[:, :, :], in0=rank[:, :, :], scalar=1.5, in1=gate[:, :, :],
                                                op0=ALU.is_lt, op1=ALU.mult))
            link(nc.vector.tensor_reduce(top[:, 0, :], weights[:, :, :], AX.X, ALU.add))
            link(nc.vector.tensor_scalar(top[:, 0, :], top[:, 0, :], 1e-6, None, ALU.add))
            link(nc.vector.reciprocal(top[:, 0, :], top[:, 0, :]))
            nc.vector.tensor_tensor(weights[:, :, :], weights[:, :, :], bc(top[:, 0, :], E), ALU.mult)\
              .then_inc(weighted, 1)
            for g in range(4):
                dve.wait_ge(wT_filled, g + 1)
                nc.vector.tensor_copy(wT[:, g * 512:(g + 1) * 512], A[0:E, g, :]).then_inc(wT_done, 1)
            for g in range(4):
                cols = slice(g * 512, (g + 1) * 512)
                dve.wait_ge(h_filled, g + 1)
                dve.wait_ge(spread_done, g + 1)
                nc.vector.tensor_tensor(hT[:, cols], C[0:ER, g, :], spread[:, cols], ALU.mult).then_inc(h_done, 1)
            for g in range(4):
                dve.wait_ge(y_filled, g + 1)
                rows_g = XS[:, 4 * g:4 * g + 4, :]
                nc.vector.tensor_tensor(rows_g, rows_g, A[:, g, :].rearrange("p (t d) -> p t d", d=D), ALU.add)\
                  .then_inc(y_added, 1)


def two_layers(nc, x, ctx_1024, L0_xattn_Wq, L0_xattn_Wk, L0_xattn_Wv, L0_xattn_Wo, L0_ffn_gate_weight, L0_ffn_W1,
               L0_ffn_b1, L0_ffn_W2, L0_ffn_b2, L0_ffn_Ws1, L0_ffn_bs1, L0_ffn_Ws2, L0_ffn_bs2, L1_xattn_Wq,
               L1_xattn_bq, L1_xattn_Wk, L1_xattn_bk, L1_xattn_Wv, L1_xattn_bv, L1_xattn_Wr, L1_xattn_br,
               L1_ffn_base_W, L1_ffn_base_b, L1_ffn_shared_A, L1_ffn_shared_B, L1_ffn_routed_A, L1_ffn_routed_B,
               L1_ffn_router_W, L1_ffn_router_b, out):
    with ExitStack() as es:
        XS = es.enter_context(nc.sbuf_tensor("tokens", [P, TILES, D], F32))
        ident = es.enter_context(nc.sbuf_tensor("ident", [P, P], F32))
        attention_0(nc, x, ctx_1024, L0_xattn_Wq, L0_xattn_Wk, L0_xattn_Wv, L0_xattn_Wo, XS, ident)
        moe_0(nc, L0_ffn_gate_weight, L0_ffn_W1, L0_ffn_b1, L0_ffn_W2, L0_ffn_b2, L0_ffn_Ws1, L0_ffn_bs1,
              L0_ffn_Ws2, L0_ffn_bs2, XS, ident)
        attention_1(nc, ctx_1024, L1_xattn_Wq, L1_xattn_bq, L1_xattn_Wk, L1_xattn_bk, L1_xattn_Wv, L1_xattn_bv,
                    L1_xattn_Wr, L1_xattn_br, XS, ident)
        ffn_1(nc, L1_ffn_base_W, L1_ffn_base_b, L1_ffn_shared_A, L1_ffn_shared_B, L1_ffn_routed_A, L1_ffn_routed_B,
              L1_ffn_router_W, L1_ffn_router_b, XS, ident, out)


_INS = ['x', 'ctx_1024', 'L0_xattn_Wq', 'L0_xattn_Wk', 'L0_xattn_Wv', 'L0_xattn_Wo', 'L0_ffn_gate_weight', 'L0_ffn_W1',
        'L0_ffn_b1', 'L0_ffn_W2', 'L0_ffn_b2', 'L0_ffn_Ws1', 'L0_ffn_bs1', 'L0_ffn_Ws2', 'L0_ffn_bs2', 'L1_xattn_Wq',
        'L1_xattn_bq', 'L1_xattn_Wk', 'L1_xattn_bk', 'L1_xattn_Wv', 'L1_xattn_bv', 'L1_xattn_Wr', 'L1_xattn_br',
        'L1_ffn_base_W', 'L1_ffn_base_b', 'L1_ffn_shared_A', 'L1_ffn_shared_B', 'L1_ffn_routed_A', 'L1_ffn_routed_B',
        'L1_ffn_router_W', 'L1_ffn_router_b']
_OUTS = [((B, S, D), 'float32')]


def kernel(**inputs):
    import numpy as _np
    import concourse.bacc as _bacc
    from concourse import mybir as _mybir
    from concourse.bass_utils import run_bass_kernel_spmd as _run

    nc = _bacc.Bacc("TRN2", target_bir_lowering=False, num_devices=1)
    arrays, args = {}, []
    for name in _INS:
        a = _np.ascontiguousarray(inputs[name])
        arrays[f"in_{name}_dram"] = a
        args.append(nc.dram_tensor(f"in_{name}_dram", a.shape, _mybir.dt.from_np(a.dtype), kind="ExternalInput").ap())
    for i, (shape, dtype) in enumerate(_OUTS):
        dt = _mybir.dt.from_np(_np.dtype(dtype))
        args.append(nc.dram_tensor(f"out_{i}_dram", shape, dt, kind="ExternalOutput").ap())
    two_layers(nc, *args)
    r = _run(nc, [arrays], core_ids=[0])
    return r.results[0]["out_0_dram"]
```

```python
import concourse.bass as bass
from concourse import mybir
from contextlib import ExitStack
import math

F32 = mybir.dt.float32
F32R = mybir.dt.float32r
BF16 = mybir.dt.bfloat16
U32 = mybir.dt.uint32
ACT = mybir.ActivationFunctionType
ALU = mybir.AluOpType
AX = mybir.AxisListType

P = 128
B, S, D = 8, 256, 128
N = 1601
H, HD = 16, 64
NC = -(-N // P)
LAST = N - (NC - 1) * P
TILES = B * S // P
MASKED = -1e30
EPS = 1e-5


def at(it, per, first):
    return first if it is None else it * per + first


def f32(ap):
    return ap.bitcast(F32)


def bc(ap, n):
    return ap.unsqueeze(2).to_broadcast([ap.shape[0], ap.shape[1], n])


def layer_norm(nc, link, src, out, squares, stats, var_ready, wait_std):
    mean, var = stats[:, 0, :], stats[:, 1, :]
    link(nc.vector.tensor_reduce(mean, src, AX.X, ALU.add))
    link(nc.vector.tensor_scalar(mean, mean, 1.0 / D, None, ALU.mult))
    link(nc.vector.tensor_tensor(out, src, bc(mean, D), ALU.subtract))
    link(nc.vector.tensor_tensor(squares, out, out, ALU.mult))
    link(nc.vector.tensor_reduce(var, squares, AX.X, ALU.add))
    nc.vector.tensor_scalar(var, var, 1.0 / D, EPS, ALU.mult, ALU.add).then_inc(var_ready, 1)
    wait_std()
    link(nc.vector.reciprocal(var, var))
    return nc.vector.tensor_tensor(out, out, bc(var, D), ALU.mult)


def attention_0(nc, x, ctx_in, wq, wk, wv, wo, XS, ident):
    G8 = H // 2
    STEPS = 2 * NC
    SLOTS = 4 * STEPS
    STAGES = 2 * B
    PIECES = [(0, 402), (402, 400), (802, 400), (1202, 400)]
    UNITS = G8 * 2

    BANKS = 4
    TAIL = 3
    V_AFTER = [2, 4, 6, 8, 10, 12, 14, 26, 38]
    LATE_V = [95, 97, 100, 102]
    MAX_END = 93
    SHIFTS = [83, 93]
    DIAG = [84, 88]
    SPREAD = [92, 93, 98, 99]
    RECIP = range(8, 24, 2)
    NORM_STEP = 6
    PROJ = 34

    def prep_slots(group):
        early = []
        if group == 0:
            early += [("cT", i) for i in range(3)] + [("cxT", 3)] + [("mask", i) for i in range(4)]
        early += [("q", i) for i in range(4)]
        vs = [("v", c) for c in range(NC)]
        for u in range(UNITS * 4):
            early.append(("max", u))
            if u in V_AFTER:
                early.append(vs.pop(0))
        slots = [[] for _ in range(SLOTS)]
        for n, item in enumerate(early):
            slots[n * MAX_END // len(early)].append(item)
        for i in range(2):
            slots[SHIFTS[i]].append(("shift", i))
        for i in range(2):
            slots[DIAG[i]].append(("diag", i))
        for i in range(4):
            slots[SPREAD[i]].append(("spread", i))
        assert len(vs) == len(LATE_V)
        for n, item in zip(LATE_V, vs):
            slots[n].append(item)
        return slots

    PREP = [sum(map(len, prep_slots(g))) - 4 for g in range(2)]

    def first_use(c):
        n = PREP[0]
        for s in range(c):
            n += (TAIL if s else 0) + (PREP[(s + 1) % 2] if s + 1 < STAGES else 0)
        return n

    PER_TURN = first_use(5) - first_use(1)
    assert PER_TURN % BANKS == 0

    def numbered(slots, use):
        out = []
        for slot in slots:
            row = []
            for kind, i in slot:
                takes = kind not in ("recip", "shift", "diag")
                row.append((kind, i, use if takes else None))
                use += takes
            out.append(row)
        return out

    def plan(c, tail, prep):
        slots = [[] for _ in range(SLOTS)]
        if tail:
            slots[3].append(("den", 0))
            slots[7].append(("den", 1))
            for i in range(8):
                slots[RECIP[i]].append(("recip", i))
            slots[PROJ].append(("proj", 0))
        if prep:
            slots = [a + b for a, b in zip(slots, prep_slots((c + 1) % 2))]
        return numbered(slots, first_use(c))

    with ExitStack() as es:
        def sb(name, shape, dt=F32):
            return es.enter_context(nc.sbuf_tensor("a_" + name, shape, dt))

        def sem(name):
            return es.enter_context(nc.semaphore("a_" + name))

        c_nat = sb("c_nat", [P, NC, D])
        cT = [[sb(f"cT_{part}{i}", [P, NC * P], F32R) for part in ("hi", "lo")] for i in range(2)]
        V = sb("V", [P, 2, NC, G8 * HD])
        Q = [[sb(f"Q_{part}{i}", [P, G8 * S], F32R) for part in ("hi", "lo")] for i in range(2)]
        shift_diag = sb("shift_diag", [P, UNITS // 2, P], F32R)
        shift = sb("shift", [P, G8 * S])
        probs = sb("probs", [P, 4, 4 * S])
        den = sb("den", [P, G8 * S])
        G = [sb("G_hi", [P, H, D], F32R), sb("G_lo", [P, H, D], F32R)]
        Wv = [sb("Wv_hi", [P, H * HD], F32R), sb("Wv_lo", [P, H * HD], F32R)]
        Wo = sb("Wo", [P, H // 2, D])
        mask_row = sb("mask_row", [P, NC * P], BF16)
        c_flag = mask_row
        mask_col = sb("mask_col", [P, 2, NC])
        acc = sb("acc", [P, 2, 2, D])
        xn_b = sb("xn_b", [P, 2, D])
        xnT = [sb("xnT_hi", [P, S], F32R), sb("xnT_lo", [P, S], F32R)]
        outT = sb("outT", [P, 4 * S])
        rden = sb("rden", [P, 4 * S])
        maxes = sb("maxes", [P, 2, UNITS * 4])
        neg_max = sb("neg_max", [P, 2, UNITS])
        stats = sb("stats", [P, 2, TILES])
        c_largest = sb("c_largest", [P, NC])
        ones = sb("ones", [P, HD])

        ones_b = sb("ones_b", [P, P], BF16)
        ones_r = sb("ones_r", [P, P], F32R)
        raw = [V[:, 1, :, :].rearrange("p c n -> p (c n)")[:, i * 1024:(i + 1) * 1024] for i in range(6)]
        wq_raw, wk_raw, wv_raw, wk_heads, wqT, wkT = raw
        squares = probs[:, 0:2, :].rearrange("p a (t d) -> p (a t) d", d=D)

        Sc = es.enter_context(nc.psum_tensor("a_scores", [P, 2, 2 * S], F32))
        PV = es.enter_context(nc.psum_tensor("a_pv", [P, 4 * S], F32))
        X = es.enter_context(nc.psum_tensor("a_work", [P, BANKS, 512], F32))
        X_setup = X[:, :, :].rearrange("p (a b) n -> p a (b n)", a=2)

        x_loaded, w_loaded, c_loaded = sem("x_loaded"), sem("w_loaded"), sem("c_loaded")
        res_loaded = sem("res_loaded")
        consts, ones_ready = sem("consts"), sem("ones_ready")
        dve_chain = sem("dve_chain")
        var_ready, std_ready = sem("var_ready"), sem("std_ready")
        wk_ready = sem("wk_ready")
        wT_filled, wT_copied = sem("wT_filled"), sem("wT_copied")
        G_filled, G_hi_done, G_ready = sem("G_filled"), sem("G_hi_done"), sem("G_ready")
        xn_all, wv_ready = sem("xn_all"), sem("wv_ready")
        bank_full = [sem(f"bank{i}_full") for i in range(BANKS)]
        bank_free = [sem(f"bank{i}_free") for i in range(BANKS)]
        hi_done = sem("hi_done")
        flag_done = sem("flag_done")
        col_done = sem("col_done")
        xn_ready = sem("xn_ready")
        shift_steps = sem("shift_steps")
        diag_done = sem("diag_done")
        scores_done, shifted = sem("scores_done"), sem("shifted")
        probs_done, pv_done = sem("probs_done"), sem("pv_done")
        pv_free = sem("pv_free")
        den_added = sem("den_added")
        recip_done, norm_done = sem("recip_done"), sem("norm_done")
        block = es.enter_context(nc.Block())

        def filled(eng, it, use):
            eng.wait_ge(bank_full[use % BANKS], at(it, PER_TURN // BANKS, use // BANKS + 1))

        def taken(eng, it, use):
            eng.wait_ge(bank_free[use % BANKS], at(it, PER_TURN // BANKS, use // BANKS + 1))

        def stages(eng, body):
            body(None, 0)
            with eng.Fori(0, 3) as it:
                for c in range(1, 5):
                    body(it, c)
            for c in range(13, STAGES):
                body(None, c)

        def steps_of(it, c, first):
            return at(it, 4 * STEPS, c * STEPS + first)

        def batch_of(it, c):
            return at(it, 2, c // 2)

        def shifts_of(it, c, j, pair):
            return at(it, 8 * STEPS, 2 * (c * STEPS + j) + pair)

        def flags(it, c):
            return c > 0 or it is not None, it is not None or c + 1 < STAGES

        def use_of(slots, kind, index):
            return [use for slot in slots for k, i, use in slot if (k, i) == (kind, index)][0]

        def the_plan(it, c):
            return plan(c, *flags(it, c))

        def prologue_items():
            return [item for slot in numbered(prep_slots(0), 0) for item in slot]

        def prep_use(it, c, kind, index):
            return use_of([prologue_items()] if c < 0 else the_plan(it, c), kind, index)

        def buffer(c, j):
            return (c * STEPS + j) % 4

        @block.sync
        def _(sp):
            sp.dma_start(XS[:, :, :], x.rearrange("b (j p) d -> p (b j) d", p=P)).then_inc(x_loaded, 16)
            sp.dma_start(wq_raw, wq).then_inc(w_loaded, 16)
            sp.dma_start(wk_raw, wk).then_inc(w_loaded, 16)
            sp.dma_start(wv_raw, wv).then_inc(w_loaded, 16)
            sp.dma_start(Wo[:, :, :], wo.rearrange("(g p) n -> p g n", p=P)).then_inc(w_loaded, 16)
            sp.wait_ge(consts, 2)

            def load_context(b):
                sp.dma_start(c_nat[:, 0:NC - 1, :],
                             ctx_in[b, 0:(NC - 1) * P, :].rearrange("(c p) d -> p c d", p=P)).then_inc(c_loaded, 16)
                sp.dma_start(c_nat[0:LAST, NC - 1, :], ctx_in[b, (NC - 1) * P:N, :]).then_inc(c_loaded, 16)

            def load_residual(b, parity):
                sp.dma_start(acc[:, parity, :, :],
                             x[b, :, :].rearrange("(j p) d -> p j d", p=P)).then_inc(res_loaded, 16)

            load_context(0)
            load_residual(0, 0)

            def body(it, c):
                if c % 2 == 0 and (it is not None or c < STAGES - 2):
                    transposed, scanned = at(it, 26, c // 2 * 13 + 4), at(it, 4, c // 2 * 2 + 1)
                    sp.wait_ge(hi_done, transposed)
                    sp.nop(nofuse=True)
                    sp.wait_ge(col_done, scanned)
                    load_context(at(it, 2, c // 2 + 1))
                    if c > 0:
                        taken(sp, it, use_of(the_plan(it, c), "proj", 0))
                    load_residual(at(it, 2, c // 2 + 1), (c // 2 + 1) % 2)

            stages(sp, body)

        @block.gpsimd
        def _(pool):
            nc.gpsimd.memset(ident[:, :], 0.0).then_inc(consts, 1)
            nc.gpsimd.memset(c_nat[:, NC - 1, :], 0.0).then_inc(consts, 1)
            nc.gpsimd.memset(ones[:, :], 1.0).then_inc(consts, 1)
            nc.gpsimd.memset(ones_b[:, :], 1.0).then_inc(consts, 1)
            pool.wait_ge(consts, 4)
            nc.gpsimd.affine_select(out=ident[:, :], in_=ident[:, :], compare_op=ALU.not_equal, fill=1.0,
                                    base=0, pattern=[[-1, P]], channel_multiplier=1).then_inc(consts, 1)

            def normalise(it, c):
                pool.wait_ge(recip_done, at(it, 32, 8 * c))
                pool.wait_ge(pv_free, at(it, 8, 2 * c))
                nc.gpsimd.tensor_tensor(outT[:, :], outT[:, :], rden[:, :], ALU.mult).then_inc(norm_done, 1)

            def body(it, c):
                for j in range(2, STEPS):
                    half = den[:, (j % 2) * 4 * S:(j % 2 + 1) * 4 * S]
                    if j < 4:
                        so_far = probs[:, buffer(c, j - 2), :]
                        if c > 0:
                            filled(pool, it, use_of(the_plan(it, c), "den", j - 2))
                    else:
                        so_far = half
                        pool.wait_ge(den_added, at(it, 4 * (STEPS - 2), c * (STEPS - 2) + j - 3))
                    pool.wait_ge(probs_done, steps_of(it, c, j + 1))
                    nc.gpsimd.tensor_tensor(half, so_far, probs[:, buffer(c, j), :], ALU.add).then_inc(den_added, 1)
                    if c > 0 and j == NORM_STEP:
                        normalise(it, c)

            stages(pool, body)
            normalise(None, STAGES)

        @block.tensor
        def _(pe):
            pe.wait_ge(consts, 5)
            pe.wait_ge(w_loaded, 64)
            for g in range(H // 2):
                nc.tensor.transpose(X_setup[:, 0, g * P:(g + 1) * P], wq_raw[:, g * P:(g + 1) * P], ident[:, :])
            pe.wait_ge(wk_ready, 1)
            for g in range(H // 2):
                last = nc.tensor.transpose(PV[:, g * P:(g + 1) * P], wk_heads[:, g * P:(g + 1) * P], ident[:, :])
            last.then_inc(wT_filled, 1)
            pe.wait_ge(wT_copied, 2)
            for g in range(H // 2):
                for odd in range(2):
                    rows = slice(HD * odd, HD * odd + HD)
                    last = nc.tensor.matmul(X_setup[:, odd, g * P:(g + 1) * P], wqT[rows, g * P:(g + 1) * P],
                                            wkT[rows, g * P:(g + 1) * P], start=True, stop=True)
            last.then_inc(G_filled, 1)
            pe.wait_ge(G_ready, 2)
            pe.wait_ge(ones_ready, 1)
            pe.wait_ge(wv_ready, 1)

            def split_product(out, a, b, cols_a, cols_b):
                nc.tensor.matmul(out, a[0][:, cols_a], b[0][:, cols_b], start=True, stop=False)
                nc.tensor.matmul(out, a[0][:, cols_a], b[1][:, cols_b], start=False, stop=False)
                return nc.tensor.matmul(out, a[1][:, cols_a], b[0][:, cols_b], start=False, stop=True)

            def item(it, c, kind, i, use):
                bank, s = use % BANKS, c + 1
                if use >= BANKS:
                    taken(pe, it, use - BANKS)
                out = X[:, bank, :]
                if kind in ("cT", "cxT"):
                    pe.wait_ge(c_loaded, at(it, 64, 32 * (s // 2 + 1)))
                    for ch in range(4 * i, min(4 * i + 4, NC)):
                        last = nc.tensor.transpose(out[:, ch % 4 * P:(ch % 4 + 1) * P], c_nat[:, ch, :], ident[:, :])
                    if kind == "cxT":
                        pe.wait_ge(xn_ready, at(it, 2, s // 2 + 1))
                        for j in range(2):
                            last = nc.tensor.transpose(out[:, (j + 1) * P:(j + 2) * P], xn_b[:, j, :], ident[:, :])
                elif kind == "mask":
                    pe.wait_ge(flag_done, at(it, 8, s // 2 * 4 + i + 1))
                    off, w = PIECES[i]
                    last = nc.tensor.matmul(out[:, :w], ones_b[:, :], c_flag[:, off:off + w], start=True, stop=True)
                elif kind == "q":
                    for k in range(2):
                        h = s % 2 * G8 + 2 * i + k
                        last = split_product(out[:, k * S:(k + 1) * S], [g[:, h, :] for g in G], xnT,
                                             slice(0, D), slice(0, S))
                elif kind == "v":
                    last = split_product(out, cT[s // 2 % 2], Wv, slice(i * P, (i + 1) * P),
                                         slice(s % 2 * G8 * HD, (s % 2 + 1) * G8 * HD))
                elif kind == "max":
                    off, w = PIECES[i % 4]
                    last = nc.tensor.matmul(out[:, :w], Q[s % 2][0][:, i // 4 * P:(i // 4 + 1) * P],
                                            cT[s // 2 % 2][0][:, off:off + w], start=True, stop=True)
                elif kind == "spread":
                    if i < 2:
                        pe.wait_ge(diag_done, at(it, 32, 8 * s + 4 * (i + 1)))
                    else:
                        pe.wait_ge(shift_steps, at(it, 20, 5 * s + 5))
                    last = nc.tensor.matmul(out, ones_r[:, :], shift_diag[:, i % 2 * 4:i % 2 * 4 + 4, :], start=True, stop=True)
                elif kind == "den":
                    pe.wait_ge(den_added, at(it, 4 * (STEPS - 2), c * (STEPS - 2) - 1 + i))
                    for k in range(2):
                        for odd in range(2):
                            h = 4 * i + 2 * k + odd
                            last = nc.tensor.matmul(out[HD * odd:HD * odd + HD, k * S:(k + 1) * S], ones[:, :],
                                                    den[:, h * S:(h + 1) * S], start=True, stop=True)
                elif kind == "proj":
                    pe.wait_ge(norm_done, at(it, 4, c))
                    for j in range(2):
                        for g in range(4):
                            last = nc.tensor.matmul(out[:, j * D:(j + 1) * D],
                                                    outT[:, g * S + j * P:g * S + (j + 1) * P],
                                                    Wo[:, (c - 1) % 2 * 4 + g, :], start=(g == 0), stop=(g == 3))
                last.then_inc(bank_full[bank], 1)

            def qk(it, c, j, pair):
                if c > 0 or j > 0:
                    pe.wait_ge(shifted, shifts_of(it, c, j - 1, pair + 1))
                first = (j % 2 * 4 + pair * 2)
                split_product(Sc[:, pair, :], cT[c // 2 % 2], Q[c % 2],
                              slice(j // 2 * P, (j // 2 + 1) * P), slice(first * S, (first + 2) * S))\
                    .then_inc(scores_done, 1)

            def pv(it, c, j, pair):
                if pair == 0:
                    pe.wait_ge(probs_done, steps_of(it, c, j + 1))
                    if j < 2 and c > 0:
                        pe.wait_ge(pv_free, at(it, 8, 2 * c - 1 + j))
                    if j == 2 * (NC - BANKS):
                        for use in range(first_use(c) - BANKS, first_use(c)):
                            taken(pe, it, use)
                for odd in range(2):
                    h = j % 2 * 4 + pair * 2 + odd
                    cols = (j % 2 * 2 + pair) * S
                    last = nc.tensor.matmul(PV[HD * odd:HD * odd + HD, cols:cols + S],
                                            V[:, c % 2, j // 2, h * HD:(h + 1) * HD],
                                            probs[:, buffer(c, j), (pair * 2 + odd) * S:(pair * 2 + odd + 1) * S],
                                            start=(j < 2 and pair == 0), stop=(j >= STEPS - 2), skip_group_check=True)
                if pair == 1:
                    last.then_inc(pv_done, 1)

            def body(it, c):
                tail, prep = flags(it, c)
                slots = the_plan(it, c)
                for j in range(STEPS):
                    for part in range(4):
                        if part == 1:
                            pv(it, c, j, 0)
                            pv(it, c, j, 1)
                        elif part > 1 and j + 2 < STEPS:
                            qk(it, c, j + 2, part - 2)
                        elif part > 1 and prep:
                            qk(it, c + 1, j + 2 - STEPS, part - 2)
                        for kind, i, use in slots[4 * j + part]:
                            if use is not None:
                                item(it, c, kind, i, use)

            for kind, i, use in prologue_items():
                if use is not None:
                    item(None, -1, kind, i, use)
            for j in range(2):
                for pair in range(2):
                    qk(None, 0, j, pair)
            stages(pe, body)
            for n, kind in enumerate(("den", "den", "proj")):
                item(None, STAGES, kind, n % 2, first_use(STAGES) + n)

        @block.scalar
        def _(act):
            act.wait_ge(var_ready, 1)
            nc.scalar.activation(stats[:, 1, :], stats[:, 1, :], ACT.Sqrt).then_inc(std_ready, 1)
            act.wait_ge(wT_filled, 1)
            nc.scalar.activation(wqT, X_setup[:, 0, :], ACT.Copy).then_inc(wT_copied, 1)
            act.wait_ge(G_filled, 1)
            for odd in range(2):
                heads = G[0].rearrange("p (g two) d -> p two g d", two=2)[:, odd, :, :]
                nc.scalar.activation(heads, X_setup[:, odd, :].rearrange("p (g d) -> p g d", d=D), ACT.Copy,
                                     scale=HD ** -0.5).then_inc(G_hi_done, 1)

            def item(it, c, kind, i, use):
                bank, s = None if use is None else use % BANKS, c + 1
                if kind == "diag":
                    act.wait_ge(shift_steps, at(it, 20, 5 * s + 2))
                    for u in range(4 * i, 4 * i + 4):
                        nc.scalar.activation(shift_diag[:, u, :], ident[:, :], ACT.Copy,
                                             scale=neg_max[:, s % 2, u:u + 1]).then_inc(diag_done, 1)
                if kind not in ("cT", "cxT", "q", "v", "spread", "den"):
                    return
                if kind == "den" and (c > 1 or it is not None):
                    act.wait_ge(norm_done, at(it, 4, c - 1))
                filled(act, it, use)
                if kind in ("cT", "cxT"):
                    w = min(4, NC - 4 * i) * P
                    nc.scalar.activation(cT[s // 2 % 2][0][:, i * 512:i * 512 + w], X[:, bank, :w], ACT.Copy)\
                      .then_inc(hi_done, 1)
                    if kind == "cxT":
                        nc.scalar.activation(xnT[0][:, :], X[:, bank, w:w + S], ACT.Copy).then_inc(hi_done, 1)
                elif kind == "q":
                    nc.scalar.activation(Q[s % 2][0][:, i * 512:(i + 1) * 512], X[:, bank, :], ACT.Copy)\
                      .then_inc(hi_done, 1)
                elif kind == "v":
                    nc.scalar.activation(V[:, s % 2, i, :], X[:, bank, :], ACT.Copy).then_inc(bank_free[bank], 1)
                elif kind == "spread":
                    if c >= 0:
                        act.wait_ge(shifted, shifts_of(it, c, STEPS - 2 + i // 2, i % 2 + 1))
                    nc.scalar.activation(shift[:, i * 512:(i + 1) * 512], X[:, bank, :], ACT.Copy)\
                      .then_inc(bank_free[bank], 1)
                elif kind == "den":
                    nc.scalar.activation(rden[:, i * 512:(i + 1) * 512], X[:, bank, :], ACT.Copy)\
                      .then_inc(bank_free[bank], 1)

            def exp(it, c, j):
                act.wait_ge(shifted, shifts_of(it, c, j, 2))
                if j == 0:
                    act.wait_ge(col_done, at(it, 4, 2 * (c // 2) + 2))
                nc.scalar.activation(probs[:, buffer(c, j), :], probs[:, buffer(c, j), :], ACT.Exp,
                                     bias=mask_col[:, c // 2 % 2, j // 2:j // 2 + 1]).then_inc(probs_done, 1)

            def copy_outT(it, c, bank):
                act.wait_ge(pv_done, steps_of(it, c, bank - 1))
                nc.scalar.activation(outT[:, bank * 512:(bank + 1) * 512], PV[:, bank * 512:(bank + 1) * 512], ACT.Copy)\
                  .then_inc(pv_free, 1)

            def body(it, c):
                tail, prep = flags(it, c)
                slots = the_plan(it, c)
                for j in range(STEPS):
                    if tail and j == 0:
                        copy_outT(it, c, 0)
                        copy_outT(it, c, 1)
                    if j + 1 < STEPS:
                        exp(it, c, j + 1)
                    elif prep:
                        exp(it, c + 1, 0)
                    for slot in slots[4 * j:4 * j + 4]:
                        for kind, i, use in slot:
                            item(it, c, kind, i, use)

            for kind, i, use in prologue_items():
                item(None, -1, kind, i, use)
            exp(None, 0, 0)
            stages(act, body)
            copy_outT(None, STAGES, 0)
            copy_outT(None, STAGES, 1)
            for i in range(2):
                item(None, STAGES, "den", i, first_use(STAGES) + i)

        @block.vector
        def _(dve):
            chain = [0]

            def link(ins):
                chain[0] += 1
                ins.then_inc(dve_chain, 1)
                dve.wait_ge(dve_chain, chain[0])

            dve.wait_ge(x_loaded, 16)
            layer_norm(nc, link, XS[:, :, :], XS[:, :, :], squares, stats, var_ready,
                       lambda: dve.wait_ge(std_ready, 1)).then_inc(xn_all, 1)
            dve.wait_ge(w_loaded, 64)
            nc.vector.tensor_copy(wk_heads.rearrange("p (h e) -> p h e", h=H),
                                  wk_raw.rearrange("p (e h) -> p h e", h=H)).then_inc(wk_ready, 1)
            wv_heads = wv_raw.rearrange("p (e h) -> p h e", h=H)
            link(nc.vector.tensor_copy(Wv[0].rearrange("p (h e) -> p h e", h=H), wv_heads))
            nc.vector.tensor_tensor(Wv[1].rearrange("p (h e) -> p h e", h=H), wv_heads,
                                    f32(Wv[0][:, :]).rearrange("p (h e) -> p h e", h=H), ALU.subtract)\
              .then_inc(wv_ready, 1)
            dve.wait_ge(consts, 5)
            nc.vector.tensor_copy(ones_r[:, :], ones_b[:, :]).then_inc(ones_ready, 1)
            dve.wait_ge(wT_filled, 1)
            nc.vector.tensor_copy(wkT, PV[:, :]).then_inc(wT_copied, 1)
            for odd in range(2):
                dve.wait_ge(G_hi_done, odd + 1)
                hi, lo = [g.rearrange("p (g two) d -> p two g d", two=2)[:, odd, :, :] for g in
                          (f32(G[0][:, :, :]), G[1][:, :, :])]
                nc.vector.scalar_tensor_tensor(out=lo, in0=X_setup[:, odd, :].rearrange("p (g d) -> p g d", d=D),
                                               scalar=HD ** -0.5, in1=hi, op0=ALU.mult, op1=ALU.subtract)\
                  .then_inc(G_ready, 1)
            dve.wait_ge(xn_all, 1)

            def low_part(it, out, hi, psum, done):
                dve.wait_ge(hi_done, at(it, 26, done))
                return nc.vector.tensor_tensor(out, psum, f32(hi), ALU.subtract)

            def item(it, c, kind, i, use):
                s = c + 1
                b, pb = s // 2, s // 2 % 2
                bank = None if use is None else use % BANKS
                if kind in ("cT", "cxT"):
                    if i == 0:
                        filled(dve, it, use)
                        nc.vector.tensor_reduce(c_largest[:, :], c_nat[:, :, :], AX.X, ALU.max,
                                                apply_absolute_value=True).then_inc(col_done, 1)
                        nc.vector.tensor_copy(xn_b[:, :, :], XS[:, bass.ds(at(it, 4, 2 * b), 2), :])\
                          .then_inc(xn_ready, 1)
                        dve.wait_ge(col_done, at(it, 4, 2 * b + 1))
                        nc.vector.tensor_scalar(mask_col[:, pb, :], c_largest[:, :], 0.0, MASKED,
                                                ALU.is_equal, ALU.mult).then_inc(col_done, 1)
                    w = min(4, NC - 4 * i) * P
                    cols = slice(i * 512, i * 512 + w)
                    last = low_part(it, cT[pb][1][:, cols], cT[pb][0][:, cols],
                                    X[:, bank, :w], 13 * b + i + (2 if kind == "cxT" else 1))
                    if kind == "cxT":
                        last = low_part(it, xnT[1][:, :], xnT[0][:, :], X[:, bank, w:w + S], 13 * b + 5)
                    last.then_inc(bank_free[bank], 1)
                    nc.vector.tensor_scalar(c_flag[:, cols], f32(cT[pb][0][:, cols]), 0.0, None, ALU.not_equal)\
                      .then_inc(flag_done, 1)
                elif kind == "mask":
                    off, w = PIECES[i]
                    filled(dve, it, use)
                    nc.vector.tensor_scalar(mask_row[:, off:off + w], X[:, bank, :w], 0.0, MASKED,
                                            ALU.is_equal, ALU.mult).then_inc(bank_free[bank], 1)
                elif kind == "q":
                    cols = slice(i * 512, (i + 1) * 512)
                    low_part(it, Q[s % 2][1][:, cols], Q[s % 2][0][:, cols], X[:, bank, :],
                             13 * b + (9 if s % 2 else 5) + i + 1).then_inc(bank_free[bank], 1)
                elif kind == "max":
                    off, w = PIECES[i % 4]
                    filled(dve, it, use)
                    dve.nop(nofuse=True)
                    nc.vector.tensor_tensor_reduce(out=X[:, bank, :w], in0=X[:, bank, :w],
                                                   in1=mask_row[:, off:off + w], scale=1.0, scalar=-3e38,
                                                   op0=ALU.add, op1=ALU.max, accum_out=maxes[:, s % 2, i:i + 1])\
                      .then_inc(bank_free[bank], 1)
                elif kind == "shift":
                    half = UNITS // 2
                    units = slice(i * half, (i + 1) * half)
                    uses = [prep_use(it, c, "max", m) for m in range(4 * half * i, 4 * half * (i + 1))]
                    for use in [max(u for u in uses if u % BANKS == k) for k in range(BANKS)]:
                        taken(dve, it, use)
                    nc.vector.tensor_reduce(neg_max[:, s % 2, units],
                                            maxes[:, s % 2, :].rearrange("p (u k) -> p u k", k=4)[:, units, :],
                                            AX.X, ALU.max, negate=True).then_inc(shift_steps, 1)
                    dve.wait_ge(shift_steps, at(it, 20, 5 * s + 2 * i + 1))
                    nc.vector.tensor_scalar(neg_max[:, s % 2, units], neg_max[:, s % 2, units], 1e20, None, ALU.min)\
                      .then_inc(shift_steps, 1)
                    if i == 1:
                        dve.wait_ge(shift_steps, at(it, 20, 5 * s + 4))
                        for quarter in range(2):
                            filled(dve, it, prep_use(it, c, "spread", quarter))
                        nc.vector.tensor_tensor(shift_diag[:, :, :],
                                                ident[:, :].unsqueeze(1).to_broadcast([P, half, P]),
                                                bc(neg_max[:, s % 2, units], P), ALU.mult).then_inc(shift_steps, 1)
                elif kind == "recip":
                    if i % 4 == 0:
                        taken(dve, it, use_of(the_plan(it, c), "den", i // 4))
                    part = rden[:, i * P:(i + 1) * P]
                    nc.vector.reciprocal(part, part).then_inc(recip_done, 1)
                elif kind == "proj":
                    filled(dve, it, use)
                    pb = (c - 1) // 2 % 2
                    psum = X[:, bank, :2 * D].rearrange("p (j d) -> p j d", d=D)
                    if (c - 1) % 2 == 0:
                        dve.wait_ge(res_loaded, at(it, 32, 16 * ((c - 1) // 2 + 1)))
                        out = acc[:, pb, :, :]
                    else:
                        taken(dve, it, use_of(the_plan(it, c - 1), "proj", 0))
                        out = XS[:, bass.ds(at(it, 4, 2 * ((c - 1) // 2)), 2), :]
                    nc.vector.tensor_tensor(out, acc[:, pb, :, :], psum, ALU.add).then_inc(bank_free[bank], 1)

            def subtract(it, c, j, pair):
                dve.wait_ge(scores_done, shifts_of(it, c, j, pair + 1))
                if pair == 0:
                    if j < 2:
                        for quarter in (2 * j, 2 * j + 1):
                            taken(dve, it, prep_use(it, c - 1, "spread", quarter))
                    if c > 0 or j > 3:
                        dve.wait_ge(pv_done, steps_of(it, c, j - 3))
                        added = 1 if j == 4 else 2 if j == 5 else j - 5 if j > 5 else j - 3
                        dve.wait_ge(den_added, at(it, 4 * (STEPS - 2), c * (STEPS - 2) + added))
                first = (j % 2 * 4 + pair * 2) * S
                nc.vector.tensor_tensor(probs[:, buffer(c, j), pair * 2 * S:(pair + 1) * 2 * S],
                                        Sc[:, pair, :],
                                        shift[:, first:first + 2 * S], ALU.add).then_inc(shifted, 1)

            def body(it, c):
                tail, prep = flags(it, c)
                slots = the_plan(it, c)
                for n in range(SLOTS):
                    j, part = n // 4, n % 4
                    if part >= 2:
                        if j + 2 < STEPS:
                            subtract(it, c, j + 2, part - 2)
                        elif prep:
                            subtract(it, c + 1, j + 2 - STEPS, part - 2)
                    for kind, i, use in slots[n]:
                        item(it, c, kind, i, use)

            for kind, i, use in prologue_items():
                item(None, -1, kind, i, use)
            for j in range(2):
                for pair in range(2):
                    subtract(None, 0, j, pair)
            stages(dve, body)
            last = first_use(STAGES)
            taken(dve, None, last)
            taken(dve, None, last + 1)
            for i in range(8):
                part = rden[:, i * P:(i + 1) * P]
                nc.vector.reciprocal(part, part).then_inc(recip_done, 1)
            item(None, STAGES, "proj", 0, last + 2)


def moe_0(nc, gate_w, w1, b1, w2, b2, ws1, bs1, ws2, bs2, XS, ident):
    E, F = w1.shape[0], w1.shape[2]
    T = B * S
    TOPK = T * 2
    FC = F // P
    TG = T // 512
    STEPS = FC * TG
    LAG = 3
    ROUNDS = 15
    ROWS = FC * (E + 1) + (E + 1) + E
    B2, GW = FC * (E + 1), FC * (E + 1) + E + 1

    with ExitStack() as es:
        def sb(name, shape, dt=F32):
            return es.enter_context(nc.sbuf_tensor("m_" + name, shape, dt))

        def sem(name):
            return es.enter_context(nc.semaphore("m_" + name))

        xn = sb("xn", [P, TILES, D])
        squares = sb("squares", [P, TILES, D])
        stats = sb("stats", [P, 2, TILES])
        xT = [sb("xT_hi", [P, T], F32R), sb("xT_lo", [P, T], F32R)]
        small = sb("small", [ROWS, D])
        smallT = sb("smallT", [P, ROWS])
        gwT = [sb("gwT_hi", [P, E], F32R), sb("gwT_lo", [P, E], F32R)]
        logits = sb("logits", [P, TILES, E])
        top = sb("top", [P, 2, TILES])
        scores = sb("scores", [P, E, TILES])
        bit_steps = sb("bit_steps", [P, ROUNDS, 3], U32)
        found = sb("found", [P, 1], U32)
        found_bits = sb("found_bits", [P, 1], U32)
        candidates = sb("candidates", [P, 3], U32)
        above = sb("above", [P, 3], BF16)
        passed = sb("passed", [P, 3])
        n_passed = sb("n_passed", [P, 1])
        junk = sb("junk", [P, 3, E * TILES], BF16)
        greater = sb("greater", [P, E * TILES])
        n_greater = sb("n_greater", [P, 1], BF16)
        n_greater_all = sb("n_greater_all", [P, 1])
        equal = sb("equal", [P, E * TILES], BF16)
        zeros = sb("zeros", [P, E * TILES])
        rank = sb("rank", [P, E * TILES])
        gate = sb("gate", [P, E * TILES])
        gateT = sb("gateT", [P, P])
        ones_b = sb("ones_b", [P, P], BF16)
        before = sb("before", [P, P], BF16)
        gate_rows = sb("gate_rows", [P, 2, T])
        w1_raw = sb("w1_raw", [P, 2, F])
        w2_raw = sb("w2_raw", [P, 2, F])
        W1 = [[sb(f"W1_{part}{i}", [P, F], F32R) for part in ("hi", "lo")] for i in range(2)]
        W2 = [[sb(f"W2_{part}{i}", [P, F], F32R) for part in ("hi", "lo")] for i in range(2)]
        h = sb("h", [P, 4, 512])
        h_hi = sb("h_hi", [P, 4, 512], F32R)
        h_lo = sb("h_lo", [P, 4, 512], F32R)
        gated = sb("gated", [P, 2, 512])
        acc = sb("acc", [P, T])
        gate_dram = nc.dram_tensor("gate_scratch", [P, P], F32, kind="Internal").ap()

        U = es.enter_context(nc.psum_tensor("m_up", [P, 4, 512], F32))
        Y = es.enter_context(nc.psum_tensor("m_y", [P, 2, 512], F32))
        R = es.enter_context(nc.psum_tensor("m_route", [P, 2, 512], F32))

        small_loaded, w_loaded = sem("small_loaded"), [sem("w_loaded0"), sem("w_loaded1")]
        consts = sem("consts")
        dve_chain = sem("dve_chain")
        var_ready, std_ready, xn_ready = sem("var_ready"), sem("std_ready"), sem("xn_ready")
        xT_filled, xT_hi_done, xT_done = sem("xT_filled"), sem("xT_hi_done"), sem("xT_done")
        small_filled, small_done = sem("small_filled"), sem("small_done")
        logits_filled, centred, exped, softmax_done = sem("logits_filled"), sem("centred"), sem("exped"), sem("softmax")
        counted, summed = sem("counted"), sem("summed")
        ties_ready, ties_summed = sem("ties_ready"), sem("ties_summed")
        gate_ready, gateT_filled, gateT_done = sem("gate_ready"), sem("gateT_filled"), sem("gateT_done")
        gate_stored, gate_loaded = sem("gate_stored"), [sem("gate_loaded0"), sem("gate_loaded1")]
        w_split, w_hi = sem("w_split"), sem("w_hi")
        up_done, gelu_done, hi_done, lo_done = sem("up_done"), sem("gelu_done"), sem("hi_done"), sem("lo_done")
        down_done, y_taken, added = sem("down_done"), sem("y_taken"), sem("added")
        accT_filled, accT_added = sem("accT_filled"), sem("accT_added")
        block = es.enter_context(nc.Block())

        def experts(eng, body):
            body(None, 0)
            body(None, 1)
            with eng.Fori(0, E // 2 - 1) as it:
                for c in (2, 3):
                    body(it, c)
            body(None, E)

        def step_of(it, c, k):
            return at(it, 2 * STEPS, c * STEPS + k)

        @block.sync
        def _(sp):
            sp.dma_start(small[0:FC, :], bs1.rearrange("(k p) -> k p", p=P)).then_inc(small_loaded, 16)
            sp.dma_start(small[FC:B2, :], b1.rearrange("e (k p) -> (e k) p", p=P)).then_inc(small_loaded, 16)
            sp.dma_start(small[B2:B2 + 1, :], bs2.rearrange("(a d) -> a d", a=1)).then_inc(small_loaded, 16)
            sp.dma_start(small[B2 + 1:GW, :], b2).then_inc(small_loaded, 16)
            sp.dma_start(small[GW:ROWS, :], gate_w).then_inc(small_loaded, 16)

            def load_weights(c, up, down):
                sp.dma_start(w1_raw[:, c % 2, :], up).then_inc(w_loaded[c % 2], 16)
                sp.dma_start(w2_raw[:, c % 2, :].rearrange("p (k d) -> p k d", d=D),
                             down.rearrange("(k p) d -> p k d", p=P)).then_inc(w_loaded[c % 2], 16)

            load_weights(0, ws1, ws2)
            load_weights(1, w1[0, :, :], w2[0, :, :])
            sp.wait_ge(gateT_done, 1)
            sp.dma_start(gate_dram, gateT[:, :]).then_inc(gate_stored, 16)
            sp.wait_ge(gate_stored, 16)

            def load_gate(c, e):
                sp.dma_start(gate_rows[:, c % 2, :].rearrange("p (t q) -> p t q", q=P),
                             gate_dram[bass.ds(e * TILES, TILES), :].partition_broadcast(P))\
                  .then_inc(gate_loaded[c % 2], 16)

            load_gate(1, 0)
            def body(it, c):
                sp.wait_ge(w_split, at(it, 8, 4 * c))
                e = at(it, 2, c)
                load_weights(c + 1, w1[e, :, :], w2[e, :, :])
                if it is not None or c > 1:
                    sp.wait_ge(y_taken, at(it, 2 * TG, c * TG))
                load_gate(c + 1, e)

            body(None, 1)
            with sp.Fori(0, E // 2 - 1) as it:
                for c in (2, 3):
                    body(it, c)

        @block.gpsimd
        def _(pool):
            nc.gpsimd.memset(ones_b[:, :], 1.0).then_inc(consts, 1)
            nc.gpsimd.memset(before[:, :], 1.0).then_inc(consts, 1)
            nc.gpsimd.memset(zeros[:, :], 0.0).then_inc(consts, 1)
            for r in range(ROUNDS):
                for j in range(3):
                    last = nc.gpsimd.memset(bit_steps[:, r, j:j + 1], (j + 1) << 2 * (ROUNDS - 1 - r))
            last.then_inc(consts, 1)
            pool.wait_ge(consts, 4)
            nc.gpsimd.affine_select(out=before[:, :], in_=before[:, :], compare_op=ALU.is_gt, fill=0.0,
                                    base=0, pattern=[[1, P]], channel_multiplier=-1).then_inc(consts, 1)

            def split(it, c):
                pool.wait_ge(w_loaded[c % 2], at(it, 32, 32 * (c // 2 + 1)))
                if it is not None or c >= 2:
                    pool.wait_ge(down_done, step_of(it, c - 1, 0))
                for n, (raw, W) in enumerate(((w1_raw, W1), (w2_raw, W2))):
                    pool.nop(nofuse=True)
                    nc.gpsimd.tensor_copy(W[c % 2][0][:, :], raw[:, c % 2, :]).then_inc(w_split, 1)
                    pool.wait_ge(w_split, at(it, 8, 4 * c + 2 * n + 1))
                    nc.gpsimd.tensor_tensor(W[c % 2][1][:, :], raw[:, c % 2, :], f32(W[c % 2][0][:, :]),
                                            ALU.subtract).then_inc(w_split, 1)

            def body(it, c):
                if c < E:
                    split(it, c + 1)
                for tg in range(TG):
                    if c > 0:
                        cols = acc[:, tg * 512:(tg + 1) * 512]
                        pool.wait_ge(y_taken, at(it, 2 * TG, c * TG + tg + 1))
                        if c > 1:
                            pool.wait_ge(added, at(it, 2 * TG, (c - 2) * TG + tg + 1))
                        nc.gpsimd.tensor_tensor(cols, cols, gated[:, tg % 2, :], ALU.add).then_inc(added, 1)

            split(None, 0)
            experts(pool, body)

        @block.tensor
        def _(pe):
            pe.wait_ge(small_loaded, 80)
            nc.tensor.transpose(R[:, 1, 0:ROWS], small[:, :], ident[0:ROWS, 0:ROWS]).then_inc(small_filled, 1)
            for g in range(4):
                pe.wait_ge(xn_ready, 1)
                for t in range(4):
                    last = nc.tensor.transpose(U[:, g, t * P:(t + 1) * P], xn[:, 4 * g + t, :], ident[:, :])
                last.then_inc(xT_filled, 1)
            pe.wait_ge(small_done, 3)
            for t in range(TILES):
                if t % 4 == 0:
                    pe.wait_ge(xT_done, t // 4 + 1)
                out, cols = R[:, 0, t * E:(t + 1) * E], slice(t * P, (t + 1) * P)
                nc.tensor.matmul(out, xT[0][:, cols], gwT[0][:, :], start=True, stop=False)
                nc.tensor.matmul(out, xT[0][:, cols], gwT[1][:, :], start=False, stop=False)
                last = nc.tensor.matmul(out, xT[1][:, cols], gwT[0][:, :], start=False, stop=True)
            last.then_inc(logits_filled, 1)

            def up(it, c, k):
                tg, fc = k // FC, k % FC
                if k == 0:
                    pe.wait_ge(w_split, at(it, 8, 4 * c + 4))
                if it is not None or c * STEPS + k >= 4:
                    pe.wait_ge(gelu_done, step_of(it, c, k - 3))
                out, W = U[:, k % 4, :], W1[c % 2]
                cols, tok = slice(fc * P, (fc + 1) * P), slice(tg * 512, (tg + 1) * 512)
                nc.tensor.matmul(out, W[0][:, cols], xT[0][:, tok], start=True, stop=False)
                nc.tensor.matmul(out, W[0][:, cols], xT[1][:, tok], start=False, stop=False)
                nc.tensor.matmul(out, W[1][:, cols], xT[0][:, tok], start=False, stop=True).then_inc(up_done, 1)

            def down(it, c, k):
                tg, fc = k // FC, k % FC
                pe.wait_ge(lo_done, step_of(it, c, k + 1))
                if fc == 0 and (it is not None or c * TG + tg >= 2):
                    pe.wait_ge(y_taken, at(it, 2 * TG, c * TG + tg - 1))
                out, W, cols = Y[:, tg % 2, :], W2[c % 2], slice(fc * P, (fc + 1) * P)
                nc.tensor.matmul(out, W[0][:, cols], h_hi[:, k % 4, :], start=(fc == 0), stop=False)
                nc.tensor.matmul(out, W[0][:, cols], h_lo[:, k % 4, :], start=False, stop=False)
                nc.tensor.matmul(out, W[1][:, cols], h_hi[:, k % 4, :], start=False, stop=(fc == FC - 1))\
                  .then_inc(down_done, 1)

            def body(it, c):
                for k in range(STEPS):
                    up(it, c, k)
                    if k >= LAG:
                        down(it, c, k - LAG)
                    elif c > 0:
                        down(it, c - 1, STEPS + k - LAG)
                    if c == 0:
                        if k < ROUNDS:
                            pe.wait_ge(counted, 3 * (k + 1))
                            nc.tensor.matmul(R[:, 1, 0:3], ones_b[:, :], above[:, :], start=True, stop=True)\
                              .then_inc(summed, 1)
                        else:
                            pe.wait_ge(ties_ready, 2)
                            nc.tensor.matmul(R[:, 0, 0:1], ones_b[:, :], n_greater[:, :], start=True, stop=True)
                            nc.tensor.matmul(R[:, 0, P:2 * P], ones_b[:, :], equal[:, :], start=True, stop=True)
                            nc.tensor.matmul(R[:, 0, 2 * P:3 * P], before[:, :], equal[:, :], start=True,
                                             stop=True).then_inc(ties_summed, 1)
                            pe.wait_ge(gate_ready, 1)
                            nc.tensor.transpose(R[:, 1, P:2 * P], gate[:, :], ident[:, :]).then_inc(gateT_filled, 1)

            pe.wait_ge(consts, 5)
            experts(pe, body)
            for k in range(STEPS - LAG, STEPS):
                down(None, E, k)
            pe.wait_ge(added, E * TG)
            for g in range(4):
                for t in range(4):
                    tile = 4 * g + t
                    last = nc.tensor.transpose(U[:, g, t * P:(t + 1) * P], acc[:, tile * P:(tile + 1) * P], ident[:, :])
                last.then_inc(accT_filled, 1)

        @block.scalar
        def _(act):
            act.wait_ge(var_ready, 1)
            nc.scalar.activation(stats[:, 1, :], stats[:, 1, :], ACT.Sqrt).then_inc(std_ready, 1)
            for g in range(4):
                act.wait_ge(xT_filled, g + 1)
                nc.scalar.activation(xT[0][:, g * 512:(g + 1) * 512], U[:, g, :], ACT.Copy).then_inc(xT_hi_done, 1)
            act.wait_ge(centred, 1)
            nc.scalar.activation(logits[:, :, :], logits[:, :, :], ACT.Exp).then_inc(exped, 1)
            act.wait_ge(xT_done, 4)

            def body(it, c):
                for k in range(STEPS):
                    act.wait_ge(up_done, step_of(it, c, k + 1))
                    if it is not None or c * STEPS + k >= 4:
                        act.wait_ge(lo_done, step_of(it, c, k - 3))
                    col = at(it, 2 * FC, c * FC + k % FC)
                    act.nop(nofuse=True)
                    nc.scalar.activation(h[:, k % 4, :], U[:, k % 4, :], ACT.Gelu_apprx_tanh,
                                         bias=smallT[:, bass.ds(col, 1)]).then_inc(gelu_done, 1)

            experts(act, body)

        @block.vector
        def _(dve):
            chain = [0]

            def link(ins):
                chain[0] += 1
                ins.then_inc(dve_chain, 1)
                dve.wait_ge(dve_chain, chain[0])

            layer_norm(nc, link, XS[:, :, :], xn[:, :, :], squares[:, :, :], stats, var_ready,
                       lambda: dve.wait_ge(std_ready, 1)).then_inc(xn_ready, 1)
            dve.wait_ge(small_filled, 1)
            nc.vector.tensor_copy(smallT[:, :], R[:, 1, 0:ROWS]).then_inc(small_done, 1)
            dve.wait_ge(small_done, 1)
            nc.vector.tensor_copy(gwT[0][:, :], smallT[:, GW:ROWS]).then_inc(small_done, 1)
            dve.wait_ge(small_done, 2)
            nc.vector.tensor_tensor(gwT[1][:, :], smallT[:, GW:ROWS], f32(gwT[0][:, :]), ALU.subtract)\
              .then_inc(small_done, 1)
            for g in range(4):
                cols = slice(g * 512, (g + 1) * 512)
                dve.wait_ge(xT_hi_done, g + 1)
                nc.vector.tensor_tensor(xT[1][:, cols], U[:, g, :], f32(xT[0][:, cols]), ALU.subtract)\
                  .then_inc(xT_done, 1)
            dve.wait_ge(logits_filled, 1)
            L = R[:, 0, 0:TILES * E].rearrange("p (t e) -> p t e", e=E)
            link(nc.vector.tensor_reduce(top[:, 0, :], L, AX.X, ALU.max))
            nc.vector.tensor_tensor(logits[:, :, :], L, bc(top[:, 0, :], E), ALU.subtract).then_inc(centred, 1)
            dve.wait_ge(exped, 1)
            link(nc.vector.tensor_reduce(top[:, 1, :], logits[:, :, :], AX.X, ALU.add))
            link(nc.vector.reciprocal(top[:, 1, :], top[:, 1, :]))
            link(nc.vector.tensor_tensor(scores[:, :, :].rearrange("p e t -> p t e"), logits[:, :, :],
                                         bc(top[:, 1, :], E), ALU.mult))
            flat = scores[:, :, :].rearrange("p e t -> p (e t)")
            dve.wait_ge(consts, 5)
            link(nc.vector.memset(found[:, :], 0))
            link(nc.vector.tensor_copy(candidates[:, :], bit_steps[:, 0, :]))

            def count():
                for j in range(3):
                    nc.vector.tensor_scalar(junk[:, j, :], flat, f32(candidates[:, j:j + 1]), None, ALU.is_ge, ALU.add,
                                            accum_out=above[:, j:j + 1]).then_inc(counted, 1)

            def narrow(r):
                dve.wait_ge(summed, r + 1)
                link(nc.vector.tensor_scalar(passed[:, :], R[:, 1, 0:3], float(TOPK), None, ALU.is_ge, ALU.add,
                                             accum_out=n_passed[:, :]))
                link(nc.vector.tensor_scalar(found_bits[:, :], n_passed[:, :], float(1 << 2 * (ROUNDS - 1 - r)), None,
                                             ALU.mult))
                link(nc.vector.tensor_tensor(found[:, :], found[:, :], found_bits[:, :], ALU.bitwise_or))
                if r + 1 < ROUNDS:
                    link(nc.vector.tensor_tensor(candidates[:, :], bit_steps[:, r + 1, :],
                                                 found[:, :].to_broadcast([P, 3]), ALU.bitwise_or))

            def tie_counts():
                threshold = f32(found[:, :])
                nc.vector.tensor_scalar(greater[:, :], flat, threshold, None, ALU.is_gt, ALU.add,
                                        accum_out=n_greater[:, :]).then_inc(ties_ready, 1)
                nc.vector.tensor_scalar(equal[:, :], flat, threshold, None, ALU.is_equal).then_inc(ties_ready, 1)

            def select():
                dve.wait_ge(ties_summed, 1)
                per_column, rows_before = R[:, 0, P:2 * P], R[:, 0, 2 * P:3 * P]
                link(nc.vector.tensor_copy(n_greater_all[:, :], R[:, 0, 0:1]))
                link(nc.vector.tensor_tensor_scan(rank[:, :], zeros[:, :], per_column, 0.0, ALU.add, ALU.add))
                link(nc.vector.tensor_tensor(rank[:, :], rank[:, :], per_column, ALU.subtract))
                link(nc.vector.tensor_tensor(rank[:, :], rank[:, :], rows_before, ALU.add))
                link(nc.vector.tensor_scalar(rank[:, :], rank[:, :], n_greater_all[:, 0:1], float(TOPK), ALU.add,
                                             ALU.is_lt))
                link(nc.vector.tensor_tensor(rank[:, :], rank[:, :], equal[:, :], ALU.mult))
                link(nc.vector.tensor_tensor(rank[:, :], rank[:, :], greater[:, :], ALU.add))
                nc.vector.tensor_tensor(gate[:, :], rank[:, :], flat, ALU.mult).then_inc(gate_ready, 1)
                dve.wait_ge(gateT_filled, 1)
                nc.vector.tensor_copy(gateT[:, :], R[:, 1, P:2 * P]).then_inc(gateT_done, 1)

            def cut(it, c, k):
                dve.wait_ge(gelu_done, step_of(it, c, k + 1))
                if it is not None or c * STEPS + k >= 4:
                    dve.wait_ge(down_done, step_of(it, c, k - 3))
                nc.vector.tensor_copy(h_hi[:, k % 4, :], h[:, k % 4, :]).then_inc(hi_done, 1)
                dve.wait_ge(hi_done, step_of(it, c, k + 1))
                nc.vector.tensor_tensor(h_lo[:, k % 4, :], h[:, k % 4, :], f32(h_hi[:, k % 4, :]), ALU.subtract)\
                  .then_inc(lo_done, 1)

            def take_y(it, c, tg):
                dve.wait_ge(down_done, step_of(it, c, (tg + 1) * FC))
                bias = smallT[:, bass.ds(at(it, 2, B2 + c), 1)]
                if c == 0:
                    nc.vector.tensor_scalar(acc[:, tg * 512:(tg + 1) * 512], Y[:, tg % 2, :], bias, None, ALU.add)\
                      .then_inc(y_taken, 1)
                    return
                if tg == 0:
                    dve.wait_ge(gate_loaded[c % 2], at(it, 16, 16 * ((c + 1) // 2)))
                if c > 1 or tg >= 2:
                    dve.wait_ge(added, at(it, 2 * TG, (c - 1) * TG + tg - 1))
                nc.vector.scalar_tensor_tensor(out=gated[:, tg % 2, :], in0=Y[:, tg % 2, :], scalar=bias,
                                               in1=gate_rows[:, c % 2, tg * 512:(tg + 1) * 512], op0=ALU.add,
                                               op1=ALU.mult).then_inc(y_taken, 1)

            def body(it, c):
                for k in range(STEPS):
                    if c == 0:
                        if k > 0 and k <= ROUNDS:
                            narrow(k - 1)
                        if k < ROUNDS:
                            count()
                        else:
                            tie_counts()
                            select()
                    cut(it, c, k)
                    if k % FC == FC - 1:
                        if k >= FC:
                            take_y(it, c, k // FC - 1)
                        elif c > 0:
                            take_y(it, c - 1, TG - 1)

            experts(dve, body)
            take_y(None, E, TG - 1)
            for g in range(4):
                dve.wait_ge(accT_filled, g + 1)
                rows = XS[:, 4 * g:4 * g + 4, :]
                nc.vector.tensor_tensor(rows, rows, U[:, g, :].rearrange("p (t d) -> p t d", d=D), ALU.add)\
                  .then_inc(accT_added, 1)


def attention_1(nc, ctx_in, wq, bq, wk, bk, wv, bv, wr, br, XS, ident):
    STEPS = (NC + 1) // 2
    SLOTS = 2 * STEPS
    STAGES = B
    PIECES = [(0, 402), (402, 400), (802, 400), (1202, 400)]
    TWO_PI = 6.2831850
    ROUND = float(3 << 22)

    PREP_USES, TAIL_USES = 16, 2

    def first_use(c):
        return PREP_USES * (1 + min(c, STAGES - 1)) + TAIL_USES * max(c - 1, 0)

    def plan(c, tail, prep):
        slots = [[] for _ in range(SLOTS)]
        if prep:
            for i in range(4):
                slots[i].append(("cT", i))
                slots[i + 2].append(("angle", i))
            for i in range(8):
                slots[6 + i // 2].append(("max", i))
            slots[9].append(("shift", 0))
        if tail:
            slots[1].append(("den", 0))
            slots[1].append(("norm", 0))
            slots[5].append(("proj", 0))
        use, out = first_use(c), []
        for slot in slots:
            row = []
            for kind, i in slot:
                takes = kind not in ("norm", "shift")
                row.append((kind, i, use if takes else None))
                use += takes
            out.append(row)
        return out

    with ExitStack() as es:
        def sb(name, shape, dt=F32):
            return es.enter_context(nc.sbuf_tensor("b_" + name, shape, dt))

        def sem(name):
            return es.enter_context(nc.semaphore("b_" + name))

        xn = sb("xn", [P, TILES, D])
        squares = sb("squares", [P, TILES, D])
        stats = sb("stats", [P, 2, TILES])
        xT = [sb("xT_hi", [P, B * S], F32R), sb("xT_lo", [P, B * S], F32R)]
        Qf = sb("Qf", [P, B * S])
        w_raw = sb("w_raw", [P, 4, D])
        wkT = sb("wkT", [P, D])
        Wq = [sb("Wq_hi", [P, D], F32R), sb("Wq_lo", [P, D], F32R)]
        Wkr = [sb("Wkr_hi", [P, D], F32R), sb("Wkr_lo", [P, D], F32R)]
        b_rows = sb("b_rows", [3, D])
        b_cols = sb("b_cols", [P, 3])
        bv_row = sb("bv_row", [1, D])
        turn = sb("turn", [P, 2])
        c_in = sb("c_in", [P, NC, D])
        c_nat = sb("c_nat", [P, 2, NC, D])
        cT = [sb("cT_hi", [P, NC * P], F32R), sb("cT_lo", [P, NC * P], F32R)]
        turns = sb("turns", [P, 4, 402])
        whole = sb("whole", [P, 4, 402])
        cosT = sb("cosT", [P, 4, 402])
        K = [[sb(f"K_{part}{i}", [P, NC * P], F32R) for part in ("hi", "lo")] for i in range(2)]
        Qs = [[sb(f"Qs_{part}{i}", [P, S], F32R) for part in ("hi", "lo")] for i in range(2)]
        maxes = sb("maxes", [P, 2, 8])
        neg_max = sb("neg_max", [P, 2, 2])
        shift_diag = sb("shift_diag", [P, 2, 2, P], BF16)
        probs = sb("probs", [P, 4, 2 * S])
        den = sb("den", [P, 2 * S])
        outT = sb("outT", [P, S])
        rden = sb("rden", [P, S])
        ones = sb("ones", [P, P])
        ones_b = sb("ones_b", [P, P], BF16)

        Sc = es.enter_context(nc.psum_tensor("b_scores", [P, 4, 512], F32))
        PV = es.enter_context(nc.psum_tensor("b_pv", [P, 2, 512], F32))
        X = es.enter_context(nc.psum_tensor("b_work", [P, 2, 512], F32))

        w_loaded, c_in_loaded, c_loaded = sem("w_loaded"), sem("c_in_loaded"), [sem("c_loaded0"), sem("c_loaded1")]
        consts, dve_chain = sem("consts"), sem("dve_chain")
        var_ready, std_ready, xn_ready = sem("var_ready"), sem("std_ready"), sem("xn_ready")
        wT_filled, wT_done = sem("wT_filled"), sem("wT_done")
        wkr_filled, w_ready = sem("wkr_filled"), sem("w_ready")
        xT_filled, xT_hi_done, xT_done = sem("xT_filled"), sem("xT_hi_done"), sem("xT_done")
        q_filled, q_biased, q_done = sem("q_filled"), sem("q_biased"), sem("q_done")
        bank_full = [sem("bank0_full"), sem("bank1_full")]
        bank_free = [sem("bank0_free"), sem("bank1_free")]
        qs_ready = sem("qs_ready")
        c_hi_done = sem("c_hi_done")
        angle_steps = sem("angle_steps")
        cos_done, k_hi_done, k_lo_done = sem("cos_done"), sem("k_hi_done"), sem("k_lo_done")
        shift_steps = sem("shift_steps")
        scores_done, probs_done, pv_done = sem("scores_done"), sem("probs_done"), sem("pv_done")
        den_added, norm_done = sem("den_added"), sem("norm_done")
        block = es.enter_context(nc.Block())

        TURN = first_use(3) - first_use(1)
        assert TURN % 2 == 0

        def filled(eng, it, use):
            eng.wait_ge(bank_full[use % 2], at(it, TURN // 2, use // 2 + 1))

        def taken(eng, it, use):
            eng.wait_ge(bank_free[use % 2], at(it, TURN // 2, use // 2 + 1))

        def stages(eng, body):
            body(None, 0)
            with eng.Fori(0, 3) as it:
                for c in (1, 2):
                    body(it, c)
            body(None, STAGES - 1)

        def flags(it, c):
            return c > 0, it is not None or c + 1 < STAGES

        def the_plan(it, c):
            return plan(c, *flags(it, c))

        def step_of(it, c, first):
            return at(it, 2 * STEPS, c * STEPS + first)

        def before_in_buffer(it, c, j):
            if j >= 4:
                return step_of(it, c, j - 3)
            return step_of(it, c - 1, (j + 4 if j < 3 else 3) + 1)

        def rows_of(j, k):
            return LAST if 2 * j + k == NC - 1 else P

        def chunks_of(j):
            return min(2, NC - 2 * j)

        @block.sync
        def _(sp):
            for i, w in enumerate((wq, wk, wr, wv)):
                sp.dma_start(w_raw[:, i, :], w).then_inc(w_loaded, 16)
            for i, b in enumerate((bq, bk, br)):
                sp.dma_start(b_rows[i:i + 1, :], b.rearrange("(a d) -> a d", a=1)).then_inc(w_loaded, 16)
            sp.dma_start(bv_row[:, :], bv.rearrange("(a d) -> a d", a=1)).then_inc(w_loaded, 16)
            sp.wait_ge(consts, 1)

            def load(dst, b, loaded):
                sp.dma_start(dst[:, 0:NC - 1, :],
                             ctx_in[b, 0:(NC - 1) * P, :].rearrange("(c p) d -> p c d", p=P)).then_inc(loaded, 16)
                sp.dma_start(dst[0:LAST, NC - 1, :], ctx_in[b, (NC - 1) * P:N, :]).then_inc(loaded, 16)

            def load_for_transposes(it, s):
                sp.wait_ge(c_hi_done, at(it, 8, 4 * s))
                load(c_in[:, :, :], at(it, 2, s), c_in_loaded)

            load(c_in[:, :, :], 0, c_in_loaded)
            load(c_nat[:, 0, :, :], 0, c_loaded[0])
            load_for_transposes(None, 1)
            load(c_nat[:, 1, :, :], 1, c_loaded[1])

            with sp.Fori(0, 3) as it:
                for c in (1, 2):
                    load_for_transposes(it, c + 1)
                    sp.wait_ge(pv_done, step_of(it, c, 0))
                    load(c_nat[:, (c + 1) % 2, :, :], at(it, 2, c + 1), c_loaded[(c + 1) % 2])

        @block.gpsimd
        def _(pool):
            nc.gpsimd.memset(c_in[:, NC - 1, :], 0.0).then_inc(consts, 1)
            nc.gpsimd.memset(ones[:, :], 1.0).then_inc(consts, 1)
            nc.gpsimd.memset(ones_b[:, :], 1.0).then_inc(consts, 1)

            def body(it, c):
                for j in range(1, STEPS - 1):
                    pool.wait_ge(probs_done, step_of(it, c, j + 1))
                    if j == 1:
                        if c > 0:
                            filled(pool, it, [u for s in the_plan(it, c) for k, i, u in s if k == "den"][0])
                        first = probs[:, 0, :]
                    else:
                        pool.wait_ge(den_added, at(it, 2 * (STEPS - 2), c * (STEPS - 2) + j - 1))
                        first = den[:, :]
                    nc.gpsimd.tensor_tensor(den[:, :], first, probs[:, j % 4, :], ALU.add).then_inc(den_added, 1)

            stages(pool, body)

        @block.tensor
        def _(pe):
            pe.wait_ge(w_loaded, 128)
            nc.tensor.transpose(X[:, 0, 0:D], w_raw[:, 1, :], ident[:, :])
            nc.tensor.transpose(X[:, 0, D:D + 3], b_rows[:, :], ident[0:3, 0:3]).then_inc(wT_filled, 1)
            pe.wait_ge(wT_done, 2)
            nc.tensor.matmul(X[:, 1, 0:D], wkT[:, :], w_raw[:, 2, :], start=True, stop=True)
            nc.tensor.matmul(X[:, 1, D:D + 1], w_raw[:, 2, :], b_cols[:, 1:2], start=True, stop=True)\
              .then_inc(wkr_filled, 1)
            pe.wait_ge(xn_ready, 1)
            for g in range(4):
                for t in range(4):
                    last = nc.tensor.transpose(Sc[:, g, t * P:(t + 1) * P], xn[:, 4 * g + t, :], ident[:, :])
                last.then_inc(xT_filled, 1)
            pe.wait_ge(w_ready, 2)

            def split_product(out, a, b, cols_a, cols_b, stop=True):
                nc.tensor.matmul(out, a[0][:, cols_a], b[0][:, cols_b], start=True, stop=False)
                nc.tensor.matmul(out, a[0][:, cols_a], b[1][:, cols_b], start=False, stop=False)
                return nc.tensor.matmul(out, a[1][:, cols_a], b[0][:, cols_b], start=False, stop=stop)

            for g in range(4):
                pe.wait_ge(xT_done, g + 1)
                if g >= 2:
                    pe.wait_ge(q_done, g - 1)
                split_product(PV[:, g % 2, :], Wq, xT, slice(0, D), slice(g * 512, (g + 1) * 512)).then_inc(q_filled, 1)
            pe.wait_ge(w_ready, 5)
            pe.wait_ge(q_done, 4)

            def item(it, c, kind, i, use):
                bank, s = use % 2, c + 1
                if use >= 2:
                    taken(pe, it, use - 2)
                out = X[:, bank, :]
                if kind == "cT":
                    pe.wait_ge(c_in_loaded, at(it, 64, 32 * (s + 1)))
                    for ch in range(4 * i, min(4 * i + 4, NC)):
                        last = nc.tensor.transpose(out[:, ch % 4 * P:(ch % 4 + 1) * P], c_in[:, ch, :],
                                                   ident[:, :])
                elif kind == "angle":
                    off, w = PIECES[i]
                    last = split_product(out[:, :w], Wkr, cT, slice(0, D), slice(off, off + w))
                elif kind == "max":
                    off, w = PIECES[i % 4]
                    if i < 4:
                        pe.wait_ge(k_hi_done, at(it, 8, 4 * s + i + 1))
                    if i == 0:
                        pe.wait_ge(qs_ready, at(it, 4, 2 * s + 2))
                    last = nc.tensor.matmul(out[:, :w], Qs[s % 2][0][:, i // 4 * P:(i // 4 + 1) * P],
                                            K[s % 2][0][:, off:off + w], start=True, stop=True)
                elif kind == "den":
                    pe.wait_ge(den_added, at(it, 2 * (STEPS - 2), c * (STEPS - 2)))
                    for k in range(2):
                        nc.tensor.matmul(out[:, 0:S], ones[:, :], den[:, k * S:(k + 1) * S], start=(k == 0), stop=False)
                    last = nc.tensor.matmul(out[:, 0:S], ones[0:LAST, :], probs[0:LAST, (STEPS - 1) % 4, 0:S],
                                            start=False, stop=True)
                elif kind == "proj":
                    pe.wait_ge(norm_done, at(it, 2, c))
                    for j in range(2):
                        half = out[:, j * D:(j + 1) * D]
                        nc.tensor.matmul(half, outT[:, j * P:(j + 1) * P], w_raw[:, 3, :], start=True, stop=False)
                        last = nc.tensor.matmul(half, ones[0:1, :], bv_row[:, :], start=False, stop=True)
                last.then_inc(bank_full[bank], 1)

            def qk(it, c, j, k):
                if k == 0:
                    if c > 0 or j > 3:
                        pe.wait_ge(probs_done, before_in_buffer(it, c, j))
                    if j == 0:
                        pe.wait_ge(shift_steps, at(it, 4, 2 * c + 2))
                        pe.wait_ge(k_lo_done, at(it, 8, 4 * c + 4))
                if k >= chunks_of(j):
                    return
                rows = rows_of(j, k)
                out = Sc[0:rows, j % 4, k * S:(k + 1) * S]
                first = (2 * j + k) * P
                split_product(out, K[c % 2], Qs[c % 2], slice(first, first + rows), slice(0, S), stop=False)
                last = nc.tensor.matmul(out, ones_b[:, 0:rows], shift_diag[:, c % 2, :, :], start=False, stop=True)
                if k == chunks_of(j) - 1:
                    last.then_inc(scores_done, 1)

            def pv(it, c, j, k):
                if k == 0:
                    pe.wait_ge(probs_done, step_of(it, c, j + 1))
                    if j == 0:
                        pe.wait_ge(c_loaded[c % 2], at(it, 32, 32 * (c // 2 + 1)))
                        if c > 1:
                            pe.wait_ge(norm_done, at(it, 2, c - 1))
                if k >= chunks_of(j):
                    return
                rows = rows_of(j, k)
                last = nc.tensor.matmul(PV[:, c % 2, 0:S], c_nat[0:rows, c % 2, 2 * j + k, :],
                                        probs[0:rows, j % 4, k * S:(k + 1) * S],
                                        start=(j == 0 and k == 0), stop=(j == STEPS - 1))
                if k == chunks_of(j) - 1:
                    last.then_inc(pv_done, 1)

            def body(it, c):
                tail, prep = flags(it, c)
                slots = the_plan(it, c)
                for j in range(STEPS):
                    for k in range(2):
                        pv(it, c, j, k)
                        if j + 2 < STEPS:
                            qk(it, c, j + 2, k)
                        elif prep:
                            qk(it, c + 1, j + 2 - STEPS, k)
                        for kind, i, use in slots[2 * j + k]:
                            if use is not None:
                                item(it, c, kind, i, use)

            pe.wait_ge(consts, 3)
            for use, (kind, i) in enumerate([("cT", i) for i in range(4)] + [("angle", i) for i in range(4)] +
                                            [("max", i) for i in range(8)]):
                item(None, -1, kind, i, use)
            for j in range(2):
                for k in range(2):
                    qk(None, 0, j, k)
            stages(pe, body)
            for n, kind in enumerate(("den", "proj")):
                item(None, STAGES, kind, 0, first_use(STAGES) + n)

        @block.scalar
        def _(act):
            act.wait_ge(var_ready, 1)
            nc.scalar.activation(stats[:, 1, :], stats[:, 1, :], ACT.Sqrt).then_inc(std_ready, 1)
            for g in range(4):
                act.wait_ge(xT_filled, g + 1)
                nc.scalar.activation(xT[0][:, g * 512:(g + 1) * 512], Sc[:, g, :], ACT.Copy).then_inc(xT_hi_done, 1)
            act.wait_ge(wT_done, 2)
            for g in range(4):
                act.wait_ge(q_filled, g + 1)
                nc.scalar.activation(Qf[:, g * 512:(g + 1) * 512], PV[:, g % 2, :], ACT.Identity, bias=b_cols[:, 0:1])\
                  .then_inc(q_done, 1)

            def item(it, c, kind, i, use):
                s = c + 1
                if kind == "cT":
                    filled(act, it, use)
                    w = min(4, NC - 4 * i) * P
                    nc.scalar.activation(cT[0][:, i * 512:i * 512 + w], X[:, use % 2, :w], ACT.Copy)\
                      .then_inc(c_hi_done, 1)
                elif kind == "angle":
                    off, w = PIECES[i]
                    act.wait_ge(angle_steps, at(it, 24, 12 * s + 3 * i + 3))
                    if s > 0:
                        act.wait_ge(k_lo_done, at(it, 8, 4 * s + i - 3))
                    nc.scalar.activation(cosT[:, i, :w], turns[:, i, :w], ACT.Sin, scale=TWO_PI)\
                      .then_inc(cos_done, 1)
                    act.wait_ge(cos_done, at(it, 8, 4 * s + i + 1))
                    nc.scalar.activation(K[s % 2][0][:, off:off + w], cosT[:, i, :w], ACT.Copy)\
                      .then_inc(k_hi_done, 1)

            def exp(it, c, j):
                act.wait_ge(scores_done, step_of(it, c, j + 1))
                if c > 0 or j > 3:
                    act.wait_ge(pv_done, before_in_buffer(it, c, j))
                if j >= 4:
                    act.wait_ge(den_added, at(it, 2 * (STEPS - 2), c * (STEPS - 2) + (j - 4 or 1)))
                elif c > 0 and j == 2:
                    filled(act, it, [u for s in the_plan(it, c) for k, i, u in s if k == "den"][0])
                elif c > 0:
                    act.wait_ge(den_added, at(it, 2 * (STEPS - 2), (c - 1) * (STEPS - 2) + (j + 4 if j < 2 else j)))
                rows, cols = rows_of(j, 0) if chunks_of(j) == 1 else P, chunks_of(j) * S
                nc.scalar.activation(probs[0:rows, j % 4, 0:cols], Sc[0:rows, j % 4, 0:cols], ACT.Exp)\
                  .then_inc(probs_done, 1)

            def body(it, c):
                tail, prep = flags(it, c)
                slots = the_plan(it, c)
                for j in range(STEPS):
                    if j + 1 < STEPS:
                        exp(it, c, j + 1)
                    elif prep:
                        exp(it, c + 1, 0)
                    for slot in slots[2 * j:2 * j + 2]:
                        for kind, i, use in slot:
                            item(it, c, kind, i, use)

            for use, (kind, i) in enumerate([("cT", i) for i in range(4)] + [("angle", i) for i in range(4)]):
                item(None, -1, kind, i, use)
            exp(None, 0, 0)
            stages(act, body)

        @block.vector
        def _(dve):
            chain = [0]

            def link(ins):
                chain[0] += 1
                ins.then_inc(dve_chain, 1)
                dve.wait_ge(dve_chain, chain[0])

            dve.wait_ge(wT_filled, 1)
            nc.vector.tensor_copy(wkT[:, :], X[:, 0, 0:D]).then_inc(wT_done, 1)
            nc.vector.tensor_copy(b_cols[:, :], X[:, 0, D:D + 3]).then_inc(wT_done, 1)
            link(nc.vector.tensor_copy(Wq[0][:, :], w_raw[:, 0, :]))
            nc.vector.tensor_tensor(Wq[1][:, :], w_raw[:, 0, :], f32(Wq[0][:, :]), ALU.subtract).then_inc(w_ready, 2)
            layer_norm(nc, link, XS[:, :, :], xn[:, :, :], squares[:, :, :], stats, var_ready,
                       lambda: dve.wait_ge(std_ready, 1)).then_inc(xn_ready, 1)
            dve.wait_ge(wkr_filled, 1)
            link(nc.vector.tensor_copy(Wkr[0][:, :], X[:, 1, 0:D]))
            nc.vector.tensor_tensor(Wkr[1][:, :], X[:, 1, 0:D], f32(Wkr[0][:, :]), ALU.subtract).then_inc(w_ready, 1)
            link(nc.vector.tensor_tensor(turn[:, 0:1], X[:, 1, D:D + 1], b_cols[:, 2:3], ALU.add))
            nc.vector.tensor_scalar(turn[:, 1:2], turn[:, 0:1], 1.0 / (2.0 * math.pi), 0.25, ALU.mult, ALU.add)\
              .then_inc(w_ready, 2)
            for g in range(4):
                cols = slice(g * 512, (g + 1) * 512)
                dve.wait_ge(xT_hi_done, g + 1)
                nc.vector.tensor_tensor(xT[1][:, cols], Sc[:, g, :], f32(xT[0][:, cols]), ALU.subtract).then_inc(xT_done, 1)
            dve.wait_ge(q_done, 4)
            dve.wait_ge(w_ready, 5)

            def take_q(it, s):
                rows = Qf[:, bass.ds(at(it, 2 * S, s * S), S)]
                nc.vector.tensor_copy(Qs[s % 2][0][:, :], rows).then_inc(qs_ready, 1)
                dve.wait_ge(qs_ready, at(it, 4, 2 * s + 1))
                nc.vector.tensor_tensor(Qs[s % 2][1][:, :], rows, f32(Qs[s % 2][0][:, :]), ALU.subtract)\
                  .then_inc(qs_ready, 1)

            def item(it, c, kind, i, use):
                s = c + 1
                bank = None if use is None else use % 2
                if kind == "cT":
                    w = min(4, NC - 4 * i) * P
                    cols = slice(i * 512, i * 512 + w)
                    dve.wait_ge(c_hi_done, at(it, 8, 4 * s + i + 1))
                    nc.vector.tensor_tensor(cT[1][:, cols], X[:, bank, :w], f32(cT[0][:, cols]), ALU.subtract)\
                      .then_inc(bank_free[bank], 1)
                    if i == 3:
                        take_q(it, s)
                elif kind == "angle":
                    off, w = PIECES[i]
                    filled(dve, it, use)
                    if s > 0:
                        dve.wait_ge(cos_done, at(it, 8, 4 * s + i - 3))
                    t, n = turns[:, i, :w], whole[:, i, :w]
                    done = at(it, 24, 12 * s + 3 * i + 1), at(it, 24, 12 * s + 3 * i + 2)
                    nc.vector.tensor_scalar(t, X[:, bank, :w], 1.0 / (2.0 * math.pi), turn[:, 1:2], ALU.mult, ALU.add)\
                      .then_inc(bank_free[bank], 1)
                    taken(dve, it, use)
                    nc.vector.tensor_scalar(n, t, ROUND, ROUND, ALU.add, ALU.subtract).then_inc(angle_steps, 1)
                    dve.wait_ge(angle_steps, done[0])
                    nc.vector.tensor_tensor(t, t, n, ALU.subtract).then_inc(angle_steps, 1)
                    dve.wait_ge(angle_steps, done[1])
                    nc.vector.tensor_scalar(t, t, 0.5, -0.5, ALU.min, ALU.max).then_inc(angle_steps, 1)
                elif kind == "max":
                    if i < 4:
                        off, w = PIECES[i]
                        dve.wait_ge(k_hi_done, at(it, 8, 4 * s + i + 1))
                        nc.vector.tensor_tensor(K[s % 2][1][:, off:off + w], cosT[:, i, :w],
                                                f32(K[s % 2][0][:, off:off + w]), ALU.subtract).then_inc(k_lo_done, 1)
                    filled(dve, it, use)
                    w = min(PIECES[i % 4][1], N - PIECES[i % 4][0])
                    nc.vector.tensor_reduce(maxes[:, s % 2, i:i + 1], X[:, bank, :w], AX.X, ALU.max)\
                      .then_inc(bank_free[bank], 1)
                elif kind == "shift":
                    taken(dve, it, last_max_use(c) - 1)
                    taken(dve, it, last_max_use(c))
                    nc.vector.tensor_reduce(neg_max[:, s % 2, :], maxes[:, s % 2, :].rearrange("p (u k) -> p u k", k=4),
                                            AX.X, ALU.max, negate=True).then_inc(shift_steps, 1)
                    dve.wait_ge(shift_steps, at(it, 4, 2 * s + 1))
                    nc.vector.tensor_tensor(shift_diag[:, s % 2, :, :],
                                            ident[:, :].unsqueeze(1).to_broadcast([P, 2, P]),
                                            bc(neg_max[:, s % 2, :], P), ALU.mult).then_inc(shift_steps, 1)
                elif kind == "den":
                    filled(dve, it, use)
                    nc.vector.reciprocal(rden[:, :], X[:, bank, 0:S]).then_inc(bank_free[bank], 1)
                    taken(dve, it, use)
                elif kind == "norm":
                    dve.wait_ge(pv_done, step_of(it, c, 0))
                    nc.vector.tensor_tensor(outT[:, :], PV[:, (c - 1) % 2, 0:S], rden[:, :], ALU.mult)\
                      .then_inc(norm_done, 1)
                elif kind == "proj":
                    filled(dve, it, use)
                    rows = XS[:, bass.ds(at(it, 4, 2 * (c - 1)), 2), :]
                    nc.vector.tensor_tensor(rows, rows, X[:, bank, :2 * D].rearrange("p (j d) -> p j d", d=D), ALU.add)\
                      .then_inc(bank_free[bank], 1)

            def last_max_use(c):
                if c < 0:
                    return PREP_USES - 1
                return max(u for slot in plan(c, c > 0, True) for k, i, u in slot if k == "max")

            def body(it, c):
                for slot in the_plan(it, c):
                    for kind, i, use in slot:
                        item(it, c, kind, i, use)

            for use, (kind, i) in enumerate([("cT", i) for i in range(4)] + [("angle", i) for i in range(4)] +
                                            [("max", i) for i in range(8)]):
                item(None, -1, kind, i, use)
            item(None, -1, "shift", 0, None)
            stages(dve, body)
            for n, (kind, use) in enumerate((("den", first_use(STAGES)), ("norm", None), ("proj", first_use(STAGES) + 1))):
                item(None, STAGES, kind, 0, use)


def ffn_1(nc, base_w, base_b, shared_a, shared_b, routed_a, routed_b, router_w, router_b, XS, ident, out):
    E, RK = routed_a.shape[0], routed_a.shape[1]
    ER = E * RK
    T = B * S
    ROWS = E + ER

    with ExitStack() as es:
        def sb(name, shape, dt=F32):
            return es.enter_context(nc.sbuf_tensor("f_" + name, shape, dt))

        def sem(name):
            return es.enter_context(nc.semaphore("f_" + name))

        xn = sb("xn", [P, TILES, D])
        squares = sb("squares", [P, TILES, D])
        stats = sb("stats", [P, 2, TILES])
        xT = sb("xT", [P, T])
        small = sb("small", [ROWS, D])
        smallT = sb("smallT", [P, ROWS])
        base = sb("base", [P, D])
        sa = sb("sa", [RK, D])
        sbn = sb("sbn", [P, RK])
        sbT = sb("sbT", [RK, D])
        rb = sb("rb", [P, E, RK])
        rbT = sb("rbT", [ER, D])
        rows = sb("rows", [1, D + E])
        Wb = sb("Wb", [P, D])
        ones = sb("ones", [1, P])
        select = sb("select", [E, ER])
        gate = sb("gate", [P, TILES, E])
        top = sb("top", [P, 2, TILES])
        rank = sb("rank", [P, TILES, E])
        ahead = sb("ahead", [P, TILES, E])
        weights = sb("weights", [P, TILES, E])
        wT = sb("wT", [E, T])
        spread = sb("spread", [ER, T])
        hT = sb("hT", [ER, T])

        A = es.enter_context(nc.psum_tensor("f_a", [P, 4, 512], F32))
        C = es.enter_context(nc.psum_tensor("f_c", [P, 4, 512], F32))

        loaded, consts, dve_chain = sem("loaded"), sem("consts"), sem("dve_chain")
        var_ready, std_ready, xn_ready = sem("var_ready"), sem("std_ready"), sem("xn_ready")
        small_filled, small_done, wb_filled, wb_done = sem("small_filled"), sem("small_done"), sem("wb_filled"), sem("wb_done")
        xT_filled, xT_done = sem("xT_filled"), sem("xT_done")
        logits_filled, centred, exped = sem("logits_filled"), sem("centred"), sem("exped")
        h_filled, weighted, wT_filled, wT_done = sem("h_filled"), sem("weighted"), sem("wT_filled"), sem("wT_done")
        spread_filled, spread_done, h_done = sem("spread_filled"), sem("spread_done"), sem("h_done")
        y_filled, y_added, stored = sem("y_filled"), sem("y_added"), sem("stored")
        block = es.enter_context(nc.Block())

        @block.sync
        def _(sp):
            sp.dma_start(small[0:E, :], router_w).then_inc(loaded, 16)
            sp.dma_start(small[E:ROWS, :], routed_a.rearrange("e r d -> (e r) d")).then_inc(loaded, 16)
            sp.dma_start(base[:, :], base_w).then_inc(loaded, 16)
            sp.dma_start(sa[:, :], shared_a).then_inc(loaded, 16)
            sp.dma_start(sbn[:, :], shared_b).then_inc(loaded, 16)
            sp.dma_start(rb[:, :, :], routed_b.rearrange("e o r -> o e r")).then_inc(loaded, 16)
            sp.dma_start(rows[:, 0:D], base_b.rearrange("(a d) -> a d", a=1)).then_inc(loaded, 16)
            sp.dma_start(rows[:, D:D + E], router_b.rearrange("(a d) -> a d", a=1)).then_inc(loaded, 16)
            tokens = out.rearrange("b (j p) d -> p (b j) d", p=P)
            for g in range(4):
                sp.wait_ge(y_added, g + 1)
                sp.dma_start(tokens[:, 4 * g:4 * g + 4, :], XS[:, 4 * g:4 * g + 4, :]).then_inc(stored, 16)
            sp.wait_ge(stored, 64)

        @block.gpsimd
        def _(pool):
            nc.gpsimd.memset(ones[:, :], 1.0).then_inc(consts, 1)
            nc.gpsimd.memset(select[:, :], 1.0).then_inc(consts, 1)
            for e in range(E):
                nc.gpsimd.memset(rank[:, :, e:e + 1], float(e)).then_inc(consts, 1)
            pool.wait_ge(consts, 2 + E)
            nc.gpsimd.affine_select(out=select[:, :], in_=select[:, :], compare_op=ALU.is_ge, fill=0.0,
                                    base=0, pattern=[[1, ER]], channel_multiplier=-RK).then_inc(consts, 1)
            pool.wait_ge(consts, 3 + E)
            nc.gpsimd.affine_select(out=select[:, :], in_=select[:, :], compare_op=ALU.is_ge, fill=0.0,
                                    base=RK - 1, pattern=[[-1, ER]], channel_multiplier=RK).then_inc(consts, 1)

        @block.tensor
        def _(pe):
            pe.wait_ge(loaded, 128)
            pe.wait_ge(consts, 4 + E)
            nc.tensor.transpose(A[:, 0, 0:ROWS], small[:, :], ident[0:ROWS, 0:ROWS])
            nc.tensor.transpose(A[0:RK, 1, 0:D], sbn[:, :], ident[:, :])
            nc.tensor.transpose(A[0:ER, 1, D:2 * D], rb[:, :, :].rearrange("p e r -> p (e r)"), ident[:, :])\
              .then_inc(small_filled, 1)
            pe.wait_ge(small_done, 3)
            nc.tensor.matmul(A[:, 2, 0:D], base[:, :], ident[:, :], start=True, stop=False)
            nc.tensor.matmul(A[:, 2, 0:D], sa[:, :], sbT[:, :], start=False, stop=True).then_inc(wb_filled, 1)
            pe.wait_ge(xn_ready, 1)
            for g in range(4):
                for t in range(4):
                    last = nc.tensor.transpose(C[:, g, t * P:(t + 1) * P], xn[:, 4 * g + t, :], ident[:, :])
                last.then_inc(xT_filled, 1)
            for t in range(TILES):
                if t % 4 == 0:
                    pe.wait_ge(xT_done, t // 4 + 1)
                o = A[:, 3, t * E:(t + 1) * E]
                nc.tensor.matmul(o, xT[:, t * P:(t + 1) * P], smallT[:, 0:E], start=True, stop=False)
                last = nc.tensor.matmul(o, ones[:, :], rows[:, D:D + E], start=False, stop=True)
            last.then_inc(logits_filled, 1)
            for g in range(4):
                nc.tensor.matmul(C[0:ER, g, :], smallT[:, E:ROWS], xT[:, g * 512:(g + 1) * 512], start=True,
                                 stop=True).then_inc(h_filled, 1)
            pe.wait_ge(weighted, 1)
            for g in range(4):
                if g == 2:
                    pe.wait_ge(wb_done, 1)
                if g == 3:
                    pe.wait_ge(centred, 1)
                for t in range(4):
                    last = nc.tensor.transpose(A[0:E, g, t * P:(t + 1) * P], weights[:, 4 * g + t, :], ident[:, :])
                last.then_inc(wT_filled, 1)
            for g in range(4):
                pe.wait_ge(wT_done, g + 1)
                nc.tensor.matmul(A[0:ER, g, :], select[:, :], wT[:, g * 512:(g + 1) * 512], start=True, stop=True)\
                  .then_inc(spread_filled, 1)
            for g in range(4):
                pe.wait_ge(h_done, g + 1)
                for t in range(4):
                    tok = slice((4 * g + t) * P, (4 * g + t + 1) * P)
                    o = A[:, g, t * D:(t + 1) * D]
                    nc.tensor.matmul(o, xT[:, tok], Wb[:, :], start=True, stop=False)
                    nc.tensor.matmul(o, hT[:, tok], rbT[:, :], start=False, stop=False)
                    last = nc.tensor.matmul(o, ones[:, :], rows[:, 0:D], start=False, stop=True)
                last.then_inc(y_filled, 1)

        @block.scalar
        def _(act):
            act.wait_ge(var_ready, 1)
            nc.scalar.activation(stats[:, 1, :], stats[:, 1, :], ACT.Sqrt).then_inc(std_ready, 1)
            act.wait_ge(wb_filled, 1)
            nc.scalar.activation(Wb[:, :], A[:, 2, 0:D], ACT.Copy).then_inc(wb_done, 1)
            for g in range(0, 4, 2):
                act.wait_ge(xT_filled, g + 2)
                nc.scalar.activation(xT[:, g * 512:(g + 2) * 512], C[:, g:g + 2, :].rearrange("p a n -> p (a n)"),
                                     ACT.Copy).then_inc(xT_done, 2)
            act.wait_ge(centred, 1)
            nc.scalar.activation(gate[:, :, :], gate[:, :, :], ACT.Exp).then_inc(exped, 1)
            for g in range(4):
                act.wait_ge(spread_filled, g + 1)
                nc.scalar.activation(spread[:, g * 512:(g + 1) * 512], A[0:ER, g, :], ACT.Copy).then_inc(spread_done, 1)

        @block.vector
        def _(dve):
            chain = [0]

            def link(ins):
                chain[0] += 1
                ins.then_inc(dve_chain, 1)
                dve.wait_ge(dve_chain, chain[0])

            layer_norm(nc, link, XS[:, :, :], xn[:, :, :], squares[:, :, :], stats, var_ready,
                       lambda: dve.wait_ge(std_ready, 1)).then_inc(xn_ready, 1)
            dve.wait_ge(small_filled, 1)
            nc.vector.tensor_copy(smallT[:, :], A[:, 0, 0:ROWS]).then_inc(small_done, 1)
            nc.vector.tensor_copy(sbT[:, :], A[0:RK, 1, 0:D]).then_inc(small_done, 1)
            nc.vector.tensor_copy(rbT[:, :], A[0:ER, 1, D:2 * D]).then_inc(small_done, 1)
            dve.wait_ge(logits_filled, 1)
            L = A[:, 3, 0:TILES * E].rearrange("p (t e) -> p t e", e=E)
            link(nc.vector.tensor_reduce(top[:, 0, :], L, AX.X, ALU.max))
            nc.vector.tensor_tensor(gate[:, :, :], L, bc(top[:, 0, :], E), ALU.subtract).then_inc(centred, 1)
            dve.wait_ge(exped, 1)
            link(nc.vector.tensor_reduce(top[:, 1, :], gate[:, :, :], AX.X, ALU.add))
            link(nc.vector.reciprocal(top[:, 1, :], top[:, 1, :]))
            link(nc.vector.tensor_tensor(gate[:, :, :], gate[:, :, :], bc(top[:, 1, :], E), ALU.mult))
            dve.wait_ge(consts, 4 + E)
            for k in range(1, E):
                link(nc.vector.tensor_tensor(ahead[:, :, 0:E - k], gate[:, :, k:E], gate[:, :, 0:E - k], ALU.is_gt))
                link(nc.vector.tensor_tensor(rank[:, :, 0:E - k], rank[:, :, 0:E - k], ahead[:, :, 0:E - k], ALU.add))
                link(nc.vector.tensor_tensor(rank[:, :, k:E], rank[:, :, k:E], ahead[:, :, 0:E - k], ALU.subtract))
            link(nc.vector.scalar_tensor_tensor(out=weights[:, :, :], in0=rank[:, :, :], scalar=1.5, in1=gate[:, :, :],
                                                op0=ALU.is_lt, op1=ALU.mult))
            link(nc.vector.tensor_reduce(top[:, 0, :], weights[:, :, :], AX.X, ALU.add))
            link(nc.vector.tensor_scalar(top[:, 0, :], top[:, 0, :], 1e-6, None, ALU.add))
            link(nc.vector.reciprocal(top[:, 0, :], top[:, 0, :]))
            nc.vector.tensor_tensor(weights[:, :, :], weights[:, :, :], bc(top[:, 0, :], E), ALU.mult)\
              .then_inc(weighted, 1)
            for g in range(4):
                dve.wait_ge(wT_filled, g + 1)
                nc.vector.tensor_copy(wT[:, g * 512:(g + 1) * 512], A[0:E, g, :]).then_inc(wT_done, 1)
            for g in range(4):
                cols = slice(g * 512, (g + 1) * 512)
                dve.wait_ge(h_filled, g + 1)
                dve.wait_ge(spread_done, g + 1)
                nc.vector.tensor_tensor(hT[:, cols], C[0:ER, g, :], spread[:, cols], ALU.mult).then_inc(h_done, 1)
            for g in range(4):
                dve.wait_ge(y_filled, g + 1)
                rows_g = XS[:, 4 * g:4 * g + 4, :]
                nc.vector.tensor_tensor(rows_g, rows_g, A[:, g, :].rearrange("p (t d) -> p t d", d=D), ALU.add)\
                  .then_inc(y_added, 1)


def two_layers(nc, x, ctx_1024, L0_xattn_Wq, L0_xattn_Wk, L0_xattn_Wv, L0_xattn_Wo, L0_ffn_gate_weight, L0_ffn_W1,
               L0_ffn_b1, L0_ffn_W2, L0_ffn_b2, L0_ffn_Ws1, L0_ffn_bs1, L0_ffn_Ws2, L0_ffn_bs2, L1_xattn_Wq,
               L1_xattn_bq, L1_xattn_Wk, L1_xattn_bk, L1_xattn_Wv, L1_xattn_bv, L1_xattn_Wr, L1_xattn_br,
               L1_ffn_base_W, L1_ffn_base_b, L1_ffn_shared_A, L1_ffn_shared_B, L1_ffn_routed_A, L1_ffn_routed_B,
               L1_ffn_router_W, L1_ffn_router_b, out):
    with ExitStack() as es:
        XS = es.enter_context(nc.sbuf_tensor("tokens", [P, TILES, D], F32))
        ident = es.enter_context(nc.sbuf_tensor("ident", [P, P], F32))
        attention_0(nc, x, ctx_1024, L0_xattn_Wq, L0_xattn_Wk, L0_xattn_Wv, L0_xattn_Wo, XS, ident)
        moe_0(nc, L0_ffn_gate_weight, L0_ffn_W1, L0_ffn_b1, L0_ffn_W2, L0_ffn_b2, L0_ffn_Ws1, L0_ffn_bs1,
              L0_ffn_Ws2, L0_ffn_bs2, XS, ident)
        attention_1(nc, ctx_1024, L1_xattn_Wq, L1_xattn_bq, L1_xattn_Wk, L1_xattn_bk, L1_xattn_Wv, L1_xattn_bv,
                    L1_xattn_Wr, L1_xattn_br, XS, ident)
        ffn_1(nc, L1_ffn_base_W, L1_ffn_base_b, L1_ffn_shared_A, L1_ffn_shared_B, L1_ffn_routed_A, L1_ffn_routed_B,
              L1_ffn_router_W, L1_ffn_router_b, XS, ident, out)


_INS = ['x', 'ctx_1024', 'L0_xattn_Wq', 'L0_xattn_Wk', 'L0_xattn_Wv', 'L0_xattn_Wo', 'L0_ffn_gate_weight', 'L0_ffn_W1',
        'L0_ffn_b1', 'L0_ffn_W2', 'L0_ffn_b2', 'L0_ffn_Ws1', 'L0_ffn_bs1', 'L0_ffn_Ws2', 'L0_ffn_bs2', 'L1_xattn_Wq',
        'L1_xattn_bq', 'L1_xattn_Wk', 'L1_xattn_bk', 'L1_xattn_Wv', 'L1_xattn_bv', 'L1_xattn_Wr', 'L1_xattn_br',
        'L1_ffn_base_W', 'L1_ffn_base_b', 'L1_ffn_shared_A', 'L1_ffn_shared_B', 'L1_ffn_routed_A', 'L1_ffn_routed_B',
        'L1_ffn_router_W', 'L1_ffn_router_b']
_OUTS = [((B, S, D), 'float32')]


def kernel(**inputs):
    import numpy as _np
    import concourse.bacc as _bacc
    from concourse import mybir as _mybir
    from concourse.bass_utils import run_bass_kernel_spmd as _run

    nc = _bacc.Bacc("TRN2", target_bir_lowering=False, num_devices=1)
    arrays, args = {}, []
    for name in _INS:
        a = _np.ascontiguousarray(inputs[name])
        arrays[f"in_{name}_dram"] = a
        args.append(nc.dram_tensor(f"in_{name}_dram", a.shape, _mybir.dt.from_np(a.dtype), kind="ExternalInput").ap())
    for i, (shape, dtype) in enumerate(_OUTS):
        dt = _mybir.dt.from_np(_np.dtype(dtype))
        args.append(nc.dram_tensor(f"out_{i}_dram", shape, dt, kind="ExternalOutput").ap())
    two_layers(nc, *args)
    r = _run(nc, [arrays], core_ids=[0])
    return r.results[0]["out_0_dram"]
```

```python
import concourse.bass as bass
from concourse import mybir
from contextlib import ExitStack
import math

F32 = mybir.dt.float32
F32R = mybir.dt.float32r
BF16 = mybir.dt.bfloat16
U32 = mybir.dt.uint32
ACT = mybir.ActivationFunctionType
ALU = mybir.AluOpType
AX = mybir.AxisListType

P = 128
B, S, D = 8, 256, 128
N = 1601
H, HD = 16, 64
NC = -(-N // P)
LAST = N - (NC - 1) * P
TILES = B * S // P
MASKED = -1e30
EPS = 1e-5


def at(it, per, first):
    return first if it is None else it * per + first


def f32(ap):
    return ap.bitcast(F32)


def bc(ap, n):
    return ap.unsqueeze(2).to_broadcast([ap.shape[0], ap.shape[1], n])


LN_GROUP = 8


def layer_norm(nc, dve, link, src, out, squares, stats, squared, var_ready, std_ready, ready):
    groups = [slice(t, t + LN_GROUP) for t in range(0, TILES, LN_GROUP)]

    def centre(g):
        mean = stats[:, 0, groups[g]]
        link(nc.vector.tensor_reduce(mean, src[:, groups[g], :], AX.X, ALU.add))
        link(nc.vector.tensor_scalar(mean, mean, 1.0 / D, None, ALU.mult))
        nc.vector.tensor_tensor(out[:, groups[g], :], src[:, groups[g], :], bc(mean, D), ALU.subtract)\
          .then_inc(squared[0], 1)

    def variance(g):
        var = stats[:, 1, groups[g]]
        dve.wait_ge(squared[1], g + 1)
        link(nc.vector.tensor_reduce(var, squares[:, groups[g], :], AX.X, ALU.add))
        nc.vector.tensor_scalar(var, var, 1.0 / D, EPS, ALU.mult, ALU.add).then_inc(var_ready, 1)

    def scale(g):
        var = stats[:, 1, groups[g]]
        dve.wait_ge(std_ready, g + 1)
        link(nc.vector.reciprocal(var, var))
        dve.wait_ge(squared[0], g + 1)
        nc.vector.tensor_tensor(out[:, groups[g], :], out[:, groups[g], :], bc(var, D), ALU.mult).then_inc(ready, 1)

    n = len(groups)
    for g in range(n + 2):
        if g < n:
            centre(g)
        if 0 <= g - 1 < n:
            variance(g - 1)
        if 0 <= g - 2:
            scale(g - 2)


def layer_norm_on_scalar(nc, act, out, squares, stats, squared, var_ready, std_ready):
    n = TILES // LN_GROUP
    for g in range(n + 1):
        if g < n:
            tiles = slice(g * LN_GROUP, (g + 1) * LN_GROUP)
            act.wait_ge(squared[0], g + 1)
            nc.scalar.activation(squares[:, tiles, :], out[:, tiles, :], ACT.Square).then_inc(squared[1], 1)
        if g >= 1:
            tiles = slice((g - 1) * LN_GROUP, g * LN_GROUP)
            act.wait_ge(var_ready, g)
            nc.scalar.activation(stats[:, 1, tiles], stats[:, 1, tiles], ACT.Sqrt).then_inc(std_ready, 1)


def attention_0(nc, x, ctx_in, wq, wk, wv, wo, XS, ident):
    G8 = H // 2
    STEPS = 2 * NC
    SLOTS = 4 * STEPS
    STAGES = 2 * B
    PIECES = [(0, 402), (402, 400), (802, 400), (1202, 400)]
    UNITS = G8 * 2

    BANKS = 4
    TAIL = 3
    V_AFTER = [1, 4, 6, 8, 10, 12, 14, 26, 38]
    LATE_V = [95, 97, 100, 102]
    MAX_END = 92
    SHIFTS = [83, 93]
    DIAG = [84, 88]
    SPREAD = [92, 93, 98, 99]
    RECIP = range(8, 24, 2)
    NORM_STEP = 6
    PROJ = 34

    def prep_slots(group):
        early = []
        if group == 0:
            early += [("cT", i) for i in range(3)] + [("cxT", 3)] + [("mask", i) for i in range(4)]
        early += [("q", i) for i in range(4)]
        vs = [("v", c) for c in range(NC)]
        for u in range(UNITS * 4):
            early.append(("max", u))
            if u in V_AFTER:
                early.append(vs.pop(0))
        slots = [[] for _ in range(SLOTS)]
        for n, item in enumerate(early):
            slots[n * MAX_END // len(early)].append(item)
        for i in range(2):
            slots[SHIFTS[i]].append(("shift", i))
        for i in range(2):
            slots[DIAG[i]].append(("diag", i))
        for i in range(4):
            slots[SPREAD[i]].append(("spread", i))
        assert len(vs) == len(LATE_V)
        for n, item in zip(LATE_V, vs):
            slots[n].append(item)
        return slots

    CONTEXT_ITEMS = 4
    PREP = [sum(map(len, prep_slots(g))) - 4 for g in range(2)]

    def first_use(c):
        n = PREP[0]
        for s in range(c):
            n += (TAIL if s else 0) + (PREP[(s + 1) % 2] if s + 1 < STAGES else 0)
        return n

    PER_TURN = first_use(5) - first_use(1)
    assert PER_TURN % BANKS == 0

    def numbered(slots, use):
        out = []
        for slot in slots:
            row = []
            for kind, i in slot:
                takes = kind not in ("recip", "shift", "diag")
                row.append((kind, i, use if takes else None))
                use += takes
            out.append(row)
        return out

    def plan(c, tail, prep):
        slots = [[] for _ in range(SLOTS)]
        if tail:
            slots[3].append(("den", 0))
            slots[7].append(("den", 1))
            for i in range(8):
                slots[RECIP[i]].append(("recip", i))
            slots[PROJ].append(("proj", 0))
        if prep:
            slots = [a + b for a, b in zip(slots, prep_slots((c + 1) % 2))]
        return numbered(slots, first_use(c))

    with ExitStack() as es:
        def sb(name, shape, dt=F32):
            return es.enter_context(nc.sbuf_tensor("a_" + name, shape, dt))

        def sem(name):
            return es.enter_context(nc.semaphore("a_" + name))

        c_nat = sb("c_nat", [P, NC, D])
        cT = [[sb(f"cT_{part}{i}", [P, NC * P], F32R) for part in ("hi", "lo")] for i in range(2)]
        V = sb("V", [P, 2, NC, G8 * HD])
        Q = [[sb(f"Q_{part}{i}", [P, G8 * S], F32R) for part in ("hi", "lo")] for i in range(2)]
        shift_diag = sb("shift_diag", [P, UNITS // 2, P], F32R)
        shift = sb("shift", [P, G8 * S])
        probs = sb("probs", [P, 4, 4 * S])
        den = sb("den", [P, G8 * S])
        G = [sb("G_hi", [P, H, D], F32R), sb("G_lo", [P, H, D], F32R)]
        Wv = [sb("Wv_hi", [P, H * HD], F32R), sb("Wv_lo", [P, H * HD], F32R)]
        Wo = sb("Wo", [P, H // 2, D])
        mask_row = sb("mask_row", [P, NC * P], BF16)
        c_flag = mask_row
        mask_col = sb("mask_col", [P, 2, NC])
        acc = sb("acc", [P, 2, 2, D])
        xn_b = sb("xn_b", [P, 2, D])
        xnT = [sb("xnT_hi", [P, S], F32R), sb("xnT_lo", [P, S], F32R)]
        outT = sb("outT", [P, 4 * S])
        rden = sb("rden", [P, 4 * S])
        maxes = sb("maxes", [P, 2, UNITS * 4])
        neg_max = sb("neg_max", [P, 2, UNITS])
        stats = sb("stats", [P, 2, TILES])
        c_largest = sb("c_largest", [P, NC])
        ones = sb("ones", [P, HD])
        ones_b = sb("ones_b", [P, P], BF16)
        ones_r = sb("ones_r", [P, P], F32R)
        raw = [V[:, 1, :, :].rearrange("p c n -> p (c n)")[:, i * 1024:(i + 1) * 1024] for i in range(6)]
        wq_raw, wk_raw, wv_raw, wk_heads, wqT, wkT = raw
        squares = probs[:, 0:2, :].rearrange("p a (t d) -> p (a t) d", d=D)

        Sc = es.enter_context(nc.psum_tensor("a_scores", [P, 2, 2 * S], F32))
        PV = es.enter_context(nc.psum_tensor("a_pv", [P, 4 * S], F32))
        X = es.enter_context(nc.psum_tensor("a_work", [P, BANKS, 512], F32))
        setup_psum = [Sc[:, :, :].rearrange("p a n -> p (a n)"), PV[:, :]]

        x_loaded, w_loaded, c_loaded = sem("x_loaded"), sem("w_loaded"), sem("c_loaded")
        res_loaded = sem("res_loaded")
        consts, ones_ready = sem("consts"), sem("ones_ready")
        dve_chain = sem("dve_chain")
        squared = [sem("centred_groups"), sem("squared_groups")]
        var_ready, std_ready = sem("var_ready"), sem("std_ready")
        wk_ready = sem("wk_ready")
        wT_filled, wT_copied = sem("wT_filled"), sem("wT_copied")
        G_filled, G_hi_done, G_ready = sem("G_filled"), sem("G_hi_done"), sem("G_ready")
        xn_all, wv_ready = sem("xn_all"), sem("wv_ready")
        bank_full = [sem(f"bank{i}_full") for i in range(BANKS)]
        bank_free = [sem(f"bank{i}_free") for i in range(BANKS)]
        hi_done = sem("hi_done")
        flag_done = sem("flag_done")
        col_done = sem("col_done")
        xn_ready = sem("xn_ready")
        shift_steps = sem("shift_steps")
        diag_done = sem("diag_done")
        scores_done, shifted = sem("scores_done"), sem("shifted")
        probs_done, pv_done = sem("probs_done"), sem("pv_done")
        pv_free = sem("pv_free")
        den_added = sem("den_added")
        recip_done, norm_done = sem("recip_done"), sem("norm_done")
        block = es.enter_context(nc.Block())

        def filled(eng, it, use):
            eng.wait_ge(bank_full[use % BANKS], at(it, PER_TURN // BANKS, use // BANKS + 1))

        def taken(eng, it, use):
            eng.wait_ge(bank_free[use % BANKS], at(it, PER_TURN // BANKS, use // BANKS + 1))

        def stages(eng, body):
            body(None, 0)
            with eng.Fori(0, 3) as it:
                for c in range(1, 5):
                    body(it, c)
            for c in range(13, STAGES):
                body(None, c)

        def steps_of(it, c, first):
            return at(it, 4 * STEPS, c * STEPS + first)

        def shifts_of(it, c, j, pair):
            return at(it, 8 * STEPS, 2 * (c * STEPS + j) + pair)

        def flags(it, c):
            return c > 0 or it is not None, it is not None or c + 1 < STAGES

        def use_of(slots, kind, index):
            return [use for slot in slots for k, i, use in slot if (k, i) == (kind, index)][0]

        def the_plan(it, c):
            return plan(c, *flags(it, c))

        def prologue_items():
            return [item for slot in numbered(prep_slots(0), 0) for item in slot]

        def prep_use(it, c, kind, index):
            return use_of([prologue_items()] if c < 0 else the_plan(it, c), kind, index)

        def buffer(c, j):
            return (c * STEPS + j) % 4

        @block.sync
        def _(sp):
            sp.dma_start(XS[:, :, :], x.rearrange("b (j p) d -> p (b j) d", p=P)).then_inc(x_loaded, 16)
            sp.dma_start(wq_raw, wq).then_inc(w_loaded, 16)
            sp.dma_start(wk_raw, wk).then_inc(w_loaded, 16)
            sp.dma_start(wv_raw, wv).then_inc(w_loaded, 16)
            sp.dma_start(Wo[:, :, :], wo.rearrange("(g p) n -> p g n", p=P)).then_inc(w_loaded, 16)
            sp.wait_ge(consts, 2)

            def load_context(b):
                sp.dma_start(c_nat[:, 0:NC - 1, :],
                             ctx_in[b, 0:(NC - 1) * P, :].rearrange("(c p) d -> p c d", p=P)).then_inc(c_loaded, 16)
                sp.dma_start(c_nat[0:LAST, NC - 1, :], ctx_in[b, (NC - 1) * P:N, :]).then_inc(c_loaded, 16)

            def load_residual(b, parity):
                sp.dma_start(acc[:, parity, :, :],
                             x[b, :, :].rearrange("(j p) d -> p j d", p=P)).then_inc(res_loaded, 16)

            load_context(0)
            load_residual(0, 0)

            def body(it, c):
                if c % 2 == 0 and (it is not None or c < STAGES - 2):
                    transposed, scanned = at(it, 26, c // 2 * 13 + 4), at(it, 4, c // 2 * 2 + 1)
                    sp.wait_ge(hi_done, transposed)
                    sp.nop(nofuse=True)
                    sp.wait_ge(col_done, scanned)
                    load_context(at(it, 2, c // 2 + 1))
                    if c > 0:
                        taken(sp, it, use_of(the_plan(it, c), "proj", 0))
                    load_residual(at(it, 2, c // 2 + 1), (c // 2 + 1) % 2)

            stages(sp, body)

        @block.gpsimd
        def _(pool):
            nc.gpsimd.memset(ident[:, :], 0.0).then_inc(consts, 1)
            nc.gpsimd.memset(c_nat[:, NC - 1, :], 0.0).then_inc(consts, 1)
            nc.gpsimd.memset(ones[:, :], 1.0).then_inc(consts, 1)
            nc.gpsimd.memset(ones_b[:, :], 1.0).then_inc(consts, 1)
            pool.wait_ge(consts, 4)
            nc.gpsimd.affine_select(out=ident[:, :], in_=ident[:, :], compare_op=ALU.not_equal, fill=1.0,
                                    base=0, pattern=[[-1, P]], channel_multiplier=1).then_inc(consts, 1)

            def normalise(it, c):
                pool.wait_ge(recip_done, at(it, 32, 8 * c))
                pool.wait_ge(pv_free, at(it, 8, 2 * c))
                nc.gpsimd.tensor_tensor(outT[:, :], outT[:, :], rden[:, :], ALU.mult).then_inc(norm_done, 1)

            def body(it, c):
                for j in range(2, STEPS):
                    half = den[:, (j % 2) * 4 * S:(j % 2 + 1) * 4 * S]
                    if j < 4:
                        so_far = probs[:, buffer(c, j - 2), :]
                        if c > 0:
                            filled(pool, it, use_of(the_plan(it, c), "den", j - 2))
                    else:
                        so_far = half
                        pool.wait_ge(den_added, at(it, 4 * (STEPS - 2), c * (STEPS - 2) + j - 3))
                    pool.wait_ge(probs_done, steps_of(it, c, j + 1))
                    nc.gpsimd.tensor_tensor(half, so_far, probs[:, buffer(c, j), :], ALU.add).then_inc(den_added, 1)
                    if c > 0 and j == NORM_STEP:
                        normalise(it, c)

            stages(pool, body)
            normalise(None, STAGES)

        @block.tensor
        def _(pe):
            pe.wait_ge(consts, 5)
            pe.wait_ge(w_loaded, 64)
            for g in range(H // 2):
                nc.tensor.transpose(setup_psum[0][:, g * P:(g + 1) * P], wq_raw[:, g * P:(g + 1) * P], ident[:, :])
            pe.wait_ge(wk_ready, 1)
            for g in range(H // 2):
                last = nc.tensor.transpose(setup_psum[1][:, g * P:(g + 1) * P], wk_heads[:, g * P:(g + 1) * P],
                                           ident[:, :])
            last.then_inc(wT_filled, 1)

            def split_product(out, a, b, cols_a, cols_b):
                nc.tensor.matmul(out, a[0][:, cols_a], b[0][:, cols_b], start=True, stop=False)
                nc.tensor.matmul(out, a[0][:, cols_a], b[1][:, cols_b], start=False, stop=False)
                return nc.tensor.matmul(out, a[1][:, cols_a], b[0][:, cols_b], start=False, stop=True)

            def item(it, c, kind, i, use):
                bank, s = use % BANKS, c + 1
                if use >= BANKS:
                    taken(pe, it, use - BANKS)
                out = X[:, bank, :]
                if kind in ("cT", "cxT"):
                    pe.wait_ge(c_loaded, at(it, 64, 32 * (s // 2 + 1)))
                    for ch in range(4 * i, min(4 * i + 4, NC)):
                        last = nc.tensor.transpose(out[:, ch % 4 * P:(ch % 4 + 1) * P], c_nat[:, ch, :], ident[:, :])
                    if kind == "cxT":
                        pe.wait_ge(xn_ready, at(it, 2, s // 2 + 1))
                        for j in range(2):
                            last = nc.tensor.transpose(out[:, (j + 1) * P:(j + 2) * P], xn_b[:, j, :], ident[:, :])
                elif kind == "mask":
                    pe.wait_ge(flag_done, at(it, 8, s // 2 * 4 + i + 1))
                    off, w = PIECES[i]
                    last = nc.tensor.matmul(out[:, :w], ones_b[:, :], c_flag[:, off:off + w], start=True, stop=True)
                elif kind == "q":
                    for k in range(2):
                        h = s % 2 * G8 + 2 * i + k
                        last = split_product(out[:, k * S:(k + 1) * S], [g[:, h, :] for g in G], xnT,
                                             slice(0, D), slice(0, S))
                elif kind == "v":
                    last = split_product(out, cT[s // 2 % 2], Wv, slice(i * P, (i + 1) * P),
                                         slice(s % 2 * G8 * HD, (s % 2 + 1) * G8 * HD))
                elif kind == "max":
                    off, w = PIECES[i % 4]
                    last = nc.tensor.matmul(out[:, :w], Q[s % 2][0][:, i // 4 * P:(i // 4 + 1) * P],
                                            cT[s // 2 % 2][0][:, off:off + w], start=True, stop=True)
                elif kind == "spread":
                    if i < 2:
                        pe.wait_ge(diag_done, at(it, 32, 8 * s + 4 * (i + 1)))
                    else:
                        pe.wait_ge(shift_steps, at(it, 20, 5 * s + 5))
                    last = nc.tensor.matmul(out, ones_r[:, :], shift_diag[:, i % 2 * 4:i % 2 * 4 + 4, :], start=True, stop=True)
                elif kind == "den":
                    pe.wait_ge(den_added, at(it, 4 * (STEPS - 2), c * (STEPS - 2) - 1 + i))
                    for k in range(2):
                        for odd in range(2):
                            h = 4 * i + 2 * k + odd
                            last = nc.tensor.matmul(out[HD * odd:HD * odd + HD, k * S:(k + 1) * S], ones[:, :],
                                                    den[:, h * S:(h + 1) * S], start=True, stop=True)
                elif kind == "proj":
                    pe.wait_ge(norm_done, at(it, 4, c))
                    for j in range(2):
                        for g in range(4):
                            last = nc.tensor.matmul(out[:, j * D:(j + 1) * D],
                                                    outT[:, g * S + j * P:g * S + (j + 1) * P],
                                                    Wo[:, (c - 1) % 2 * 4 + g, :], start=(g == 0), stop=(g == 3))
                last.then_inc(bank_full[bank], 1)

            def qk(it, c, j, pair):
                if c > 0 or j > 0:
                    pe.wait_ge(shifted, shifts_of(it, c, j - 1, pair + 1))
                first = (j % 2 * 4 + pair * 2)
                split_product(Sc[:, pair, :], cT[c // 2 % 2], Q[c % 2],
                              slice(j // 2 * P, (j // 2 + 1) * P), slice(first * S, (first + 2) * S))\
                    .then_inc(scores_done, 1)

            def pv(it, c, j, pair):
                if pair == 0:
                    pe.wait_ge(probs_done, steps_of(it, c, j + 1))
                    if j < 2 and c > 0:
                        pe.wait_ge(pv_free, at(it, 8, 2 * c - 1 + j))
                    if j == 2 * (NC - BANKS):
                        for use in range(first_use(c) - BANKS, first_use(c)):
                            taken(pe, it, use)
                for odd in range(2):
                    h = j % 2 * 4 + pair * 2 + odd
                    cols = (j % 2 * 2 + pair) * S
                    last = nc.tensor.matmul(PV[HD * odd:HD * odd + HD, cols:cols + S],
                                            V[:, c % 2, j // 2, h * HD:(h + 1) * HD],
                                            probs[:, buffer(c, j), (pair * 2 + odd) * S:(pair * 2 + odd + 1) * S],
                                            start=(j < 2 and pair == 0), stop=(j >= STEPS - 2), skip_group_check=True)
                if pair == 1:
                    last.then_inc(pv_done, 1)

            def body(it, c):
                tail, prep = flags(it, c)
                slots = the_plan(it, c)
                for j in range(STEPS):
                    for part in range(4):
                        if part == 1:
                            pv(it, c, j, 0)
                            pv(it, c, j, 1)
                        elif part > 1 and j + 2 < STEPS:
                            qk(it, c, j + 2, part - 2)
                        elif part > 1 and prep:
                            qk(it, c + 1, j + 2 - STEPS, part - 2)
                        for kind, i, use in slots[4 * j + part]:
                            if use is not None:
                                item(it, c, kind, i, use)

            for kind, i, use in prologue_items()[:CONTEXT_ITEMS]:
                item(None, -1, kind, i, use)
            pe.wait_ge(wT_copied, 2)
            for g in range(H // 2):
                for odd in range(2):
                    rows = slice(HD * odd, HD * odd + HD)
                    last = nc.tensor.matmul(setup_psum[odd][:, g * P:(g + 1) * P], wqT[rows, g * P:(g + 1) * P],
                                            wkT[rows, g * P:(g + 1) * P], start=True, stop=True)
            last.then_inc(G_filled, 1)
            pe.wait_ge(G_ready, 2)
            pe.wait_ge(ones_ready, 1)
            pe.wait_ge(wv_ready, 1)
            for kind, i, use in prologue_items()[CONTEXT_ITEMS:]:
                if use is not None:
                    item(None, -1, kind, i, use)
            for j in range(2):
                for pair in range(2):
                    qk(None, 0, j, pair)
            stages(pe, body)
            for n, kind in enumerate(("den", "den", "proj")):
                item(None, STAGES, kind, n % 2, first_use(STAGES) + n)

        @block.scalar
        def _(act):
            layer_norm_on_scalar(nc, act, XS, squares, stats, squared, var_ready, std_ready)
            act.wait_ge(wT_filled, 1)
            nc.scalar.activation(wqT, setup_psum[0], ACT.Copy).then_inc(wT_copied, 1)

            def item(it, c, kind, i, use):
                bank, s = None if use is None else use % BANKS, c + 1
                if kind == "diag":
                    act.wait_ge(shift_steps, at(it, 20, 5 * s + 2))
                    for u in range(4 * i, 4 * i + 4):
                        nc.scalar.activation(shift_diag[:, u, :], ident[:, :], ACT.Copy,
                                             scale=neg_max[:, s % 2, u:u + 1]).then_inc(diag_done, 1)
                if kind not in ("cT", "cxT", "q", "v", "spread", "den"):
                    return
                if kind == "den" and (c > 1 or it is not None):
                    act.wait_ge(norm_done, at(it, 4, c - 1))
                filled(act, it, use)
                if kind in ("cT", "cxT"):
                    w = min(4, NC - 4 * i) * P
                    nc.scalar.activation(cT[s // 2 % 2][0][:, i * 512:i * 512 + w], X[:, bank, :w], ACT.Copy)\
                      .then_inc(hi_done, 1)
                    if kind == "cxT":
                        nc.scalar.activation(xnT[0][:, :], X[:, bank, w:w + S], ACT.Copy).then_inc(hi_done, 1)
                elif kind == "q":
                    nc.scalar.activation(Q[s % 2][0][:, i * 512:(i + 1) * 512], X[:, bank, :], ACT.Copy)\
                      .then_inc(hi_done, 1)
                elif kind == "v":
                    nc.scalar.activation(V[:, s % 2, i, :], X[:, bank, :], ACT.Copy).then_inc(bank_free[bank], 1)
                elif kind == "spread":
                    if c >= 0:
                        act.wait_ge(shifted, shifts_of(it, c, STEPS - 2 + i // 2, i % 2 + 1))
                    nc.scalar.activation(shift[:, i * 512:(i + 1) * 512], X[:, bank, :], ACT.Copy)\
                      .then_inc(bank_free[bank], 1)
                elif kind == "den":
                    nc.scalar.activation(rden[:, i * 512:(i + 1) * 512], X[:, bank, :], ACT.Copy)\
                      .then_inc(bank_free[bank], 1)

            def exp(it, c, j):
                act.wait_ge(shifted, shifts_of(it, c, j, 2))
                if j == 0:
                    act.wait_ge(col_done, at(it, 4, 2 * (c // 2) + 2))
                nc.scalar.activation(probs[:, buffer(c, j), :], probs[:, buffer(c, j), :], ACT.Exp,
                                     bias=mask_col[:, c // 2 % 2, j // 2:j // 2 + 1]).then_inc(probs_done, 1)

            def copy_outT(it, c, bank):
                act.wait_ge(pv_done, steps_of(it, c, bank - 1))
                nc.scalar.activation(outT[:, bank * 512:(bank + 1) * 512], PV[:, bank * 512:(bank + 1) * 512], ACT.Copy)\
                  .then_inc(pv_free, 1)

            def body(it, c):
                tail, prep = flags(it, c)
                slots = the_plan(it, c)
                for j in range(STEPS):
                    if tail and j == 0:
                        copy_outT(it, c, 0)
                        copy_outT(it, c, 1)
                    if j + 1 < STEPS:
                        exp(it, c, j + 1)
                    elif prep:
                        exp(it, c + 1, 0)
                    for slot in slots[4 * j:4 * j + 4]:
                        for kind, i, use in slot:
                            item(it, c, kind, i, use)

            for kind, i, use in prologue_items()[:CONTEXT_ITEMS]:
                item(None, -1, kind, i, use)
            act.wait_ge(G_filled, 1)
            for odd in range(2):
                heads = G[0].rearrange("p (g two) d -> p two g d", two=2)[:, odd, :, :]
                nc.scalar.activation(heads, setup_psum[odd].rearrange("p (g d) -> p g d", d=D), ACT.Copy,
                                     scale=HD ** -0.5).then_inc(G_hi_done, 1)
            for kind, i, use in prologue_items()[CONTEXT_ITEMS:]:
                item(None, -1, kind, i, use)
            exp(None, 0, 0)
            stages(act, body)
            copy_outT(None, STAGES, 0)
            copy_outT(None, STAGES, 1)
            for i in range(2):
                item(None, STAGES, "den", i, first_use(STAGES) + i)

        @block.vector
        def _(dve):
            chain = [0]

            def link(ins):
                chain[0] += 1
                ins.then_inc(dve_chain, 1)
                dve.wait_ge(dve_chain, chain[0])

            dve.wait_ge(x_loaded, 16)
            layer_norm(nc, dve, link, XS, XS, squares, stats, squared, var_ready, std_ready, xn_all)
            dve.wait_ge(w_loaded, 64)
            nc.vector.tensor_copy(wk_heads.rearrange("p (h e) -> p h e", h=H),
                                  wk_raw.rearrange("p (e h) -> p h e", h=H)).then_inc(wk_ready, 1)
            wv_heads = wv_raw.rearrange("p (e h) -> p h e", h=H)
            link(nc.vector.tensor_copy(Wv[0].rearrange("p (h e) -> p h e", h=H), wv_heads))
            nc.vector.tensor_tensor(Wv[1].rearrange("p (h e) -> p h e", h=H), wv_heads,
                                    f32(Wv[0][:, :]).rearrange("p (h e) -> p h e", h=H), ALU.subtract)\
              .then_inc(wv_ready, 1)
            dve.wait_ge(consts, 5)
            nc.vector.tensor_copy(ones_r[:, :], ones_b[:, :]).then_inc(ones_ready, 1)
            dve.wait_ge(wT_filled, 1)
            nc.vector.tensor_copy(wkT, setup_psum[1]).then_inc(wT_copied, 1)
            dve.wait_ge(xn_all, TILES // LN_GROUP)

            def low_part(it, out, hi, psum, done):
                dve.wait_ge(hi_done, at(it, 26, done))
                return nc.vector.tensor_tensor(out, psum, f32(hi), ALU.subtract)

            def item(it, c, kind, i, use):
                s = c + 1
                b, pb = s // 2, s // 2 % 2
                bank = None if use is None else use % BANKS
                if kind in ("cT", "cxT"):
                    if i == 0:
                        filled(dve, it, use)
                        nc.vector.tensor_reduce(c_largest[:, :], c_nat[:, :, :], AX.X, ALU.max,
                                                apply_absolute_value=True).then_inc(col_done, 1)
                        nc.vector.tensor_copy(xn_b[:, :, :], XS[:, bass.ds(at(it, 4, 2 * b), 2), :])\
                          .then_inc(xn_ready, 1)
                        dve.wait_ge(col_done, at(it, 4, 2 * b + 1))
                        nc.vector.tensor_scalar(mask_col[:, pb, :], c_largest[:, :], 0.0, MASKED,
                                                ALU.is_equal, ALU.mult).then_inc(col_done, 1)
                    w = min(4, NC - 4 * i) * P
                    cols = slice(i * 512, i * 512 + w)
                    last = low_part(it, cT[pb][1][:, cols], cT[pb][0][:, cols],
                                    X[:, bank, :w], 13 * b + i + (2 if kind == "cxT" else 1))
                    if kind == "cxT":
                        last = low_part(it, xnT[1][:, :], xnT[0][:, :], X[:, bank, w:w + S], 13 * b + 5)
                    last.then_inc(bank_free[bank], 1)
                    nc.vector.tensor_scalar(c_flag[:, cols], f32(cT[pb][0][:, cols]), 0.0, None, ALU.not_equal)\
                      .then_inc(flag_done, 1)
                elif kind == "mask":
                    off, w = PIECES[i]
                    filled(dve, it, use)
                    nc.vector.tensor_scalar(mask_row[:, off:off + w], X[:, bank, :w], 0.0, MASKED,
                                            ALU.is_equal, ALU.mult).then_inc(bank_free[bank], 1)
                elif kind == "q":
                    cols = slice(i * 512, (i + 1) * 512)
                    low_part(it, Q[s % 2][1][:, cols], Q[s % 2][0][:, cols], X[:, bank, :],
                             13 * b + (9 if s % 2 else 5) + i + 1).then_inc(bank_free[bank], 1)
                elif kind == "max":
                    off, w = PIECES[i % 4]
                    filled(dve, it, use)
                    dve.nop(nofuse=True)
                    nc.vector.tensor_tensor_reduce(out=X[:, bank, :w], in0=X[:, bank, :w],
                                                   in1=mask_row[:, off:off + w], scale=1.0, scalar=-3e38,
                                                   op0=ALU.add, op1=ALU.max, accum_out=maxes[:, s % 2, i:i + 1])\
                      .then_inc(bank_free[bank], 1)
                elif kind == "shift":
                    half = UNITS // 2
                    units = slice(i * half, (i + 1) * half)
                    uses = [prep_use(it, c, "max", m) for m in range(4 * half * i, 4 * half * (i + 1))]
                    for use in [max(u for u in uses if u % BANKS == k) for k in range(BANKS)]:
                        taken(dve, it, use)
                    nc.vector.tensor_reduce(neg_max[:, s % 2, units],
                                            maxes[:, s % 2, :].rearrange("p (u k) -> p u k", k=4)[:, units, :],
                                            AX.X, ALU.max, negate=True).then_inc(shift_steps, 1)
                    dve.wait_ge(shift_steps, at(it, 20, 5 * s + 2 * i + 1))
                    nc.vector.tensor_scalar(neg_max[:, s % 2, units], neg_max[:, s % 2, units], 1e20, None, ALU.min)\
                      .then_inc(shift_steps, 1)
                    if i == 1:
                        dve.wait_ge(shift_steps, at(it, 20, 5 * s + 4))
                        for quarter in range(2):
                            filled(dve, it, prep_use(it, c, "spread", quarter))
                        nc.vector.tensor_tensor(shift_diag[:, :, :],
                                                ident[:, :].unsqueeze(1).to_broadcast([P, half, P]),
                                                bc(neg_max[:, s % 2, units], P), ALU.mult).then_inc(shift_steps, 1)
                elif kind == "recip":
                    if i % 4 == 0:
                        taken(dve, it, use_of(the_plan(it, c), "den", i // 4))
                    part = rden[:, i * P:(i + 1) * P]
                    nc.vector.reciprocal(part, part).then_inc(recip_done, 1)
                elif kind == "proj":
                    filled(dve, it, use)
                    pb = (c - 1) // 2 % 2
                    psum = X[:, bank, :2 * D].rearrange("p (j d) -> p j d", d=D)
                    if (c - 1) % 2 == 0:
                        dve.wait_ge(res_loaded, at(it, 32, 16 * ((c - 1) // 2 + 1)))
                        out = acc[:, pb, :, :]
                    else:
                        taken(dve, it, use_of(the_plan(it, c - 1), "proj", 0))
                        out = XS[:, bass.ds(at(it, 4, 2 * ((c - 1) // 2)), 2), :]
                    nc.vector.tensor_tensor(out, acc[:, pb, :, :], psum, ALU.add).then_inc(bank_free[bank], 1)

            def subtract(it, c, j, pair):
                dve.wait_ge(scores_done, shifts_of(it, c, j, pair + 1))
                if pair == 0:
                    if j < 2:
                        for quarter in (2 * j, 2 * j + 1):
                            taken(dve, it, prep_use(it, c - 1, "spread", quarter))
                    if c > 0 or j > 3:
                        dve.wait_ge(pv_done, steps_of(it, c, j - 3))
                        added = 1 if j == 4 else 2 if j == 5 else j - 5 if j > 5 else j - 3
                        dve.wait_ge(den_added, at(it, 4 * (STEPS - 2), c * (STEPS - 2) + added))
                first = (j % 2 * 4 + pair * 2) * S
                nc.vector.tensor_tensor(probs[:, buffer(c, j), pair * 2 * S:(pair + 1) * 2 * S],
                                        Sc[:, pair, :],
                                        shift[:, first:first + 2 * S], ALU.add).then_inc(shifted, 1)

            def body(it, c):
                tail, prep = flags(it, c)
                slots = the_plan(it, c)
                for n in range(SLOTS):
                    j, part = n // 4, n % 4
                    if part >= 2:
                        if j + 2 < STEPS:
                            subtract(it, c, j + 2, part - 2)
                        elif prep:
                            subtract(it, c + 1, j + 2 - STEPS, part - 2)
                    for kind, i, use in slots[n]:
                        item(it, c, kind, i, use)

            for kind, i, use in prologue_items()[:CONTEXT_ITEMS]:
                item(None, -1, kind, i, use)
            for odd in range(2):
                dve.wait_ge(G_hi_done, odd + 1)
                hi, lo = [g.rearrange("p (g two) d -> p two g d", two=2)[:, odd, :, :] for g in
                          (f32(G[0][:, :, :]), G[1][:, :, :])]
                nc.vector.scalar_tensor_tensor(out=lo, in0=setup_psum[odd].rearrange("p (g d) -> p g d", d=D),
                                               scalar=HD ** -0.5, in1=hi, op0=ALU.mult, op1=ALU.subtract)\
                  .then_inc(G_ready, 1)
            for kind, i, use in prologue_items()[CONTEXT_ITEMS:]:
                item(None, -1, kind, i, use)
            for j in range(2):
                for pair in range(2):
                    subtract(None, 0, j, pair)
            stages(dve, body)
            last = first_use(STAGES)
            taken(dve, None, last)
            taken(dve, None, last + 1)
            for i in range(8):
                part = rden[:, i * P:(i + 1) * P]
                nc.vector.reciprocal(part, part).then_inc(recip_done, 1)
            item(None, STAGES, "proj", 0, last + 2)


def moe_0(nc, gate_w, w1, b1, w2, b2, ws1, bs1, ws2, bs2, XS, ident):
    E, F = w1.shape[0], w1.shape[2]
    T = B * S
    TOPK = T * 2
    FC = F // P
    TG = T // 512
    STEPS = FC * TG
    LAG = 3
    SPLITS = [2, 6]
    ROUNDS = 15
    ROWS = FC * (E + 1) + (E + 1) + E
    B2, GW = FC * (E + 1), FC * (E + 1) + E + 1

    with ExitStack() as es:
        def sb(name, shape, dt=F32):
            return es.enter_context(nc.sbuf_tensor("m_" + name, shape, dt))

        def sem(name):
            return es.enter_context(nc.semaphore("m_" + name))

        xn = sb("xn", [P, TILES, D])
        squares = sb("squares", [P, TILES, D])
        stats = sb("stats", [P, 2, TILES])
        xT = [sb("xT_hi", [P, T], F32R), sb("xT_lo", [P, T], F32R)]
        small = sb("small", [ROWS, D])
        smallT = sb("smallT", [P, ROWS])
        gwT = [sb("gwT_hi", [P, E], F32R), sb("gwT_lo", [P, E], F32R)]
        logits = sb("logits", [P, TILES, E])
        top = sb("top", [P, 2, TILES])
        scores = sb("scores", [P, E, TILES])
        bit_steps = sb("bit_steps", [P, ROUNDS, 3], U32)
        found = sb("found", [P, 1], U32)
        found_bits = sb("found_bits", [P, 1], U32)
        candidates = sb("candidates", [P, 3], U32)
        above = sb("above", [P, 3], BF16)
        passed = sb("passed", [P, 3])
        n_passed = sb("n_passed", [P, 1])
        junk = sb("junk", [P, 3, E * TILES], BF16)
        greater = sb("greater", [P, E * TILES])
        n_greater = sb("n_greater", [P, 1], BF16)
        n_greater_all = sb("n_greater_all", [P, 1])
        equal = sb("equal", [P, E * TILES], BF16)
        zeros = sb("zeros", [P, E * TILES])
        rank = sb("rank", [P, E * TILES])
        gate = sb("gate", [P, E * TILES])
        gateT = sb("gateT", [P, P])
        ones_b = sb("ones_b", [P, P], BF16)
        before = sb("before", [P, P], BF16)
        gate_rows = sb("gate_rows", [P, 2, T])
        w1_raw = sb("w1_raw", [P, 2, F])
        w2_raw = sb("w2_raw", [P, 2, F])
        W1 = [[sb(f"W1_{part}{i}", [P, F], F32R) for part in ("hi", "lo")] for i in range(2)]
        W2 = [[sb(f"W2_{part}{i}", [P, F], F32R) for part in ("hi", "lo")] for i in range(2)]
        h = sb("h", [P, 4, 512])
        h_hi = sb("h_hi", [P, 4, 512], F32R)
        h_lo = sb("h_lo", [P, 4, 512], F32R)
        gated = sb("gated", [P, 2, 512])
        acc = sb("acc", [P, T])
        gate_dram = nc.dram_tensor("gate_scratch", [P, P], F32, kind="Internal").ap()

        U = es.enter_context(nc.psum_tensor("m_up", [P, 4, 512], F32))
        Y = es.enter_context(nc.psum_tensor("m_y", [P, 2, 512], F32))
        R = es.enter_context(nc.psum_tensor("m_route", [P, 2, 512], F32))

        small_loaded, w_loaded = sem("small_loaded"), [sem("w_loaded0"), sem("w_loaded1")]
        consts = sem("consts")
        dve_chain = sem("dve_chain")
        squared = [sem("centred_groups"), sem("squared_groups")]
        var_ready, std_ready, xn_ready = sem("var_ready"), sem("std_ready"), sem("xn_ready")
        xT_filled, xT_hi_done, xT_done = sem("xT_filled"), sem("xT_hi_done"), sem("xT_done")
        small_filled, small_done = sem("small_filled"), sem("small_done")
        logits_filled, centred, exped = sem("logits_filled"), sem("centred"), sem("exped")
        counted, summed = sem("counted"), sem("summed")
        ties_ready, ties_summed = sem("ties_ready"), sem("ties_summed")
        gate_ready, gateT_filled, gateT_done = sem("gate_ready"), sem("gateT_filled"), sem("gateT_done")
        gate_stored, gate_loaded = sem("gate_stored"), [sem("gate_loaded0"), sem("gate_loaded1")]
        w_split = sem("w_split")
        up_done, gelu_done, hi_done, lo_done = sem("up_done"), sem("gelu_done"), sem("hi_done"), sem("lo_done")
        down_done, y_taken, added = sem("down_done"), sem("y_taken"), sem("added")
        accT_filled, accT_added = sem("accT_filled"), sem("accT_added")
        block = es.enter_context(nc.Block())

        def experts(eng, body):
            body(None, 0)
            body(None, 1)
            with eng.Fori(0, E // 2 - 1) as it:
                for c in (2, 3):
                    body(it, c)
            body(None, E)

        def step_of(it, c, k):
            return at(it, 2 * STEPS, c * STEPS + k)

        def cut(engine, waiting, it, c, k):
            if it is not None or c * STEPS + k >= 4:
                waiting.wait_ge(down_done, step_of(it, c, k - 3))
            waiting.wait_ge(hi_done, step_of(it, c, k + 1))
            engine.tensor_tensor(h_lo[:, k % 4, :], h[:, k % 4, :], f32(h_hi[:, k % 4, :]), ALU.subtract)\
                  .then_inc(lo_done, 1)

        @block.sync
        def _(sp):
            sp.dma_start(small[0:FC, :], bs1.rearrange("(k p) -> k p", p=P)).then_inc(small_loaded, 16)
            sp.dma_start(small[FC:B2, :], b1.rearrange("e (k p) -> (e k) p", p=P)).then_inc(small_loaded, 16)
            sp.dma_start(small[B2:B2 + 1, :], bs2.rearrange("(a d) -> a d", a=1)).then_inc(small_loaded, 16)
            sp.dma_start(small[B2 + 1:GW, :], b2).then_inc(small_loaded, 16)
            sp.dma_start(small[GW:ROWS, :], gate_w).then_inc(small_loaded, 16)

            def load_weights(c, up, down):
                sp.dma_start(w1_raw[:, c % 2, :], up).then_inc(w_loaded[c % 2], 16)
                sp.dma_start(w2_raw[:, c % 2, :].rearrange("p (k d) -> p k d", d=D),
                             down.rearrange("(k p) d -> p k d", p=P)).then_inc(w_loaded[c % 2], 16)

            load_weights(0, ws1, ws2)
            load_weights(1, w1[0, :, :], w2[0, :, :])
            sp.wait_ge(gateT_done, 1)
            sp.dma_start(gate_dram, gateT[:, :]).then_inc(gate_stored, 16)
            sp.wait_ge(gate_stored, 16)

            def load_gate(c, e):
                sp.dma_start(gate_rows[:, c % 2, :].rearrange("p (t q) -> p t q", q=P),
                             gate_dram[bass.ds(e * TILES, TILES), :].partition_broadcast(P))\
                  .then_inc(gate_loaded[c % 2], 16)

            load_gate(1, 0)
            def body(it, c):
                sp.wait_ge(w_split, at(it, 8, 4 * c))
                e = at(it, 2, c)
                load_weights(c + 1, w1[e, :, :], w2[e, :, :])
                if it is not None or c > 1:
                    sp.wait_ge(y_taken, at(it, 2 * TG, c * TG))
                load_gate(c + 1, e)

            body(None, 1)
            with sp.Fori(0, E // 2 - 1) as it:
                for c in (2, 3):
                    body(it, c)

        @block.gpsimd
        def _(pool):
            nc.gpsimd.memset(ones_b[:, :], 1.0).then_inc(consts, 1)
            nc.gpsimd.memset(before[:, :], 1.0).then_inc(consts, 1)
            nc.gpsimd.memset(zeros[:, :], 0.0).then_inc(consts, 1)
            for r in range(ROUNDS):
                for j in range(3):
                    last = nc.gpsimd.memset(bit_steps[:, r, j:j + 1], (j + 1) << 2 * (ROUNDS - 1 - r))
            last.then_inc(consts, 1)
            pool.wait_ge(consts, 4)
            nc.gpsimd.affine_select(out=before[:, :], in_=before[:, :], compare_op=ALU.is_gt, fill=0.0,
                                    base=0, pattern=[[1, P]], channel_multiplier=-1).then_inc(consts, 1)

            def split(it, c, n):
                raw, W = ((w1_raw, W1), (w2_raw, W2))[n]
                if n == 0:
                    pool.wait_ge(w_loaded[c % 2], at(it, 32, 32 * (c // 2 + 1)))
                    if it is not None or c >= 2:
                        pool.wait_ge(down_done, step_of(it, c - 1, 0))
                        pool.nop(nofuse=True)
                nc.gpsimd.tensor_copy(W[c % 2][0][:, :], raw[:, c % 2, :]).then_inc(w_split, 1)
                pool.wait_ge(w_split, at(it, 8, 4 * c + 2 * n + 1))
                nc.gpsimd.tensor_tensor(W[c % 2][1][:, :], raw[:, c % 2, :], f32(W[c % 2][0][:, :]),
                                        ALU.subtract).then_inc(w_split, 1)

            def body(it, c):
                if c == 0:
                    for k in range(STEPS):
                        cut(nc.gpsimd, pool, it, c, k)
                        if k in SPLITS:
                            split(it, c + 1, SPLITS.index(k))
                elif c < E:
                    for n in range(2):
                        split(it, c + 1, n)
                for tg in range(TG):
                    if c > 0:
                        cols = acc[:, tg * 512:(tg + 1) * 512]
                        pool.wait_ge(y_taken, at(it, 2 * TG, c * TG + tg + 1))
                        if c > 1:
                            pool.wait_ge(added, at(it, 2 * TG, (c - 2) * TG + tg + 1))
                        nc.gpsimd.tensor_tensor(cols, cols, gated[:, tg % 2, :], ALU.add).then_inc(added, 1)

            for n in range(2):
                split(None, 0, n)
            experts(pool, body)

        @block.tensor
        def _(pe):
            pe.wait_ge(small_loaded, 80)
            nc.tensor.transpose(R[:, 1, 0:ROWS], small[:, :], ident[0:ROWS, 0:ROWS]).then_inc(small_filled, 1)
            for g in range(4):
                pe.wait_ge(xn_ready, 4 * g // LN_GROUP + 1)
                for t in range(4):
                    last = nc.tensor.transpose(U[:, g, t * P:(t + 1) * P], xn[:, 4 * g + t, :], ident[:, :])
                last.then_inc(xT_filled, 1)
            pe.wait_ge(small_done, 3)
            for t in range(TILES):
                if t % 4 == 0:
                    pe.wait_ge(xT_done, t // 4 + 1)
                out, cols = R[:, 0, t * E:(t + 1) * E], slice(t * P, (t + 1) * P)
                nc.tensor.matmul(out, xT[0][:, cols], gwT[0][:, :], start=True, stop=False)
                nc.tensor.matmul(out, xT[0][:, cols], gwT[1][:, :], start=False, stop=False)
                last = nc.tensor.matmul(out, xT[1][:, cols], gwT[0][:, :], start=False, stop=True)
            last.then_inc(logits_filled, 1)

            def up(it, c, k):
                tg, fc = k // FC, k % FC
                if k == 0:
                    pe.wait_ge(w_split, at(it, 8, 4 * c + 4))
                if it is not None or c * STEPS + k >= 4:
                    pe.wait_ge(gelu_done, step_of(it, c, k - 3))
                out, W = U[:, k % 4, :], W1[c % 2]
                cols, tok = slice(fc * P, (fc + 1) * P), slice(tg * 512, (tg + 1) * 512)
                nc.tensor.matmul(out, W[0][:, cols], xT[0][:, tok], start=True, stop=False)
                nc.tensor.matmul(out, W[0][:, cols], xT[1][:, tok], start=False, stop=False)
                nc.tensor.matmul(out, W[1][:, cols], xT[0][:, tok], start=False, stop=True).then_inc(up_done, 1)

            def down(it, c, k):
                tg, fc = k // FC, k % FC
                pe.wait_ge(lo_done, step_of(it, c, k + 1))
                if fc == 0 and (it is not None or c * TG + tg >= 2):
                    pe.wait_ge(y_taken, at(it, 2 * TG, c * TG + tg - 1))
                out, W, cols = Y[:, tg % 2, :], W2[c % 2], slice(fc * P, (fc + 1) * P)
                nc.tensor.matmul(out, W[0][:, cols], h_hi[:, k % 4, :], start=(fc == 0), stop=False)
                nc.tensor.matmul(out, W[0][:, cols], h_lo[:, k % 4, :], start=False, stop=False)
                nc.tensor.matmul(out, W[1][:, cols], h_hi[:, k % 4, :], start=False, stop=(fc == FC - 1))\
                  .then_inc(down_done, 1)

            def body(it, c):
                for k in range(STEPS):
                    up(it, c, k)
                    if k >= LAG:
                        down(it, c, k - LAG)
                    elif c > 0:
                        down(it, c - 1, STEPS + k - LAG)
                    if c == 0:
                        if k < ROUNDS:
                            pe.wait_ge(counted, 3 * (k + 1))
                            nc.tensor.matmul(R[:, 1, 0:3], ones_b[:, :], above[:, :], start=True, stop=True)\
                              .then_inc(summed, 1)
                        else:
                            pe.wait_ge(ties_ready, 2)
                            nc.tensor.matmul(R[:, 0, 0:1], ones_b[:, :], n_greater[:, :], start=True, stop=True)
                            nc.tensor.matmul(R[:, 0, P:2 * P], ones_b[:, :], equal[:, :], start=True, stop=True)
                            nc.tensor.matmul(R[:, 0, 2 * P:3 * P], before[:, :], equal[:, :], start=True,
                                             stop=True).then_inc(ties_summed, 1)
                            pe.wait_ge(gate_ready, 1)
                            nc.tensor.transpose(R[:, 1, P:2 * P], gate[:, :], ident[:, :]).then_inc(gateT_filled, 1)

            pe.wait_ge(consts, 5)
            experts(pe, body)
            for k in range(STEPS - LAG, STEPS):
                down(None, E, k)
            pe.wait_ge(added, E * TG)
            for g in range(4):
                for t in range(4):
                    tile = 4 * g + t
                    last = nc.tensor.transpose(U[:, g, t * P:(t + 1) * P], acc[:, tile * P:(tile + 1) * P], ident[:, :])
                last.then_inc(accT_filled, 1)

        @block.scalar
        def _(act):
            layer_norm_on_scalar(nc, act, xn, squares, stats, squared, var_ready, std_ready)
            for g in range(4):
                act.wait_ge(xT_filled, g + 1)
                nc.scalar.activation(xT[0][:, g * 512:(g + 1) * 512], U[:, g, :], ACT.Copy).then_inc(xT_hi_done, 1)
            act.wait_ge(centred, 1)
            nc.scalar.activation(logits[:, :, :], logits[:, :, :], ACT.Exp).then_inc(exped, 1)
            act.wait_ge(xT_done, 4)

            def body(it, c):
                for k in range(STEPS):
                    act.wait_ge(up_done, step_of(it, c, k + 1))
                    if it is not None or c * STEPS + k >= 4:
                        act.wait_ge(lo_done, step_of(it, c, k - 3))
                    col = at(it, 2 * FC, c * FC + k % FC)
                    act.nop(nofuse=True)
                    nc.scalar.activation(h[:, k % 4, :], U[:, k % 4, :], ACT.Gelu_apprx_tanh,
                                         bias=smallT[:, bass.ds(col, 1)]).then_inc(gelu_done, 1)
                    act.wait_ge(gelu_done, step_of(it, c, k + 1))
                    if it is not None or c * STEPS + k >= 4:
                        act.wait_ge(down_done, step_of(it, c, k - 3))
                    nc.scalar.activation(h_hi[:, k % 4, :], h[:, k % 4, :], ACT.Copy).then_inc(hi_done, 1)

            experts(act, body)

        @block.vector
        def _(dve):
            chain = [0]

            def link(ins):
                chain[0] += 1
                ins.then_inc(dve_chain, 1)
                dve.wait_ge(dve_chain, chain[0])

            layer_norm(nc, dve, link, XS, xn, squares, stats, squared, var_ready, std_ready, xn_ready)
            dve.wait_ge(small_filled, 1)
            nc.vector.tensor_copy(smallT[:, :], R[:, 1, 0:ROWS]).then_inc(small_done, 1)
            dve.wait_ge(small_done, 1)
            nc.vector.tensor_copy(gwT[0][:, :], smallT[:, GW:ROWS]).then_inc(small_done, 1)
            dve.wait_ge(small_done, 2)
            nc.vector.tensor_tensor(gwT[1][:, :], smallT[:, GW:ROWS], f32(gwT[0][:, :]), ALU.subtract)\
              .then_inc(small_done, 1)
            for g in range(4):
                cols = slice(g * 512, (g + 1) * 512)
                dve.wait_ge(xT_hi_done, g + 1)
                nc.vector.tensor_tensor(xT[1][:, cols], U[:, g, :], f32(xT[0][:, cols]), ALU.subtract)\
                  .then_inc(xT_done, 1)
            dve.wait_ge(logits_filled, 1)
            L = R[:, 0, 0:TILES * E].rearrange("p (t e) -> p t e", e=E)
            link(nc.vector.tensor_reduce(top[:, 0, :], L, AX.X, ALU.max))
            nc.vector.tensor_tensor(logits[:, :, :], L, bc(top[:, 0, :], E), ALU.subtract).then_inc(centred, 1)
            dve.wait_ge(exped, 1)
            link(nc.vector.tensor_reduce(top[:, 1, :], logits[:, :, :], AX.X, ALU.add))
            link(nc.vector.reciprocal(top[:, 1, :], top[:, 1, :]))
            link(nc.vector.tensor_tensor(scores[:, :, :].rearrange("p e t -> p t e"), logits[:, :, :],
                                         bc(top[:, 1, :], E), ALU.mult))
            flat = scores[:, :, :].rearrange("p e t -> p (e t)")
            dve.wait_ge(consts, 5)
            link(nc.vector.memset(found[:, :], 0))
            link(nc.vector.tensor_copy(candidates[:, :], bit_steps[:, 0, :]))

            def count():
                for j in range(3):
                    nc.vector.tensor_scalar(junk[:, j, :], flat, f32(candidates[:, j:j + 1]), None, ALU.is_ge, ALU.add,
                                            accum_out=above[:, j:j + 1]).then_inc(counted, 1)

            def narrow(r):
                dve.wait_ge(summed, r + 1)
                link(nc.vector.tensor_scalar(passed[:, :], R[:, 1, 0:3], float(TOPK), None, ALU.is_ge, ALU.add,
                                             accum_out=n_passed[:, :]))
                link(nc.vector.tensor_scalar(found_bits[:, :], n_passed[:, :], float(1 << 2 * (ROUNDS - 1 - r)), None,
                                             ALU.mult))
                link(nc.vector.tensor_tensor(found[:, :], found[:, :], found_bits[:, :], ALU.bitwise_or))
                if r + 1 < ROUNDS:
                    link(nc.vector.tensor_tensor(candidates[:, :], bit_steps[:, r + 1, :],
                                                 found[:, :].to_broadcast([P, 3]), ALU.bitwise_or))

            def tie_counts():
                threshold = f32(found[:, :])
                nc.vector.tensor_scalar(greater[:, :], flat, threshold, None, ALU.is_gt, ALU.add,
                                        accum_out=n_greater[:, :]).then_inc(ties_ready, 1)
                nc.vector.tensor_scalar(equal[:, :], flat, threshold, None, ALU.is_equal).then_inc(ties_ready, 1)

            def select():
                dve.wait_ge(ties_summed, 1)
                per_column, rows_before = R[:, 0, P:2 * P], R[:, 0, 2 * P:3 * P]
                link(nc.vector.tensor_copy(n_greater_all[:, :], R[:, 0, 0:1]))
                link(nc.vector.tensor_tensor_scan(rank[:, :], zeros[:, :], per_column, 0.0, ALU.add, ALU.add))
                link(nc.vector.tensor_tensor(rank[:, :], rank[:, :], per_column, ALU.subtract))
                link(nc.vector.tensor_tensor(rank[:, :], rank[:, :], rows_before, ALU.add))
                link(nc.vector.tensor_scalar(rank[:, :], rank[:, :], n_greater_all[:, 0:1], float(TOPK), ALU.add,
                                             ALU.is_lt))
                link(nc.vector.tensor_tensor(rank[:, :], rank[:, :], equal[:, :], ALU.mult))
                link(nc.vector.tensor_tensor(rank[:, :], rank[:, :], greater[:, :], ALU.add))
                nc.vector.tensor_tensor(gate[:, :], rank[:, :], flat, ALU.mult).then_inc(gate_ready, 1)
                dve.wait_ge(gateT_filled, 1)
                nc.vector.tensor_copy(gateT[:, :], R[:, 1, P:2 * P]).then_inc(gateT_done, 1)

            def take_y(it, c, tg):
                dve.wait_ge(down_done, step_of(it, c, (tg + 1) * FC))
                bias = smallT[:, bass.ds(at(it, 2, B2 + c), 1)]
                if c == 0:
                    nc.vector.tensor_scalar(acc[:, tg * 512:(tg + 1) * 512], Y[:, tg % 2, :], bias, None, ALU.add)\
                      .then_inc(y_taken, 1)
                    return
                if tg == 0:
                    dve.wait_ge(gate_loaded[c % 2], at(it, 16, 16 * ((c + 1) // 2)))
                if c > 1 or tg >= 2:
                    dve.wait_ge(added, at(it, 2 * TG, (c - 1) * TG + tg - 1))
                nc.vector.scalar_tensor_tensor(out=gated[:, tg % 2, :], in0=Y[:, tg % 2, :], scalar=bias,
                                               in1=gate_rows[:, c % 2, tg * 512:(tg + 1) * 512], op0=ALU.add,
                                               op1=ALU.mult).then_inc(y_taken, 1)

            def body(it, c):
                for k in range(STEPS):
                    if c == 0:
                        if k > 0 and k <= ROUNDS:
                            narrow(k - 1)
                        if k < ROUNDS:
                            count()
                        else:
                            tie_counts()
                            select()
                    if c == 1 and k == 0:
                        dve.wait_ge(lo_done, STEPS)
                    if c > 0:
                        cut(nc.vector, dve, it, c, k)
                    if k % FC == FC - 1:
                        if k >= FC:
                            take_y(it, c, k // FC - 1)
                        elif c > 0:
                            take_y(it, c - 1, TG - 1)

            experts(dve, body)
            take_y(None, E, TG - 1)
            for g in range(4):
                dve.wait_ge(accT_filled, g + 1)
                rows = XS[:, 4 * g:4 * g + 4, :]
                nc.vector.tensor_tensor(rows, rows, U[:, g, :].rearrange("p (t d) -> p t d", d=D), ALU.add)\
                  .then_inc(accT_added, 1)


def attention_1(nc, ctx_in, wq, bq, wk, bk, wv, bv, wr, br, XS, ident):
    STEPS = (NC + 1) // 2
    SLOTS = 2 * STEPS
    STAGES = B
    PIECES = [(0, 402), (402, 400), (802, 400), (1202, 400)]
    TWO_PI = 6.2831850
    ROUND = float(3 << 22)

    def prep_of(c, kind):
        return c + 2 if kind in ("cT", "angle") else c + 1

    def uses_of(c):
        return 2 * (c > 0) + 8 * (c + 1 < STAGES) + 8 * (c + 2 < STAGES)

    def numbered(items, use):
        out = []
        for c, kind, i in items:
            takes = kind in ("cT", "angle", "max", "den", "proj")
            out.append((c, kind, i, use if takes else None))
            use += takes
        return out

    PROLOGUE = numbered([(-2, kind, i) for kind in ("cT", "angle") for i in range(4)] +
                        [(-1, kind, i) for kind in ("cos", "k_hi") for i in range(4)] +
                        [(-1, "max", i) for i in range(8)] + [(-1, "shift", 0)] +
                        [(-1, kind, i) for kind in ("cT", "angle") for i in range(4)], 0)

    def first_use(c):
        return 24 + sum(map(uses_of, range(c)))

    COS, K_HI, MAX, SHIFT = [1, 1, 1, 1], [3, 4, 5, 6], [4, 5, 6, 7, 8, 8, 9, 9], 9
    TRANSPOSE, ANGLE = [6, 7, 9, 10], [9, 10, 11, 12]

    def plan(c, tail, maxima, angles):
        slots = [[] for _ in range(SLOTS)]
        if tail:
            slots[1].append(("den", 0))
            slots[1].append(("norm", 0))
            slots[5].append(("proj", 0))
        if maxima:
            for kind, where in (("cos", COS), ("k_hi", K_HI), ("max", MAX), ("shift", [SHIFT])):
                for i, slot in enumerate(where):
                    slots[slot].append((kind, i))
        if angles:
            for kind, where in (("cT", TRANSPOSE), ("angle", ANGLE)):
                for i, slot in enumerate(where):
                    slots[slot].append((kind, i))
        use, out = first_use(c), []
        for slot in slots:
            row = [(kind, i, use) for _, kind, i, use in numbered([(c, kind, i) for kind, i in slot], use)]
            use += sum(u is not None for _, _, u in row)
            out.append(row)
        return out

    with ExitStack() as es:
        def sb(name, shape, dt=F32):
            return es.enter_context(nc.sbuf_tensor("b_" + name, shape, dt))

        def sem(name):
            return es.enter_context(nc.semaphore("b_" + name))

        xn = sb("xn", [P, TILES, D])
        squares = sb("squares", [P, TILES, D])
        stats = sb("stats", [P, 2, TILES])
        xT = [sb("xT_hi", [P, B * S], F32R), sb("xT_lo", [P, B * S], F32R)]
        Qf = sb("Qf", [P, B * S])
        w_raw = sb("w_raw", [P, 4, D])
        wkT = sb("wkT", [P, D])
        Wq = [sb("Wq_hi", [P, D], F32R), sb("Wq_lo", [P, D], F32R)]
        Wkr = [sb("Wkr_hi", [P, D], F32R), sb("Wkr_lo", [P, D], F32R)]
        b_rows = sb("b_rows", [3, D])
        b_cols = sb("b_cols", [P, 3])
        bv_row = sb("bv_row", [1, D])
        turn = sb("turn", [P, 2])
        c_in = sb("c_in", [P, NC, D])
        c_nat = sb("c_nat", [P, 2, NC, D])
        cT = [sb("cT_hi", [P, NC * P], F32R), sb("cT_lo", [P, NC * P], F32R)]
        turns = sb("turns", [P, 4, 402])
        whole = sb("whole", [P, 4, 402])
        cosT = sb("cosT", [P, 4, 402])
        K = [[sb(f"K_{part}{i}", [P, NC * P], F32R) for part in ("hi", "lo")] for i in range(2)]
        Qs = [[sb(f"Qs_{part}{i}", [P, S], F32R) for part in ("hi", "lo")] for i in range(2)]
        maxes = sb("maxes", [P, 2, 8])
        neg_max = sb("neg_max", [P, 2, 2])
        shift_diag = sb("shift_diag", [P, 2, 2, P], BF16)
        probs = sb("probs", [P, 4, 2 * S])
        den = sb("den", [P, 2 * S])
        outT = sb("outT", [P, S])
        rden = sb("rden", [P, S])
        ones = sb("ones", [P, P])
        ones_b = sb("ones_b", [P, P], BF16)

        Sc = es.enter_context(nc.psum_tensor("b_scores", [P, 4, 512], F32))
        PV = es.enter_context(nc.psum_tensor("b_pv", [P, 2, 512], F32))
        X = es.enter_context(nc.psum_tensor("b_work", [P, 2, 512], F32))

        w_loaded, c_in_loaded, c_loaded = sem("w_loaded"), sem("c_in_loaded"), [sem("c_loaded0"), sem("c_loaded1")]
        consts, dve_chain = sem("consts"), sem("dve_chain")
        squared = [sem("centred_groups"), sem("squared_groups")]
        var_ready, std_ready, xn_ready = sem("var_ready"), sem("std_ready"), sem("xn_ready")
        wT_filled, wT_done = sem("wT_filled"), sem("wT_done")
        wkr_filled, w_ready = sem("wkr_filled"), sem("w_ready")
        xT_filled, xT_hi_done, xT_done = sem("xT_filled"), sem("xT_hi_done"), sem("xT_done")
        q_filled, q_done = sem("q_filled"), sem("q_done")
        bank_full = [sem("bank0_full"), sem("bank1_full")]
        bank_free = [sem("bank0_free"), sem("bank1_free")]
        qs_ready = sem("qs_ready")
        c_hi_done = sem("c_hi_done")
        angle_steps = sem("angle_steps")
        cos_done, k_hi_done, k_lo_done = sem("cos_done"), sem("k_hi_done"), sem("k_lo_done")
        shift_steps = sem("shift_steps")
        scores_done, probs_done, pv_done = sem("scores_done"), sem("probs_done"), sem("pv_done")
        den_added, norm_done = sem("den_added"), sem("norm_done")
        block = es.enter_context(nc.Block())

        TURN = first_use(3) - first_use(1)
        assert TURN % 2 == 0

        def filled(eng, it, use):
            eng.wait_ge(bank_full[use % 2], at(it, TURN // 2, use // 2 + 1))

        def taken(eng, it, use):
            eng.wait_ge(bank_free[use % 2], at(it, TURN // 2, use // 2 + 1))

        def stages(eng, body):
            body(None, 0)
            with eng.Fori(0, 2) as it:
                for c in (1, 2):
                    body(it, c)
            for c in range(5, STAGES):
                body(None, c)

        def flags(it, c):
            return c > 0, it is not None or c + 1 < STAGES, it is not None or c + 2 < STAGES

        def the_plan(it, c):
            return plan(c, *flags(it, c))

        def step_of(it, c, first):
            return at(it, 2 * STEPS, c * STEPS + first)

        def before_in_buffer(it, c, j):
            if j >= 4:
                return step_of(it, c, j - 3)
            return step_of(it, c - 1, (j + 4 if j < 3 else 3) + 1)

        def rows_of(j, k):
            return LAST if 2 * j + k == NC - 1 else P

        def chunks_of(j):
            return min(2, NC - 2 * j)

        @block.sync
        def _(sp):
            for i, w in enumerate((wq, wk, wr, wv)):
                sp.dma_start(w_raw[:, i, :], w).then_inc(w_loaded, 16)
            for i, b in enumerate((bq, bk, br)):
                sp.dma_start(b_rows[i:i + 1, :], b.rearrange("(a d) -> a d", a=1)).then_inc(w_loaded, 16)
            sp.dma_start(bv_row[:, :], bv.rearrange("(a d) -> a d", a=1)).then_inc(w_loaded, 16)
            sp.wait_ge(consts, 1)

            def load(dst, b, loaded):
                sp.dma_start(dst[:, 0:NC - 1, :],
                             ctx_in[b, 0:(NC - 1) * P, :].rearrange("(c p) d -> p c d", p=P)).then_inc(loaded, 16)
                sp.dma_start(dst[0:LAST, NC - 1, :], ctx_in[b, (NC - 1) * P:N, :]).then_inc(loaded, 16)

            def load_for_transposes(it, s):
                sp.wait_ge(c_hi_done, at(it, 8, 4 * s))
                load(c_in[:, :, :], at(it, 2, s), c_in_loaded)

            load(c_in[:, :, :], 0, c_in_loaded)
            load(c_nat[:, 0, :, :], 0, c_loaded[0])
            load_for_transposes(None, 1)
            load(c_nat[:, 1, :, :], 1, c_loaded[1])

            def body(it, c):
                tail, maxima, angles = flags(it, c)
                if angles:
                    load_for_transposes(it, c + 2)
                if c > 0 and maxima:
                    sp.wait_ge(pv_done, step_of(it, c, 0))
                    load(c_nat[:, (c + 1) % 2, :, :], at(it, 2, c + 1), c_loaded[(c + 1) % 2])

            stages(sp, body)

        @block.gpsimd
        def _(pool):
            nc.gpsimd.memset(c_in[:, NC - 1, :], 0.0).then_inc(consts, 1)
            nc.gpsimd.memset(ones[:, :], 1.0).then_inc(consts, 1)
            nc.gpsimd.memset(ones_b[:, :], 1.0).then_inc(consts, 1)

            def k_low(it, c, i):
                s, (off, w) = prep_of(c, "k_hi"), PIECES[i]
                pool.wait_ge(k_hi_done, at(it, 8, 4 * s + i + 1))
                nc.gpsimd.tensor_tensor(K[s % 2][1][:, off:off + w], cosT[:, i, :w],
                                        f32(K[s % 2][0][:, off:off + w]), ALU.subtract).then_inc(k_lo_done, 1)

            def body(it, c):
                slots = the_plan(it, c)
                for j in range(STEPS):
                    if 0 < j < STEPS - 1:
                        add_probs(it, c, j)
                    for kind, i, use in slots[2 * j] + slots[2 * j + 1]:
                        if kind == "k_hi":
                            k_low(it, c, i)

            def add_probs(it, c, j):
                pool.wait_ge(probs_done, step_of(it, c, j + 1))
                if j == 1:
                    if c > 0:
                        filled(pool, it, [u for s in the_plan(it, c) for k, i, u in s if k == "den"][0])
                    first = probs[:, 0, :]
                else:
                    pool.wait_ge(den_added, at(it, 2 * (STEPS - 2), c * (STEPS - 2) + j - 1))
                    first = den[:, :]
                nc.gpsimd.tensor_tensor(den[:, :], first, probs[:, j % 4, :], ALU.add).then_inc(den_added, 1)

            for c, kind, i, use in PROLOGUE:
                if kind == "k_hi":
                    k_low(None, c, i)
            stages(pool, body)

        @block.tensor
        def _(pe):
            pe.wait_ge(w_loaded, 128)
            nc.tensor.transpose(X[:, 0, 0:D], w_raw[:, 1, :], ident[:, :])
            nc.tensor.transpose(X[:, 0, D:D + 3], b_rows[:, :], ident[0:3, 0:3]).then_inc(wT_filled, 1)
            pe.wait_ge(wT_done, 2)
            nc.tensor.matmul(X[:, 1, 0:D], wkT[:, :], w_raw[:, 2, :], start=True, stop=True)
            nc.tensor.matmul(X[:, 1, D:D + 1], w_raw[:, 2, :], b_cols[:, 1:2], start=True, stop=True)\
              .then_inc(wkr_filled, 1)
            for g in range(4):
                pe.wait_ge(xn_ready, 4 * g // LN_GROUP + 1)
                for t in range(4):
                    last = nc.tensor.transpose(Sc[:, g, t * P:(t + 1) * P], xn[:, 4 * g + t, :], ident[:, :])
                last.then_inc(xT_filled, 1)
            pe.wait_ge(w_ready, 2)

            def split_product(out, a, b, cols_a, cols_b, stop=True):
                nc.tensor.matmul(out, a[0][:, cols_a], b[0][:, cols_b], start=True, stop=False)
                nc.tensor.matmul(out, a[0][:, cols_a], b[1][:, cols_b], start=False, stop=False)
                return nc.tensor.matmul(out, a[1][:, cols_a], b[0][:, cols_b], start=False, stop=stop)

            for g in range(4):
                pe.wait_ge(xT_done, g + 1)
                if g >= 2:
                    pe.wait_ge(q_done, g - 1)
                split_product(PV[:, g % 2, :], Wq, xT, slice(0, D), slice(g * 512, (g + 1) * 512)).then_inc(q_filled, 1)
            pe.wait_ge(w_ready, 5)
            pe.wait_ge(q_done, 4)

            def item(it, c, kind, i, use):
                bank, s = use % 2, prep_of(c, kind)
                if use >= 2:
                    taken(pe, it, use - 2)
                out = X[:, bank, :]
                if kind == "cT":
                    pe.wait_ge(c_in_loaded, at(it, 64, 32 * (s + 1)))
                    for ch in range(4 * i, min(4 * i + 4, NC)):
                        last = nc.tensor.transpose(out[:, ch % 4 * P:(ch % 4 + 1) * P], c_in[:, ch, :],
                                                   ident[:, :])
                elif kind == "angle":
                    off, w = PIECES[i]
                    last = split_product(out[:, :w], Wkr, cT, slice(0, D), slice(off, off + w))
                elif kind == "max":
                    off, w = PIECES[i % 4]
                    if i < 4:
                        pe.wait_ge(k_hi_done, at(it, 8, 4 * s + i + 1))
                    if i == 0:
                        pe.wait_ge(qs_ready, at(it, 4, 2 * s + 2))
                    last = nc.tensor.matmul(out[:, :w], Qs[s % 2][0][:, i // 4 * P:(i // 4 + 1) * P],
                                            K[s % 2][0][:, off:off + w], start=True, stop=True)
                elif kind == "den":
                    pe.wait_ge(den_added, at(it, 2 * (STEPS - 2), c * (STEPS - 2)))
                    for k in range(2):
                        nc.tensor.matmul(out[:, 0:S], ones[:, :], den[:, k * S:(k + 1) * S], start=(k == 0), stop=False)
                    last = nc.tensor.matmul(out[:, 0:S], ones[0:LAST, :], probs[0:LAST, (STEPS - 1) % 4, 0:S],
                                            start=False, stop=True)
                elif kind == "proj":
                    pe.wait_ge(norm_done, at(it, 2, c))
                    for j in range(2):
                        half = out[:, j * D:(j + 1) * D]
                        nc.tensor.matmul(half, outT[:, j * P:(j + 1) * P], w_raw[:, 3, :], start=True, stop=False)
                        last = nc.tensor.matmul(half, ones[0:1, :], bv_row[:, :], start=False, stop=True)
                last.then_inc(bank_full[bank], 1)

            def qk(it, c, j, k):
                if k == 0:
                    if c > 0 or j > 3:
                        pe.wait_ge(probs_done, before_in_buffer(it, c, j))
                    if j == 0:
                        pe.wait_ge(shift_steps, at(it, 4, 2 * c + 2))
                        pe.wait_ge(k_lo_done, at(it, 8, 4 * c + 4))
                if k >= chunks_of(j):
                    return
                rows = rows_of(j, k)
                out = Sc[0:rows, j % 4, k * S:(k + 1) * S]
                first = (2 * j + k) * P
                split_product(out, K[c % 2], Qs[c % 2], slice(first, first + rows), slice(0, S), stop=False)
                last = nc.tensor.matmul(out, ones_b[:, 0:rows], shift_diag[:, c % 2, :, :], start=False, stop=True)
                if k == chunks_of(j) - 1:
                    last.then_inc(scores_done, 1)

            def pv(it, c, j, k):
                if k == 0:
                    pe.wait_ge(probs_done, step_of(it, c, j + 1))
                    if j == 0:
                        pe.wait_ge(c_loaded[c % 2], at(it, 32, 32 * (c // 2 + 1)))
                        if c > 1:
                            pe.wait_ge(norm_done, at(it, 2, c - 1))
                if k >= chunks_of(j):
                    return
                rows = rows_of(j, k)
                last = nc.tensor.matmul(PV[:, c % 2, 0:S], c_nat[0:rows, c % 2, 2 * j + k, :],
                                        probs[0:rows, j % 4, k * S:(k + 1) * S],
                                        start=(j == 0 and k == 0), stop=(j == STEPS - 1))
                if k == chunks_of(j) - 1:
                    last.then_inc(pv_done, 1)

            def body(it, c):
                tail, maxima, angles = flags(it, c)
                slots = the_plan(it, c)
                for j in range(STEPS):
                    for k in range(2):
                        pv(it, c, j, k)
                        if j + 2 < STEPS:
                            qk(it, c, j + 2, k)
                        elif maxima:
                            qk(it, c + 1, j + 2 - STEPS, k)
                        for kind, i, use in slots[2 * j + k]:
                            if use is not None:
                                item(it, c, kind, i, use)

            pe.wait_ge(consts, 3)
            for c, kind, i, use in PROLOGUE:
                if use is not None:
                    item(None, c, kind, i, use)
            for j in range(2):
                for k in range(2):
                    qk(None, 0, j, k)
            stages(pe, body)
            for n, kind in enumerate(("den", "proj")):
                item(None, STAGES, kind, 0, first_use(STAGES) + n)

        @block.scalar
        def _(act):
            layer_norm_on_scalar(nc, act, xn, squares, stats, squared, var_ready, std_ready)
            for g in range(4):
                act.wait_ge(xT_filled, g + 1)
                nc.scalar.activation(xT[0][:, g * 512:(g + 1) * 512], Sc[:, g, :], ACT.Copy).then_inc(xT_hi_done, 1)
            act.wait_ge(wT_done, 2)
            for g in range(4):
                act.wait_ge(q_filled, g + 1)
                nc.scalar.activation(Qf[:, g * 512:(g + 1) * 512], PV[:, g % 2, :], ACT.Identity, bias=b_cols[:, 0:1])\
                  .then_inc(q_done, 1)

            def item(it, c, kind, i, use):
                s = prep_of(c, kind)
                if kind == "cT":
                    filled(act, it, use)
                    w = min(4, NC - 4 * i) * P
                    nc.scalar.activation(cT[0][:, i * 512:i * 512 + w], X[:, use % 2, :w], ACT.Copy)\
                      .then_inc(c_hi_done, 1)
                elif kind == "cos":
                    w = PIECES[i][1]
                    act.wait_ge(angle_steps, at(it, 24, 12 * s + 3 * i + 3))
                    if s > 0:
                        act.wait_ge(k_lo_done, at(it, 8, 4 * s + i - 3))
                    nc.scalar.activation(cosT[:, i, :w], turns[:, i, :w], ACT.Sin, scale=TWO_PI)\
                      .then_inc(cos_done, 1)
                elif kind == "k_hi":
                    off, w = PIECES[i]
                    act.wait_ge(cos_done, at(it, 8, 4 * s + i + 1))
                    nc.scalar.activation(K[s % 2][0][:, off:off + w], cosT[:, i, :w], ACT.Copy)\
                      .then_inc(k_hi_done, 1)

            def exp(it, c, j):
                act.wait_ge(scores_done, step_of(it, c, j + 1))
                if c > 0 or j > 3:
                    act.wait_ge(pv_done, before_in_buffer(it, c, j))
                if j >= 4:
                    act.wait_ge(den_added, at(it, 2 * (STEPS - 2), c * (STEPS - 2) + (j - 4 or 1)))
                elif c > 0 and j == 2:
                    filled(act, it, [u for s in the_plan(it, c) for k, i, u in s if k == "den"][0])
                elif c > 0:
                    act.wait_ge(den_added, at(it, 2 * (STEPS - 2), (c - 1) * (STEPS - 2) + (j + 4 if j < 2 else j)))
                rows, cols = rows_of(j, 0) if chunks_of(j) == 1 else P, chunks_of(j) * S
                nc.scalar.activation(probs[0:rows, j % 4, 0:cols], Sc[0:rows, j % 4, 0:cols], ACT.Exp)\
                  .then_inc(probs_done, 1)

            def body(it, c):
                tail, maxima, angles = flags(it, c)
                slots = the_plan(it, c)
                for j in range(STEPS):
                    if j + 1 < STEPS:
                        exp(it, c, j + 1)
                    elif maxima:
                        exp(it, c + 1, 0)
                    for slot in slots[2 * j:2 * j + 2]:
                        for kind, i, use in slot:
                            item(it, c, kind, i, use)

            for c, kind, i, use in PROLOGUE:
                item(None, c, kind, i, use)
            exp(None, 0, 0)
            stages(act, body)

        @block.vector
        def _(dve):
            chain = [0]

            def link(ins):
                chain[0] += 1
                ins.then_inc(dve_chain, 1)
                dve.wait_ge(dve_chain, chain[0])

            layer_norm(nc, dve, link, XS, xn, squares, stats, squared, var_ready, std_ready, xn_ready)
            dve.wait_ge(wT_filled, 1)
            nc.vector.tensor_copy(wkT[:, :], X[:, 0, 0:D]).then_inc(wT_done, 1)
            nc.vector.tensor_copy(b_cols[:, :], X[:, 0, D:D + 3]).then_inc(wT_done, 1)
            link(nc.vector.tensor_copy(Wq[0][:, :], w_raw[:, 0, :]))
            nc.vector.tensor_tensor(Wq[1][:, :], w_raw[:, 0, :], f32(Wq[0][:, :]), ALU.subtract).then_inc(w_ready, 2)
            dve.wait_ge(wkr_filled, 1)
            link(nc.vector.tensor_copy(Wkr[0][:, :], X[:, 1, 0:D]))
            nc.vector.tensor_tensor(Wkr[1][:, :], X[:, 1, 0:D], f32(Wkr[0][:, :]), ALU.subtract).then_inc(w_ready, 1)
            link(nc.vector.tensor_tensor(turn[:, 0:1], X[:, 1, D:D + 1], b_cols[:, 2:3], ALU.add))
            nc.vector.tensor_scalar(turn[:, 1:2], turn[:, 0:1], 1.0 / (2.0 * math.pi), 0.25, ALU.mult, ALU.add)\
              .then_inc(w_ready, 2)
            for g in range(4):
                cols = slice(g * 512, (g + 1) * 512)
                dve.wait_ge(xT_hi_done, g + 1)
                nc.vector.tensor_tensor(xT[1][:, cols], Sc[:, g, :], f32(xT[0][:, cols]), ALU.subtract).then_inc(xT_done, 1)
            dve.wait_ge(q_done, 4)
            dve.wait_ge(w_ready, 5)

            def take_q(it, s):
                rows = Qf[:, bass.ds(at(it, 2 * S, s * S), S)]
                nc.vector.tensor_copy(Qs[s % 2][0][:, :], rows).then_inc(qs_ready, 1)
                dve.wait_ge(qs_ready, at(it, 4, 2 * s + 1))
                nc.vector.tensor_tensor(Qs[s % 2][1][:, :], rows, f32(Qs[s % 2][0][:, :]), ALU.subtract)\
                  .then_inc(qs_ready, 1)

            def item(it, c, kind, i, use):
                s = prep_of(c, kind)
                bank = None if use is None else use % 2
                if kind == "cos" and i == 0:
                    take_q(it, s)
                elif kind == "cT":
                    w = min(4, NC - 4 * i) * P
                    cols = slice(i * 512, i * 512 + w)
                    dve.wait_ge(c_hi_done, at(it, 8, 4 * s + i + 1))
                    nc.vector.tensor_tensor(cT[1][:, cols], X[:, bank, :w], f32(cT[0][:, cols]), ALU.subtract)\
                      .then_inc(bank_free[bank], 1)
                elif kind == "angle":
                    off, w = PIECES[i]
                    filled(dve, it, use)
                    if s > 0:
                        dve.wait_ge(cos_done, at(it, 8, 4 * s + i - 3))
                    t, n = turns[:, i, :w], whole[:, i, :w]
                    done = at(it, 24, 12 * s + 3 * i + 1), at(it, 24, 12 * s + 3 * i + 2)
                    nc.vector.tensor_scalar(t, X[:, bank, :w], 1.0 / (2.0 * math.pi), turn[:, 1:2], ALU.mult, ALU.add)\
                      .then_inc(bank_free[bank], 1)
                    taken(dve, it, use)
                    nc.vector.tensor_scalar(n, t, ROUND, ROUND, ALU.add, ALU.subtract).then_inc(angle_steps, 1)
                    dve.wait_ge(angle_steps, done[0])
                    nc.vector.tensor_tensor(t, t, n, ALU.subtract).then_inc(angle_steps, 1)
                    dve.wait_ge(angle_steps, done[1])
                    nc.vector.tensor_scalar(t, t, 0.5, -0.5, ALU.min, ALU.max).then_inc(angle_steps, 1)
                elif kind == "max":
                    filled(dve, it, use)
                    w = min(PIECES[i % 4][1], N - PIECES[i % 4][0])
                    nc.vector.tensor_reduce(maxes[:, s % 2, i:i + 1], X[:, bank, :w], AX.X, ALU.max)\
                      .then_inc(bank_free[bank], 1)
                elif kind == "shift":
                    uses = max_uses(it, c)
                    for bank in range(2):
                        taken(dve, it, max(u for u in uses if u % 2 == bank))
                    nc.vector.tensor_reduce(neg_max[:, s % 2, :], maxes[:, s % 2, :].rearrange("p (u k) -> p u k", k=4),
                                            AX.X, ALU.max, negate=True).then_inc(shift_steps, 1)
                    dve.wait_ge(shift_steps, at(it, 4, 2 * s + 1))
                    nc.vector.tensor_tensor(shift_diag[:, s % 2, :, :],
                                            ident[:, :].unsqueeze(1).to_broadcast([P, 2, P]),
                                            bc(neg_max[:, s % 2, :], P), ALU.mult).then_inc(shift_steps, 1)
                elif kind == "den":
                    filled(dve, it, use)
                    nc.vector.reciprocal(rden[:, :], X[:, bank, 0:S]).then_inc(bank_free[bank], 1)
                    taken(dve, it, use)
                elif kind == "norm":
                    dve.wait_ge(pv_done, step_of(it, c, 0))
                    nc.vector.tensor_tensor(outT[:, :], PV[:, (c - 1) % 2, 0:S], rden[:, :], ALU.mult)\
                      .then_inc(norm_done, 1)
                elif kind == "proj":
                    filled(dve, it, use)
                    rows = XS[:, bass.ds(at(it, 4, 2 * (c - 1)), 2), :]
                    nc.vector.tensor_tensor(rows, rows, X[:, bank, :2 * D].rearrange("p (j d) -> p j d", d=D), ALU.add)\
                      .then_inc(bank_free[bank], 1)

            def max_uses(it, c):
                items = PROLOGUE if c < 0 else [(c, *item) for slot in the_plan(it, c) for item in slot]
                return [use for _, kind, _, use in items if kind == "max"]

            def body(it, c):
                for slot in the_plan(it, c):
                    for kind, i, use in slot:
                        item(it, c, kind, i, use)

            for c, kind, i, use in PROLOGUE:
                item(None, c, kind, i, use)
            stages(dve, body)
            for n, (kind, use) in enumerate((("den", first_use(STAGES)), ("norm", None), ("proj", first_use(STAGES) + 1))):
                item(None, STAGES, kind, 0, use)


def ffn_1(nc, base_w, base_b, shared_a, shared_b, routed_a, routed_b, router_w, router_b, XS, ident, out):
    E, RK = routed_a.shape[0], routed_a.shape[1]
    ER = E * RK
    T = B * S
    ROWS = ER + E

    with ExitStack() as es:
        def sb(name, shape, dt=F32):
            return es.enter_context(nc.sbuf_tensor("f_" + name, shape, dt))

        def sem(name):
            return es.enter_context(nc.semaphore("f_" + name))

        xn = sb("xn", [P, TILES, D])
        squares = sb("squares", [P, TILES, D])
        stats = sb("stats", [P, 2, TILES])
        xT = sb("xT", [P, T])
        small = sb("small", [ROWS, D])
        smallT = sb("smallT", [P, ROWS])
        base = sb("base", [P, D])
        sa = sb("sa", [RK, D])
        sbn = sb("sbn", [P, RK])
        sbT = sb("sbT", [RK, D])
        rb = sb("rb", [P, E, RK])
        rbT = sb("rbT", [ER + 1, D])
        router_col = sb("router_col", [ROWS, 1])
        logitsT = sb("logitsT", [ROWS, T])
        Wb = sb("Wb", [P, D])
        gate = sb("gate", [P, TILES, E])
        top = sb("top", [P, 2, TILES])
        rank = sb("rank", [P, TILES, E])
        ahead = sb("ahead", [P, TILES, E])
        weights = sb("weights", [P, TILES, E])
        spread_weights = sb("spread_weights", [P, TILES, ER])
        spread = sb("spread", [ER, T])
        hT = sb("hT", [ER + 1, T])

        A = es.enter_context(nc.psum_tensor("f_a", [P, 4, 512], F32))
        C = es.enter_context(nc.psum_tensor("f_c", [P, 4, 512], F32))

        loaded, consts, dve_chain = sem("loaded"), sem("consts"), sem("dve_chain")
        squared = [sem("centred_groups"), sem("squared_groups")]
        var_ready, std_ready, xn_ready = sem("var_ready"), sem("std_ready"), sem("xn_ready")
        small_filled, small_done, wb_filled, wb_done = sem("small_filled"), sem("small_done"), sem("wb_filled"), sem("wb_done")
        xT_filled, xT_done = sem("xT_filled"), sem("xT_done")
        logitsT_done, logits_filled = sem("logitsT_done"), sem("logits_filled")
        centred, exped = sem("centred"), sem("exped")
        h_filled, weighted = sem("h_filled"), sem("weighted")
        spread_filled, spread_done, h_done = sem("spread_filled"), sem("spread_done"), sem("h_done")
        y_filled, y_added, stored = sem("y_filled"), sem("y_added"), sem("stored")
        block = es.enter_context(nc.Block())

        @block.sync
        def _(sp):
            sp.dma_start(small[ER:ROWS, :], router_w).then_inc(loaded, 16)
            sp.dma_start(small[0:ER, :], routed_a.rearrange("e r d -> (e r) d")).then_inc(loaded, 16)
            sp.dma_start(base[:, :], base_w).then_inc(loaded, 16)
            sp.dma_start(sa[:, :], shared_a).then_inc(loaded, 16)
            sp.dma_start(sbn[:, :], shared_b).then_inc(loaded, 16)
            sp.dma_start(rb[:, :, :], routed_b.rearrange("e o r -> o e r")).then_inc(loaded, 16)
            sp.dma_start(rbT[ER:ER + 1, :], base_b.rearrange("(a d) -> a d", a=1)).then_inc(loaded, 16)
            sp.dma_start(router_col[ER:ROWS, :], router_b.rearrange("(d a) -> d a", a=1)).then_inc(loaded, 16)
            tokens = out.rearrange("b (j p) d -> p (b j) d", p=P)
            for g in range(4):
                sp.wait_ge(y_added, g + 1)
                sp.dma_start(tokens[:, 4 * g:4 * g + 4, :], XS[:, 4 * g:4 * g + 4, :]).then_inc(stored, 16)
            sp.wait_ge(stored, 64)

        @block.gpsimd
        def _(pool):
            nc.gpsimd.memset(hT[ER:ER + 1, :], 1.0).then_inc(consts, 1)
            pool.wait_ge(consts, 1)
            for e in range(E):
                nc.gpsimd.memset(rank[:, :, e:e + 1], float(e)).then_inc(consts, 1)

        @block.tensor
        def _(pe):
            pe.wait_ge(loaded, 128)
            pe.wait_ge(consts, 1)
            nc.tensor.transpose(A[:, 0, 0:ROWS], small[:, :], ident[0:ROWS, 0:ROWS])
            nc.tensor.transpose(A[0:RK, 1, 0:D], sbn[:, :], ident[:, :])
            nc.tensor.transpose(A[0:ER, 1, D:2 * D], rb[:, :, :].rearrange("p e r -> p (e r)"), ident[:, :])\
              .then_inc(small_filled, 1)
            pe.wait_ge(small_done, 3)
            nc.tensor.matmul(A[:, 2, 0:D], base[:, :], ident[:, :], start=True, stop=False)
            nc.tensor.matmul(A[:, 2, 0:D], sa[:, :], sbT[:, :], start=False, stop=True).then_inc(wb_filled, 1)
            for g in range(4):
                pe.wait_ge(xn_ready, 4 * g // LN_GROUP + 1)
                for t in range(4):
                    last = nc.tensor.transpose(C[:, g, t * P:(t + 1) * P], xn[:, 4 * g + t, :], ident[:, :])
                last.then_inc(xT_filled, 1)
            for g in range(4):
                pe.wait_ge(xT_done, g + 1)
                nc.tensor.matmul(C[0:ROWS, g, :], smallT[:, :], xT[:, g * 512:(g + 1) * 512], start=True,
                                 stop=True).then_inc(h_filled, 1)
            for t in range(TILES):
                if t % 4 == 0:
                    pe.wait_ge(logitsT_done, t // 4 + 1)
                last = nc.tensor.transpose(A[:, 3, t * E:(t + 1) * E], logitsT[ER:ROWS, t * P:(t + 1) * P],
                                           ident[ER:ROWS, ER:ROWS])
            last.then_inc(logits_filled, 1)
            for g in range(4):
                pe.wait_ge(weighted, g + 1)
                if g == 2:
                    pe.wait_ge(wb_done, 1)
                if g == 3:
                    pe.wait_ge(centred, 1)
                for t in range(4):
                    last = nc.tensor.transpose(A[0:ER, g, t * P:(t + 1) * P], spread_weights[:, 4 * g + t, :],
                                               ident[:, :])
                last.then_inc(spread_filled, 1)
            for g in range(4):
                pe.wait_ge(h_done, g + 1)
                for t in range(4):
                    tok = slice((4 * g + t) * P, (4 * g + t + 1) * P)
                    o = A[:, g, t * D:(t + 1) * D]
                    nc.tensor.matmul(o, xT[:, tok], Wb[:, :], start=True, stop=False)
                    last = nc.tensor.matmul(o, hT[:, tok], rbT[:, :], start=False, stop=True)
                last.then_inc(y_filled, 1)

        @block.scalar
        def _(act):
            layer_norm_on_scalar(nc, act, xn, squares, stats, squared, var_ready, std_ready)
            act.wait_ge(wb_filled, 1)
            nc.scalar.activation(Wb[:, :], A[:, 2, 0:D], ACT.Copy).then_inc(wb_done, 1)
            for g in range(0, 4, 2):
                act.wait_ge(xT_filled, g + 2)
                nc.scalar.activation(xT[:, g * 512:(g + 2) * 512], C[:, g:g + 2, :].rearrange("p a n -> p (a n)"),
                                     ACT.Copy).then_inc(xT_done, 2)
            for g in range(4):
                act.wait_ge(h_filled, g + 1)
                nc.scalar.activation(logitsT[ER:ROWS, g * 512:(g + 1) * 512], C[ER:ROWS, g, :], ACT.Identity,
                                     bias=router_col[ER:ROWS, 0:1]).then_inc(logitsT_done, 1)
            act.wait_ge(centred, 1)
            nc.scalar.activation(gate[:, :, :], gate[:, :, :], ACT.Exp).then_inc(exped, 1)
            for g in range(4):
                act.wait_ge(spread_filled, g + 1)
                nc.scalar.activation(spread[:, g * 512:(g + 1) * 512], A[0:ER, g, :], ACT.Copy).then_inc(spread_done, 1)

        @block.vector
        def _(dve):
            chain = [0]

            def link(ins):
                chain[0] += 1
                ins.then_inc(dve_chain, 1)
                dve.wait_ge(dve_chain, chain[0])

            layer_norm(nc, dve, link, XS, xn, squares, stats, squared, var_ready, std_ready, xn_ready)
            dve.wait_ge(small_filled, 1)
            nc.vector.tensor_copy(smallT[:, :], A[:, 0, 0:ROWS]).then_inc(small_done, 1)
            nc.vector.tensor_copy(sbT[:, :], A[0:RK, 1, 0:D]).then_inc(small_done, 1)
            nc.vector.tensor_copy(rbT[0:ER, :], A[0:ER, 1, D:2 * D]).then_inc(small_done, 1)
            dve.wait_ge(logits_filled, 1)
            L = A[:, 3, 0:TILES * E].rearrange("p (t e) -> p t e", e=E)
            link(nc.vector.tensor_reduce(top[:, 0, :], L, AX.X, ALU.max))
            nc.vector.tensor_tensor(gate[:, :, :], L, bc(top[:, 0, :], E), ALU.subtract).then_inc(centred, 1)
            dve.wait_ge(exped, 1)
            link(nc.vector.tensor_reduce(top[:, 1, :], gate[:, :, :], AX.X, ALU.add))
            link(nc.vector.reciprocal(top[:, 1, :], top[:, 1, :]))
            link(nc.vector.tensor_tensor(gate[:, :, :], gate[:, :, :], bc(top[:, 1, :], E), ALU.mult))
            dve.wait_ge(consts, 1 + E)
            for k in range(1, E):
                link(nc.vector.tensor_tensor(ahead[:, :, 0:E - k], gate[:, :, k:E], gate[:, :, 0:E - k], ALU.is_gt))
                link(nc.vector.tensor_tensor(rank[:, :, 0:E - k], rank[:, :, 0:E - k], ahead[:, :, 0:E - k], ALU.add))
                link(nc.vector.tensor_tensor(rank[:, :, k:E], rank[:, :, k:E], ahead[:, :, 0:E - k], ALU.subtract))
            link(nc.vector.scalar_tensor_tensor(out=weights[:, :, :], in0=rank[:, :, :], scalar=1.5, in1=gate[:, :, :],
                                                op0=ALU.is_lt, op1=ALU.mult))
            link(nc.vector.tensor_reduce(top[:, 0, :], weights[:, :, :], AX.X, ALU.add))
            link(nc.vector.tensor_scalar(top[:, 0, :], top[:, 0, :], 1e-6, None, ALU.add))
            link(nc.vector.reciprocal(top[:, 0, :], top[:, 0, :]))
            for g in range(4):
                tiles, shape = slice(4 * g, 4 * g + 4), [P, 4, E, RK]
                nc.vector.tensor_tensor(spread_weights[:, tiles, :].rearrange("p t (e r) -> p t e r", r=RK),
                                        weights[:, tiles, :].unsqueeze(3).to_broadcast(shape),
                                        top[:, 0, tiles].unsqueeze(2).unsqueeze(3).to_broadcast(shape), ALU.mult)\
                  .then_inc(weighted, 1)
            for g in range(4):
                cols = slice(g * 512, (g + 1) * 512)
                dve.wait_ge(h_filled, g + 1)
                dve.wait_ge(spread_done, g + 1)
                nc.vector.tensor_tensor(hT[0:ER, cols], C[0:ER, g, :], spread[:, cols], ALU.mult).then_inc(h_done, 1)
            for g in range(4):
                dve.wait_ge(y_filled, g + 1)
                rows_g = XS[:, 4 * g:4 * g + 4, :]
                nc.vector.tensor_tensor(rows_g, rows_g, A[:, g, :].rearrange("p (t d) -> p t d", d=D), ALU.add)\
                  .then_inc(y_added, 1)


def two_layers(nc, x, ctx_1024, L0_xattn_Wq, L0_xattn_Wk, L0_xattn_Wv, L0_xattn_Wo, L0_ffn_gate_weight, L0_ffn_W1,
               L0_ffn_b1, L0_ffn_W2, L0_ffn_b2, L0_ffn_Ws1, L0_ffn_bs1, L0_ffn_Ws2, L0_ffn_bs2, L1_xattn_Wq,
               L1_xattn_bq, L1_xattn_Wk, L1_xattn_bk, L1_xattn_Wv, L1_xattn_bv, L1_xattn_Wr, L1_xattn_br,
               L1_ffn_base_W, L1_ffn_base_b, L1_ffn_shared_A, L1_ffn_shared_B, L1_ffn_routed_A, L1_ffn_routed_B,
               L1_ffn_router_W, L1_ffn_router_b, out):
    with ExitStack() as es:
        XS = es.enter_context(nc.sbuf_tensor("tokens", [P, TILES, D], F32))
        ident = es.enter_context(nc.sbuf_tensor("ident", [P, P], F32))
        attention_0(nc, x, ctx_1024, L0_xattn_Wq, L0_xattn_Wk, L0_xattn_Wv, L0_xattn_Wo, XS, ident)
        moe_0(nc, L0_ffn_gate_weight, L0_ffn_W1, L0_ffn_b1, L0_ffn_W2, L0_ffn_b2, L0_ffn_Ws1, L0_ffn_bs1,
              L0_ffn_Ws2, L0_ffn_bs2, XS, ident)
        attention_1(nc, ctx_1024, L1_xattn_Wq, L1_xattn_bq, L1_xattn_Wk, L1_xattn_bk, L1_xattn_Wv, L1_xattn_bv,
                    L1_xattn_Wr, L1_xattn_br, XS, ident)
        ffn_1(nc, L1_ffn_base_W, L1_ffn_base_b, L1_ffn_shared_A, L1_ffn_shared_B, L1_ffn_routed_A, L1_ffn_routed_B,
              L1_ffn_router_W, L1_ffn_router_b, XS, ident, out)


_INS = ['x', 'ctx_1024', 'L0_xattn_Wq', 'L0_xattn_Wk', 'L0_xattn_Wv', 'L0_xattn_Wo', 'L0_ffn_gate_weight', 'L0_ffn_W1',
        'L0_ffn_b1', 'L0_ffn_W2', 'L0_ffn_b2', 'L0_ffn_Ws1', 'L0_ffn_bs1', 'L0_ffn_Ws2', 'L0_ffn_bs2', 'L1_xattn_Wq',
        'L1_xattn_bq', 'L1_xattn_Wk', 'L1_xattn_bk', 'L1_xattn_Wv', 'L1_xattn_bv', 'L1_xattn_Wr', 'L1_xattn_br',
        'L1_ffn_base_W', 'L1_ffn_base_b', 'L1_ffn_shared_A', 'L1_ffn_shared_B', 'L1_ffn_routed_A', 'L1_ffn_routed_B',
        'L1_ffn_router_W', 'L1_ffn_router_b']
_OUTS = [((B, S, D), 'float32')]


def kernel(**inputs):
    import numpy as _np
    import concourse.bacc as _bacc
    from concourse import mybir as _mybir
    from concourse.bass_utils import run_bass_kernel_spmd as _run

    nc = _bacc.Bacc("TRN2", target_bir_lowering=False, num_devices=1)
    arrays, args = {}, []
    for name in _INS:
        a = _np.ascontiguousarray(inputs[name])
        arrays[f"in_{name}_dram"] = a
        args.append(nc.dram_tensor(f"in_{name}_dram", a.shape, _mybir.dt.from_np(a.dtype), kind="ExternalInput").ap())
    for i, (shape, dtype) in enumerate(_OUTS):
        dt = _mybir.dt.from_np(_np.dtype(dtype))
        args.append(nc.dram_tensor(f"out_{i}_dram", shape, dt, kind="ExternalOutput").ap())
    two_layers(nc, *args)
    r = _run(nc, [arrays], core_ids=[0])
    return r.results[0]["out_0_dram"]
```
